# Optimizing a Trainium2 kernel written in Bass

```python
import numpy as np
import jax
import jax.numpy as jnp

def _softmax(x, axis=-1):
    return jax.nn.softmax(x, axis=axis)

def _gelu(x):
    return jax.nn.gelu(x, approximate=True)

def _silu(x):
    return jax.nn.silu(x)

def _sigmoid(x):
    return jax.nn.sigmoid(x)

def _layernorm(x, axis=-1, eps=1e-05):
    m = jnp.mean(x, axis=axis, keepdims=True)
    v = jnp.var(x, axis=axis, keepdims=True)
    return (x - m) / jnp.sqrt(v + eps)

def _scatter_add(tgt, idx, src, axis=0):
    return tgt.at[idx].add(src)

def _segment_sum(src, seg, n):
    return jax.ops.segment_sum(src, seg, n)
kernel_name = 'mk_gnn_preln_d4_gnn_r32_730553'

def setup_inputs(seed: int=0):
    np.random.seed(seed)
    _w = jnp.asarray

    def _rec_inputs():
        import jax
        import jax.numpy as jnp
        _gk = jax.random.key(seed)
        x = -0.000202 + 1 * jax.random.normal(jax.random.fold_in(_gk, 1), (3125, 128), jnp.float32)
        _s = jax.random.randint(jax.random.fold_in(_gk, 2), (25000,), 0, 3125, jnp.int32)
        _d = jax.random.randint(jax.random.fold_in(_gk, 3), (25000,), 0, 3125, jnp.int32)
        _loop = jnp.arange(3125, dtype=jnp.int32)
        src = jnp.concatenate([_s, _d, _loop])
        dst = jnp.concatenate([_d, _s, _loop])
        _o = jnp.argsort(dst, stable=True)
        src = src[_o]
        dst = dst[_o]
        edge_type_5 = jax.random.randint(jax.random.fold_in(_gk, 13), (53125,), 0, 5, jnp.int32)
        return (x, src, dst, edge_type_5)
    x, src, dst, edge_type_5 = _rec_inputs()

    def _L0_gnn_setup():
        import jax, jax.numpy as jnp
        import numpy as np
        N_NODES = 50000
        N_EDGES = 18750
        D_IN = 128
        D_OUT = 128
        N_BASES = 4
        N_RATINGS = 5
        key = jax.random.key(seed)
        k1, k2, k3, k4, k5, k6 = jax.random.split(key, 6)
        x = jax.random.normal(k1, (N_NODES, D_IN), dtype=jnp.float32)
        edge_index = jax.random.randint(k2, (2, N_EDGES), 0, N_NODES, dtype=jnp.int64)
        edge_type = jax.random.randint(k3, (N_EDGES,), 0, N_RATINGS, dtype=jnp.int64)
        B = jax.random.normal(k4, (N_BASES, D_OUT, D_IN), dtype=jnp.float32) * 0.05
        A = jax.random.normal(k5, (N_RATINGS, N_BASES), dtype=jnp.float32) * 0.05
        W0 = jax.random.normal(k6, (D_OUT, D_IN), dtype=jnp.float32) * 0.05
        return {'x': x, 'edge_index': edge_index, 'edge_type': edge_type, 'B': B, 'A': A, 'W0': W0}
    _L0_gnn_all = _L0_gnn_setup()
    _L0_gnn_in = {k: v for k, v in _L0_gnn_all.items() if k in ('B', 'A', 'W0')}
    del _L0_gnn_all

    def _L1_gnn_setup():
        import jax, jax.numpy as jnp
        import numpy as np
        N_NODES = 50000
        N_EDGES = 25000
        D_FEAT = 128
        D_OUT = 128
        key = jax.random.key(seed)
        k1, k2, k3, k4 = jax.random.split(key, 4)
        x = jax.random.normal(k1, (N_NODES, D_FEAT), dtype=jnp.float32)
        edge_index = jax.random.randint(k2, (2, N_EDGES), 0, N_NODES, dtype=jnp.int64)
        W = jax.random.normal(k3, (D_OUT, 2 * D_FEAT), dtype=jnp.float32) * (1.0 / np.sqrt(2 * D_FEAT))
        b = jax.random.normal(k4, (D_OUT,), dtype=jnp.float32) * 0.01
        return {'x': x, 'edge_index': edge_index, 'W': W, 'b': b}
    _L1_gnn_all = _L1_gnn_setup()
    _L1_gnn_in = {k: v for k, v in _L1_gnn_all.items() if k in ('W', 'b')}
    del _L1_gnn_all

    def _L2_gnn_setup():
        import jax, jax.numpy as jnp
        import numpy as np
        NEG_SLOPE = 0.2
        BN_EPS = 1e-05
        key = jax.random.key(seed)
        ks = jax.random.split(key, 5)
        N, E, D_IN, D_OUT = (3125, 50000, 128, 128)
        feature = jax.random.normal(ks[0], (N, D_IN), dtype=jnp.float32)
        src = jax.random.randint(ks[1], (E,), 0, N, dtype=jnp.int64)
        dst = jax.random.randint(ks[2], (E,), 0, N, dtype=jnp.int64)
        W = jax.random.normal(ks[3], (D_OUT, D_IN), dtype=jnp.float32) * (1.0 / np.sqrt(D_IN))
        b = jax.random.normal(ks[4], (D_OUT,), dtype=jnp.float32) * 0.01
        gamma = jnp.ones((D_OUT,), dtype=jnp.float32)
        beta = jnp.zeros((D_OUT,), dtype=jnp.float32)
        return {'feature': feature, 'src': src, 'dst': dst, 'W': W, 'b': b, 'gamma': gamma, 'beta': beta}
    _L2_gnn_all = _L2_gnn_setup()
    _L2_gnn_in = {k: v for k, v in _L2_gnn_all.items() if k in ('W', 'b', 'gamma', 'beta')}
    del _L2_gnn_all

    def _L3_gnn_setup():
        import jax, jax.numpy as jnp
        import numpy as np
        N_NODES = 50000
        N_EDGES = 25000
        IN_CH = 128
        HIDDEN = 32
        HEADS = 4
        OUT_CH = 128

        def _lin_params(key, fan_in, fan_out):
            kw, kb = jax.random.split(key)
            scale = 1.0 / np.sqrt(fan_in)
            W = jax.random.uniform(kw, (fan_in, fan_out), minval=-scale, maxval=scale, dtype=jnp.float32)
            b = jax.random.uniform(kb, (fan_out,), minval=-scale, maxval=scale, dtype=jnp.float32)
            return (W, b)

        def transformer_conv(x, src, dst, Wq, bq, Wk, bk, Wv, bv, Ws, bs, heads, n_nodes):
            H = heads
            d = Wq.shape[1] // H
            q = (x @ Wq + bq).reshape(n_nodes, H, d)
            k = (x @ Wk + bk).reshape(n_nodes, H, d)
            v = (x @ Wv + bv).reshape(n_nodes, H, d)
            q_e = q[dst]
            k_e = k[src]
            alpha = jnp.einsum('ehd,ehd->eh', q_e, k_e) / jnp.sqrt(jnp.float32(d))
            m = jax.ops.segment_max(alpha, dst, num_segments=n_nodes)
            m = jnp.where(jnp.isfinite(m), m, 0.0)
            e = jnp.exp(alpha - m[dst])
            denom = jax.ops.segment_sum(e, dst, num_segments=n_nodes)
            attn = e / (denom[dst] + 1e-16)
            msg = v[src] * attn[:, :, None]
            out = jax.ops.segment_sum(msg, dst, num_segments=n_nodes)
            out = out.reshape(n_nodes, H * d)
            return out + (x @ Ws + bs)
        key = jax.random.key(seed)
        ks = jax.random.split(key, 10)
        x = jax.random.normal(ks[0], (N_NODES, IN_CH), dtype=jnp.float32)
        edge_index = jax.random.randint(ks[1], (2, N_EDGES), 0, N_NODES, dtype=jnp.int64)
        d1 = HIDDEN * HEADS
        Wq1, bq1 = _lin_params(ks[2], IN_CH, d1)
        Wk1, bk1 = _lin_params(ks[3], IN_CH, d1)
        Wv1, bv1 = _lin_params(ks[4], IN_CH, d1)
        Ws1, bs1 = _lin_params(ks[5], IN_CH, d1)
        Wq2, bq2 = _lin_params(ks[6], d1, OUT_CH)
        Wk2, bk2 = _lin_params(ks[7], d1, OUT_CH)
        Wv2, bv2 = _lin_params(ks[8], d1, OUT_CH)
        Ws2, bs2 = _lin_params(ks[9], d1, OUT_CH)
        return dict(x=x, edge_index=edge_index, Wq1=Wq1, bq1=bq1, Wk1=Wk1, bk1=bk1, Wv1=Wv1, bv1=bv1, Ws1=Ws1, bs1=bs1, Wq2=Wq2, bq2=bq2, Wk2=Wk2, bk2=bk2, Wv2=Wv2, bv2=bv2, Ws2=Ws2, bs2=bs2)
    _L3_gnn_all = _L3_gnn_setup()
    _L3_gnn_in = {k: v for k, v in _L3_gnn_all.items() if k in ('Wq1', 'bq1', 'Wk1', 'bk1', 'Wv1', 'bv1', 'Ws1', 'bs1', 'Wq2', 'bq2', 'Wk2', 'bk2', 'Wv2', 'bv2', 'Ws2', 'bs2')}
    del _L3_gnn_all
    return {'x': x, 'src': src, 'dst': dst, 'edge_type_5': edge_type_5, 'L0_gnn_B': _L0_gnn_in['B'], 'L0_gnn_A': _L0_gnn_in['A'], 'L0_gnn_W0': _L0_gnn_in['W0'], 'L1_gnn_W': _L1_gnn_in['W'], 'L1_gnn_b': _L1_gnn_in['b'], 'L2_gnn_W': _L2_gnn_in['W'], 'L2_gnn_b': _L2_gnn_in['b'], 'L2_gnn_gamma': _L2_gnn_in['gamma'], 'L2_gnn_beta': _L2_gnn_in['beta'], 'L3_gnn_Wq1': _L3_gnn_in['Wq1'], 'L3_gnn_bq1': _L3_gnn_in['bq1'], 'L3_gnn_Wk1': _L3_gnn_in['Wk1'], 'L3_gnn_bk1': _L3_gnn_in['bk1'], 'L3_gnn_Wv1': _L3_gnn_in['Wv1'], 'L3_gnn_bv1': _L3_gnn_in['bv1'], 'L3_gnn_Ws1': _L3_gnn_in['Ws1'], 'L3_gnn_bs1': _L3_gnn_in['bs1'], 'L3_gnn_Wq2': _L3_gnn_in['Wq2'], 'L3_gnn_bq2': _L3_gnn_in['bq2'], 'L3_gnn_Wk2': _L3_gnn_in['Wk2'], 'L3_gnn_bk2': _L3_gnn_in['bk2'], 'L3_gnn_Wv2': _L3_gnn_in['Wv2'], 'L3_gnn_bv2': _L3_gnn_in['bv2'], 'L3_gnn_Ws2': _L3_gnn_in['Ws2'], 'L3_gnn_bs2': _L3_gnn_in['bs2']}

def reference(x, src, dst, edge_type_5, L0_gnn_B, L0_gnn_A, L0_gnn_W0, L1_gnn_W, L1_gnn_b, L2_gnn_W, L2_gnn_b, L2_gnn_gamma, L2_gnn_beta, L3_gnn_Wq1, L3_gnn_bq1, L3_gnn_Wk1, L3_gnn_bk1, L3_gnn_Wv1, L3_gnn_bv1, L3_gnn_Ws1, L3_gnn_bs1, L3_gnn_Wq2, L3_gnn_bq2, L3_gnn_Wk2, L3_gnn_bk2, L3_gnn_Wv2, L3_gnn_bv2, L3_gnn_Ws2, L3_gnn_bs2):
    import jax
    import jax.numpy as jnp

    def _L0_gnn_ref(x, edge_index, edge_type, B, A, W0):
        import jax, jax.numpy as jnp
        import numpy as np
        N_NODES = 50000
        N_EDGES = 18750
        D_IN = 128
        D_OUT = 128
        N_BASES = 4
        N_RATINGS = 5
        n_nodes = x.shape[0]
        src, tgt = (edge_index[0], edge_index[1])
        out = x @ W0.T
        W = jnp.einsum('rk,kod->rod', A, B)
        n_ratings = A.shape[0]
        for r in range(n_ratings):
            h = x @ W[r].T
            msg = jnp.where((edge_type == r)[:, None], h[src], jnp.float32(0))
            out = out + jax.ops.segment_sum(msg, tgt, num_segments=n_nodes)
        return out

    def _L1_gnn_ref(x, edge_index, W, b):
        import jax, jax.numpy as jnp
        import numpy as np
        N_NODES = 50000
        N_EDGES = 25000
        D_FEAT = 128
        D_OUT = 128
        src, dst = (edge_index[0], edge_index[1])
        agg = jax.ops.segment_sum(x[src], dst, num_segments=x.shape[0])
        h = jnp.concatenate([x, agg], axis=1)
        h = h @ W.T + b
        return jax.nn.relu(h)

    def _L2_gnn_ref(feature, src, dst, W, b, gamma, beta):
        import jax, jax.numpy as jnp
        import numpy as np
        NEG_SLOPE = 0.2
        BN_EPS = 1e-05
        N = feature.shape[0]
        h = jnp.where(feature >= 0, feature, NEG_SLOPE * feature)
        agg = jax.ops.segment_sum(h[src], dst, num_segments=N)
        z = jnp.einsum('nd,od->no', agg, W) + b
        mean = jnp.mean(z, axis=0)
        var = jnp.mean((z - mean) ** 2, axis=0)
        out = gamma * (z - mean) * jax.lax.rsqrt(var + BN_EPS) + beta
        return out

    def _L3_gnn_ref(x, edge_index, Wq1, bq1, Wk1, bk1, Wv1, bv1, Ws1, bs1, Wq2, bq2, Wk2, bk2, Wv2, bv2, Ws2, bs2):
        import jax, jax.numpy as jnp
        import numpy as np
        N_NODES = 50000
        N_EDGES = 25000
        IN_CH = 128
        HIDDEN = 32
        HEADS = 4
        OUT_CH = 128

        def _lin_params(key, fan_in, fan_out):
            kw, kb = jax.random.split(key)
            scale = 1.0 / np.sqrt(fan_in)
            W = jax.random.uniform(kw, (fan_in, fan_out), minval=-scale, maxval=scale, dtype=jnp.float32)
            b = jax.random.uniform(kb, (fan_out,), minval=-scale, maxval=scale, dtype=jnp.float32)
            return (W, b)

        def transformer_conv(x, src, dst, Wq, bq, Wk, bk, Wv, bv, Ws, bs, heads, n_nodes):
            H = heads
            d = Wq.shape[1] // H
            q = (x @ Wq + bq).reshape(n_nodes, H, d)
            k = (x @ Wk + bk).reshape(n_nodes, H, d)
            v = (x @ Wv + bv).reshape(n_nodes, H, d)
            q_e = q[dst]
            k_e = k[src]
            alpha = jnp.einsum('ehd,ehd->eh', q_e, k_e) / jnp.sqrt(jnp.float32(d))
            m = jax.ops.segment_max(alpha, dst, num_segments=n_nodes)
            m = jnp.where(jnp.isfinite(m), m, 0.0)
            e = jnp.exp(alpha - m[dst])
            denom = jax.ops.segment_sum(e, dst, num_segments=n_nodes)
            attn = e / (denom[dst] + 1e-16)
            msg = v[src] * attn[:, :, None]
            out = jax.ops.segment_sum(msg, dst, num_segments=n_nodes)
            out = out.reshape(n_nodes, H * d)
            return out + (x @ Ws + bs)
        src = edge_index[0]
        dst = edge_index[1]
        n = x.shape[0]
        h = transformer_conv(x, src, dst, Wq1, bq1, Wk1, bk1, Wv1, bv1, Ws1, bs1, HEADS, n)
        h = jax.nn.relu(h)
        out = transformer_conv(h, src, dst, Wq2, bq2, Wk2, bk2, Wv2, bv2, Ws2, bs2, 1, n)
        return out
    edge_index = jnp.stack([src, dst])
    h = jnp.maximum(_layernorm(x, axis=-1), 0.0)
    x = x + _L0_gnn_ref(h, edge_index, edge_type_5, L0_gnn_B, L0_gnn_A, L0_gnn_W0)
    h = jnp.maximum(_layernorm(x, axis=-1), 0.0)
    x = x + _L1_gnn_ref(h, edge_index, L1_gnn_W, L1_gnn_b)
    h = jnp.maximum(_layernorm(x, axis=-1), 0.0)
    x = x + _L2_gnn_ref(h, src, dst, L2_gnn_W, L2_gnn_b, L2_gnn_gamma, L2_gnn_beta)
    h = jnp.maximum(_layernorm(x, axis=-1), 0.0)
    x = x + _L3_gnn_ref(h, edge_index, L3_gnn_Wq1, L3_gnn_bq1, L3_gnn_Wk1, L3_gnn_bk1, L3_gnn_Wv1, L3_gnn_bv1, L3_gnn_Ws1, L3_gnn_bs1, L3_gnn_Wq2, L3_gnn_bq2, L3_gnn_Wk2, L3_gnn_bk2, L3_gnn_Wv2, L3_gnn_bv2, L3_gnn_Ws2, L3_gnn_bs2)
    return x

_drawn_inputs = setup_inputs


def setup_inputs(seed=0):
    import zlib

    import numpy as np

    out = dict(_drawn_inputs(seed))
    spreads = {'L2_gnn_gamma': (1.0, 0.2), 'L2_gnn_beta': (0.0, 0.302)}
    factors = {'L1_gnn_b': 30.329,
     'L2_gnn_b': 200.0,
     'L3_gnn_Wq1': 8.0,
     'L3_gnn_bq1': 64.0,
     'L3_gnn_Wk1': 8.0,
     'L3_gnn_bk1': 200.0,
     'L3_gnn_bv1': 7.584,
     'L3_gnn_bs1': 7.306,
     'L3_gnn_Wq2': 23.825,
     'L3_gnn_bq2': 200.0,
     'L3_gnn_Wk2': 23.208,
     'L3_gnn_bk2': 200.0,
     'L3_gnn_bv2': 4.508,
     'L3_gnn_bs2': 4.815}
    for name, (base, spread) in spreads.items():
        noise = np.random.default_rng([zlib.crc32(name.encode()), seed]).standard_normal(out[name].shape)
        drawn = base * np.exp(spread * noise) if base else spread * noise
        out[name] = jnp.asarray(drawn.astype(out[name].dtype))
    for name, factor in factors.items():
        out[name] = (out[name] * factor).astype(out[name].dtype)
    return out
```

```python
from collections import namedtuple
from contextlib import ExitStack

import concourse.bass as bass
from concourse import mybir

ALU = mybir.AluOpType
ACT = mybir.ActivationFunctionType
AX = mybir.AxisListType
BF16 = mybir.dt.bfloat16
F32 = mybir.dt.float32
I32 = mybir.dt.int32

P = 128
N, D, E = 3125, 128, 53125
NB = 25
BN = N // NB
TJ = 18
GE = TJ * P
CH = 3
NC = TJ // CH
GG = -(-E // GE)
TYPES, BASES = 5, 4
HALF = TJ // 2
EW = 425
ER = E // EW
FAR = 1.0e6
BIG = float(2 ** 100)
EPS = 1e-5
LAYERS = 5
HEADS = (0, 0, 0, 4, 1)
TABLE = (TYPES * D, D, D, 2 * D, 2 * D)
KV = 2 * D + 4
assert NB * BN == N and ER * EW == E and NB % 2 == 1 and GG % 2 == 0 and TJ * NB >= TJ * GG

Turn = namedtuple("Turn", "half use logit top msg acc block col")


def sorted_turns(eng, layer):
    att = max(layer - 3, 0) * NB

    def turn(half, i, b):
        return Turn(half, ((NB + 1) // 2 if half == 0 else NB // 2) * layer + i, att + b, att + b, att + b,
                    NB * layer + b, b, b)

    with eng.Fori(0, NB // 2) as i:
        yield turn(0, i, 2 * i)
        yield turn(1, i, 2 * i + 1)
    yield turn(0, NB // 2, NB - 1)


def any_turns(eng, layer, block, sweep):
    h = GG // 2
    att = layer - 3
    use0 = NB * h * layer if layer < 3 else NB * h * 3 + 2 * NB * h * att
    with eng.Fori(0, h) as k:
        for half in range(2):
            g = 2 * k + half
            n = block * GG + g
            if layer < 3:
                yield Turn(half, use0 + block * h + k, 0, 0, 0, NB * GG * layer + n, block, g)
            else:
                yield Turn(half, use0 + block * GG + sweep * h + k,
                           2 * NB * GG * att + block * (2 * GG) + sweep * GG + g,
                           NB * GG * att + n, NB * GG * att + n, NB * GG * layer + n, block, g)


def halves(eng, layer):
    with eng.Fori(0, NB // 2) as i:
        yield 0, (NB + 1) // 2 * layer + i, 2 * i
        yield 1, NB // 2 * layer + i, 2 * i + 1
    yield 0, (NB + 1) // 2 * layer + NB // 2, NB - 1


def build(nc, x, src, dst, etype, B, A, W0, W1, b1, W2, b2, gamma, beta, att1, att2, out):
    with ExitStack() as ctx:
        def sb(name, shape, dt=F32):
            return ctx.enter_context(nc.sbuf_tensor(name, shape, dt))

        def sem(name):
            return ctx.enter_context(nc.semaphore(name))

        def pair(name):
            return [sem(f"{name}{i}") for i in range(2)]

        bank = [ctx.enter_context(nc.psum_tensor(f"bank{i}", [P, 512], F32)) for i in range(8)]
        ps_qe, ps_st, ps_mx, ps_misc, ps_acc = bank[0:2], bank[2:4], bank[4:6], bank[6], bank[7]

        xs = sb("xs", [BN, NB * D])
        xc = sb("xc", [BN, NB * D])
        root = sb("root", [BN, NB * D])
        qs = sb("qs", [BN, NB * D])
        stat = sb("stat", [BN, 4 * NB])
        hcur = sb("hcur", [BN, 2, D])
        hT = sb("hT", [P, 2, BN])
        rows = sb("rows", [BN, 2, TYPES * D])
        bn_s = sb("bn_s", [BN, 4, D])
        src_i = sb("src_i", [P, NB * TJ], I32)
        dst_i = sb("dst_i", [P, NB * TJ], I32)
        typ_i = sb("typ_i", [P, NB * TJ], I32)
        dst_f = sb("dst_f", [P, NB * TJ])
        idx = sb("idx", [P, 2, TJ], I32)
        dloc = sb("dloc", [P, 2, TJ])
        kv = sb("kv", [P, 2, TJ, KV])
        S = sb("S", [P, 2, TJ, BN])
        ST = sb("ST", [BN, 2, TJ, P])
        mask = sb("mask", [BN, 2, TJ, P], BF16)
        prod = sb("prod", [P, 2, CH * D])
        alpha = sb("alpha", [P, 2, TJ * 4])
        rest = sb("rest", [P, 2, TJ * 4])
        parts = sb("parts", [P, TJ * 4, 3], BF16)
        partsT = sb("partsT", [HALF * 12, 2, P], BF16)
        tops = sb("tops", [BN, 4, TJ])
        top = sb("top", [BN, 4])
        topn = sb("topn", [BN, 4])
        den = sb("den", [BN, 4])
        rden = sb("rden", [BN, 4])
        onorm = sb("onorm", [BN, D])
        msum = sb("msum", [BN, D + 4])
        iota_n = sb("iota_n", [P, BN])
        iota_e = sb("iota_e", [P, TJ])
        base_n = sb("base_n", [P, NB])
        ident = sb("ident", [P, P])
        ident_b = sb("ident_b", [P, P], BF16)
        sel = sb("sel", [HALF * 12, HALF * 4, BN], BF16)
        ones = sb("ones", [P, P])
        w_in = sb("w_in", [P, 4 * D])
        w_r = sb("w_r", [P, 9, D])
        a_bc = sb("a_bc", [P, TYPES * BASES])
        w0 = sb("w0", [P, (TYPES + 1) * D])
        w1 = sb("w1", [P, 2 * D])
        w2 = sb("w2", [P, D])
        w3 = sb("w3", [P, 4 * D])
        w4 = sb("w4", [P, 4 * D])
        bias1, bias2, gam, bet = (sb(n, [BN, D]) for n in ("bias1", "bias2", "gam", "bet"))
        bias3 = sb("bias3", [BN, 4 * D])
        bias4 = sb("bias4", [BN, 4 * D])
        all_i = S[0:ER, 0, 0:4, :].rearrange("p a b -> p (a b)").bitcast(I32)[:, 0:EW]
        all_f = S[0:ER, 0, 4:8, :].rearrange("p a b -> p (a b)")[:, 0:EW]
        hits = S[0:ER, 0, 8:12, :].rearrange("p a b -> p (a b)")[:, 0:EW]
        nxt_i = sb("nxt_i", [ER, 1], I32)
        nxt_f = sb("nxt_f", [ER, 1])
        cnt = sb("cnt", [ER, NB + 3])
        total = sb("total", [1, NB + 3])
        steps = sb("steps", [1, NB + 3])
        plan_f = sb("plan_f", [1, NB + 3])
        plan = sb("plan", [1, NB + 3], I32)

        tables = [nc.dram_tensor(f"table{i}", (N, TABLE[i]), F32, kind="Internal").ap() for i in range(LAYERS)]

        in_x, in_w, in_b, in_all, in_a = sem("in_x"), sem("in_w"), sem("in_b"), sem("in_all"), sem("in_a")
        pool_step, dve_step, act_step = sem("pool_step"), sem("dve_step"), sem("act_step")
        consts_made, w_made, w_turned = sem("consts_made"), sem("w_made"), sem("w_turned")
        w_copied, all_made, counted, planned = sem("w_copied"), sem("all_made"), sem("counted"), sem("planned")
        edges_in, edges_made = sem("edges_in"), sem("edges_made")
        var_made, std_made, bn_asked, bn_summed = sem("var_made"), sem("std_made"), sem("bn_asked"), sem("bn_summed")
        h_made, h_turned, ht_copied = pair("h_made"), pair("h_turned"), pair("ht_copied")
        relu_made = pair("relu_made")
        lin_made, lin_read, rows_out = pair("lin_made"), pair("lin_read"), pair("rows_out")
        idx_made, dloc_made, s_made, group_used = pair("idx_made"), pair("dloc_made"), pair("s_made"), pair("group_used")
        gathered = [[sem(f"gathered{h}_{c}") for c in range(NC)] for h in range(2)]
        acc_read, idx_seen, sums_cleared = sem("acc_read"), sem("idx_seen"), sem("sums_cleared")
        st_made, st_copied, qe_made, qe_read = pair("st_made"), pair("st_copied"), pair("qe_made"), pair("qe_read")
        logits_made = pair("logits_made")
        split, parts_turned, parts_copied = (
            sem("split"), sem("parts_turned"), sem("parts_copied"))
        mx_made, mx_read = pair("mx_made"), pair("mx_read")
        top_made, top_all, me_made, shifted, exp_made, v_scaled, normed, out_added = (
            sem("top_made"), sem("top_all"), sem("me_made"), sem("shifted"), sem("exp_made"), sem("v_scaled"),
            sem("normed"), sem("out_added"))
        x_done, stored = sem("x_done"), sem("stored")

        block = ctx.enter_context(nc.Block())

        def cols(t, b, w=D):
            return t[:, bass.ds(b * w, w)] if not isinstance(b, int) else t[:, b * w:(b + 1) * w]

        WALL = [w0, w1, w2, w3, w4]

        def layers_sp(sp):
            for layer in range(LAYERS):
                tab = tables[layer]
                for half, use, b in halves(sp, layer):
                    to = tab[bass.ds(b * BN, BN), :]
                    sp.wait_ge(lin_read[half], use + 1)
                    sp.dma_start(to, rows[:, half, 0:TABLE[layer]]).then_inc(rows_out[half], 16)
            sp.wait_ge(x_done, 1)
            sp.dma_start(out.rearrange("(b p) d -> p b d", p=BN), xs[:].rearrange("p (b d) -> p b d", d=D)).then_inc(stored, 16)
            sp.wait_ge(stored, 16)
            sp.wait_ge(rows_out[0], 16 * LAYERS * ((NB + 1) // 2))
            sp.wait_ge(rows_out[1], 16 * LAYERS * (NB // 2))

        @block.sync
        def _(sp):
            sp.dma_start(all_i, dst.rearrange("(p w) -> p w", w=EW)).then_inc(in_all, 16)
            sp.dma_start(nxt_i[0:ER - 1, :], dst[EW:E].rearrange("(p w) -> p w", w=EW)[:, 0:1],
                         allow_slow_non_contiguous=True).then_inc(in_all, 16)
            sp.dma_start(xs[:].rearrange("p (b d) -> p b d", d=D), x.rearrange("(b p) d -> p b d", p=BN)).then_inc(in_x, 16)
            sp.wait_ge(planned, 1)
            together = sp.value_load(plan[0:1, NB:NB + 1], min_val=0, max_val=1)
            with sp.If(together > 0):
                with sp.Fori(0, NB) as b:
                    at = sp.value_load(plan[0:1, bass.ds(b, 1)], min_val=0, max_val=E - GE)
                    for arr, own in ((dst, dst_i), (src, src_i), (etype, typ_i)):
                        sp.dma_start(own[:, bass.ds(b * TJ, TJ)],
                                     arr[bass.ds(at, GE)].rearrange("(p j) -> p j", j=TJ)).then_inc(edges_in, 16)
                layers_sp(sp)
            with sp.Else():
                with sp.Fori(0, GG - 1) as g:
                    for arr, own in ((dst, dst_i), (src, src_i), (etype, typ_i)):
                        sp.dma_start(own[:, bass.ds(g * TJ, TJ)],
                                     arr[bass.ds(g * GE, GE)].rearrange("(p j) -> p j", j=TJ)).then_inc(edges_in, 16)
                for arr, own in ((dst, dst_i), (src, src_i), (etype, typ_i)):
                    sp.dma_start(own[:, (GG - 1) * TJ:GG * TJ],
                                 arr[E - GE:E].rearrange("(p j) -> p j", j=TJ)).then_inc(edges_in, 16)
                layers_sp(sp)
            sp.nop()

        def layers_pool(pool, together):
            pool.wait_ge(edges_made, 3)

            def gather(t, layer):
                own = (typ_i if layer == 0 else src_i)[:, bass.ds(t.col * TJ, TJ)] if not isinstance(t.col, int) \
                    else (typ_i if layer == 0 else src_i)[:, t.col * TJ:(t.col + 1) * TJ]
                table = tables[layer] if layer else tables[0].rearrange("n (r d) -> (n r) d", d=D)
                w = table.shape[1]
                pool.wait_ge(group_used[t.half], t.use)
                pool.wait_ge(edges_made, 3)
                pool.tensor_copy(idx[:, t.half, :], own).then_inc(idx_made[t.half], 1)
                pool.wait_ge(idx_made[t.half], t.use + 1)
                pool.sem_inc(idx_seen, 1)
                for j in range(TJ):
                    pool.indirect_dma_start(kv[:, t.half, j, 0:w], None, table,
                                            bass.IndirectOffsetOnAxis(ap=idx[:, t.half, j:j + 1], axis=0)
                                            ).then_inc(gathered[t.half][j // CH], 16)

            for layer in range(LAYERS):
                pool.wait_ge(rows_out[0], 16 * (layer + 1) * ((NB + 1) // 2))
                pool.wait_ge(rows_out[1], 16 * (layer + 1) * (NB // 2))
                if together:
                    for t in sorted_turns(pool, layer):
                        gather(t, layer)
                else:
                    with pool.Fori(0, NB) as b:
                        for sweep in range(1 if layer < 3 else 2):
                            for t in any_turns(pool, layer, b, sweep):
                                gather(t, layer)

        @block.gpsimd
        def _(pool):
            pool.iota(iota_n[:], [[1, BN]], base=0, channel_multiplier=0, allow_small_or_imprecise_dtypes=True)
            pool.iota(iota_e[:], [[1, TJ]], base=0, channel_multiplier=TJ, allow_small_or_imprecise_dtypes=True)
            pool.iota(base_n[:], [[BN, NB]], base=0, channel_multiplier=0, allow_small_or_imprecise_dtypes=True)
            pool.memset(ones[:], 1.0).then_inc(pool_step, 1)
            pool.memset(ident[:], 0.0).then_inc(pool_step, 1)
            pool.memset(sel[:], 1.0).then_inc(pool_step, 1)
            pool.memset(nxt_f[:], FAR).then_inc(pool_step, 1)
            pool.wait_ge(pool_step, 4)
            pool.affine_select(out=ident[:], in_=ident[:], compare_op=ALU.not_equal, fill=1.0, base=0,
                               pattern=[[-1, P]], channel_multiplier=1).then_inc(pool_step, 1)
            pool.affine_select(out=sel[:], in_=sel[:], compare_op=ALU.is_ge, fill=0.0, base=0,
                               pattern=[[-3, HALF * 4], [0, BN]], channel_multiplier=1).then_inc(pool_step, 1)
            pool.wait_ge(pool_step, 6)
            pool.affine_select(out=sel[:], in_=sel[:], compare_op=ALU.is_ge, fill=0.0, base=2,
                               pattern=[[3, HALF * 4], [0, BN]], channel_multiplier=-1).then_inc(pool_step, 1)
            pool.wait_ge(pool_step, 7)
            pool.tensor_copy(ident_b[:], ident[:]).then_inc(consts_made, 1)
            pool.wait_ge(planned, 1)
            together = pool.value_load(plan[0:1, NB:NB + 1], min_val=0, max_val=1)
            with pool.If(together > 0):
                layers_pool(pool, True)
            with pool.Else():
                layers_pool(pool, False)
            pool.nop()

        def layers_act(act, together):
            def turned_rows(layer):
                for half, use, b in halves(act, layer):
                    act.wait_ge(h_turned[half], use + 1)
                    act.copy(hT[:, half, :], ps_st[half][:, 0:BN]).then_inc(ht_copied[half], 1)

            def logit(t):
                for c in range(NC):
                    k = c % 2
                    if c == 0:
                        act.wait_ge(group_used[t.half], t.use)
                    act.wait_ge(st_made[k], t.logit * (NC // 2) + c // 2 + 1)
                    at = ps_st[k][0:BN, 0:CH * P].rearrange("p (j e) -> p j e", e=P)
                    act.activation(mask[:, t.half, c * CH:(c + 1) * CH, :], at, ACT.Copy, bias=-BIG, scale=BIG)
                    act.copy(ST[:, t.half, c * CH:(c + 1) * CH, :], at).then_inc(st_copied[k], 1)

            def turn_parts(t, H):
                act.wait_ge(parts_turned, t.top + 1)
                act.copy(partsT[0:HALF * H * 3, :, :],
                         ps_misc[:].bitcast(BF16)[0:HALF * H * 3, 0:2 * P].rearrange("k (a e) -> k a e", e=P)
                         ).then_inc(parts_copied, 1)

            def exponent(t, H, scale):
                act.wait_ge(shifted, t.msg + 1)
                act.activation(kv[:, t.half, :, 2 * D:2 * D + H], rest[:, t.half, 0:TJ * H].rearrange("p (j h) -> p j h", h=H),
                               ACT.Exp, scale=scale).then_inc(exp_made, 1)

            stds = 0
            for layer in range(LAYERS):
                H = HEADS[layer]
                if layer < 4:
                    stds += 1
                    act.wait_ge(var_made, stds)
                    act.sqrt(stat[:, 3 * NB:4 * NB], stat[:, 2 * NB:3 * NB]).then_inc(std_made, 1)
                turned_rows(layer)
                if H:
                    scale = float(H / D) ** 0.5
                    if together:
                        for t in sorted_turns(act, layer):
                            logit(t)
                            turn_parts(t, H)
                            exponent(t, H, scale)
                    else:
                        with act.Fori(0, NB) as b:
                            for t in any_turns(act, layer, b, 0):
                                logit(t)
                                turn_parts(t, H)
                            for t in any_turns(act, layer, b, 1):
                                logit(t)
                                exponent(t, H, scale)
                if layer == 2:
                    stds += 1
                    act.wait_ge(var_made, stds)
                    act.sqrt(bn_s[:, 3, :], bn_s[:, 2, :]).then_inc(std_made, 1)

        @block.scalar
        def _(act):
            act.dma_start(w_in[:].rearrange("o (k d) -> o k d", d=D), B.rearrange("k o d -> o k d")).then_inc(in_w, 16)
            act.dma_start(a_bc[:], A.rearrange("r k -> (r k)").rearrange("(a n) -> a n", a=1).to_broadcast([P, TYPES * BASES])).then_inc(in_w, 16)
            act.dma_start(w_r[:, TYPES, :], W0).then_inc(in_w, 16)
            act.dma_start(w_r[:, TYPES + 1:TYPES + 3, :].rearrange("o a d -> o (a d)"), W1).then_inc(in_w, 16)
            act.dma_start(w_r[:, TYPES + 3, :], W2).then_inc(in_w, 16)
            for vec, own in ((b1, bias1), (b2, bias2), (gamma, gam), (beta, bet)):
                act.dma_start(own[:], vec.rearrange("(a n) -> a n", a=1).to_broadcast([BN, D])).then_inc(in_b, 16)
            for (ws, bs), w, bias in ((att1, w3, bias3), (att2, w4, bias4)):
                for k in range(4):
                    act.dma_start(w[:, k * D:(k + 1) * D], ws[k]).then_inc(in_a, 16)
                    act.dma_start(bias[:, k * D:(k + 1) * D],
                                  bs[k].rearrange("(a n) -> a n", a=1).to_broadcast([BN, D])).then_inc(in_a, 16)
            for k in range(3):
                act.wait_ge(w_turned, k + 1)
                outs = (w0[:, 0:3 * D], w0[:, 3 * D:6 * D], None)[k]
                if k < 2:
                    act.copy(outs, ps_st[k][:, 0:3 * D]).then_inc(w_copied, 1)
                else:
                    act.copy(w1[:, D:2 * D], ps_qe[0][:, 0:D])
                    act.copy(w1[:, 0:D], ps_qe[0][:, D:2 * D])
                    act.copy(w2[:], ps_qe[0][:, 2 * D:3 * D]).then_inc(w_copied, 1)
            act.wait_ge(planned, 1)
            together = act.value_load(plan[0:1, NB:NB + 1], min_val=0, max_val=1)
            with act.If(together > 0):
                layers_act(act, True)
            with act.Else():
                layers_act(act, False)
            act.nop()

        def layers_pe(pe, together):
            def linear(layer):
                w = WALL[layer]
                width = w.shape[1]
                for half, use, b in halves(pe, layer):
                    pe.wait_ge(h_made[half], use + 1)
                    pe.transpose(ps_st[half][:, 0:BN], hcur[:, half, :], ident[0:BN, 0:BN]).then_inc(h_turned[half], 1)
                    pe.wait_ge(lin_read[half], use)
                    pe.wait_ge(ht_copied[half], use + 1)
                    for k, to in enumerate((ps_qe[half], ps_mx[half])[0:-(-width // 512)]):
                        n = min(512, width - 512 * k)
                        mm = pe.matmul(to[0:BN, 0:n], hT[:, half, :], w[:, 512 * k:512 * k + n], start=True, stop=True)
                    mm.then_inc(lin_made[half], 1)

            def add_up(t, H):
                lo, w = (D, D + H) if H else (0, D)
                for c in range(NC):
                    if c == 0:
                        pe.wait_ge(acc_read, t.acc)
                    if H:
                        pe.wait_ge(v_scaled, t.msg * NC + c + 1)
                    else:
                        pe.wait_ge(gathered[t.half][c], 16 * CH * (t.use + 1))
                        pe.wait_ge(s_made[t.half], t.use * NC + c + 1)
                    for j in range(c * CH, (c + 1) * CH):
                        mm = pe.matmul(ps_acc[0:BN, 0:w], S[:, t.half, j, :], kv[:, t.half, j, lo:lo + w],
                                       start=(j == 0), stop=(j == TJ - 1))
                mm.then_inc(group_used[t.half], 1)

            def logit(t):
                def turn(c):
                    k = c % 2
                    pe.wait_ge(s_made[t.half], t.use * NC + c + 1)
                    pe.wait_ge(st_copied[k], t.logit * (NC // 2) + c // 2)
                    for i in range(CH):
                        mm = pe.transpose(ps_st[k][0:BN, i * P:(i + 1) * P], S[:, t.half, c * CH + i, :], ident[:])
                    mm.then_inc(st_made[k], 1)

                def queries(c):
                    k = c % 2
                    pe.wait_ge(st_copied[k], t.logit * (NC // 2) + c // 2 + 1)
                    pe.wait_ge(qe_read[k], t.logit * (NC // 2) + c // 2)
                    for i in range(CH):
                        mm = pe.matmul(ps_qe[k][:, i * D:(i + 1) * D], ST[:, t.half, c * CH + i, :], cols(qs, t.block),
                                       start=True, stop=True)
                    mm.then_inc(qe_made[k], 1)

                turn(0)
                for c in range(NC):
                    if c + 1 < NC:
                        turn(c + 1)
                    queries(c)

            def maxima(t, H, last):
                pe.wait_ge(split, 5 * (t.top + 1))
                n = HALF * H * 3
                for a in range(2):
                    mm = pe.transpose(ps_misc[:].bitcast(BF16)[0:n, a * P:(a + 1) * P],
                                      parts[:, a * HALF * H:(a + 1) * HALF * H, :].rearrange("p i k -> p (i k)"), ident_b[:])
                mm.then_inc(parts_turned, 1)
                pe.wait_ge(parts_copied, t.top + 1)
                for j in range(TJ):
                    k = j % 2
                    pe.wait_ge(mx_read[k], t.top * HALF + j // 2)
                    own = mask[:, t.half, j, :]
                    for h in range(H):
                        pe.matmul(ps_mx[k][0:BN, h * P:(h + 1) * P], ident_b[0:BN, 0:BN], own, start=True, stop=False)
                        mm = pe.matmul(ps_mx[k][0:BN, h * P:(h + 1) * P], sel[0:n, (j % HALF) * H + h, :],
                                       partsT[0:n, j // HALF, :], start=False, stop=True)
                    mm.then_inc(mx_made[k], 1)
                if last:
                    pe.wait_ge(mx_read[0], (t.top + 1) * HALF)
                    pe.wait_ge(mx_read[1], (t.top + 1) * HALF)
                    pe.matmul(ps_misc[0:1, 0:1], ones[:, 0:1], ones[:, 0:1], start=True, stop=True).then_inc(group_used[t.half], 1)

            def spread(t, H, made):
                pe.wait_ge(top_all, made)
                for j in range(TJ):
                    mm = pe.matmul(ps_misc[:, j * H:(j + 1) * H], ST[:, t.half, j, :], top[:, 0:H], start=True, stop=True)
                mm.then_inc(me_made, 1)

            for layer in range(LAYERS):
                H = HEADS[layer]
                linear(layer)
                if together:
                    for t in sorted_turns(pe, layer):
                        if H:
                            logit(t)
                            maxima(t, H, False)
                            spread(t, H, t.top + 1)
                        add_up(t, H)
                else:
                    with pe.Fori(0, NB) as b:
                        for sweep in range(2 if H else 1):
                            for t in any_turns(pe, layer, b, sweep):
                                if H:
                                    logit(t)
                                if H and sweep == 0:
                                    maxima(t, H, True)
                                else:
                                    if H:
                                        spread(t, H, (layer - 3) * NB * GG + (b + 1) * GG)
                                    add_up(t, H)
                if layer == 2:
                    for k in range(2):
                        pe.wait_ge(bn_asked, k + 1)
                        pe.matmul(ps_misc[0:BN, k * D:(k + 1) * D], ones[0:BN, 0:BN], bn_s[:, 0, :], start=True, stop=True).then_inc(bn_summed, 1)

        @block.tensor
        def _(pe):
            pe.wait_ge(consts_made, 1)
            pe.wait_ge(all_made, 1)
            pe.matmul(ps_acc[0:1, 0:NB + 3], ones[0:ER, 0:1], cnt[:], start=True, stop=True).then_inc(counted, 1)
            for k in range(3):
                pe.wait_ge(w_made, 1)
                to = (ps_st[0], ps_st[1], ps_qe[0])[k]
                for i in range(3):
                    mm = pe.transpose(to[:, i * D:(i + 1) * D], w_r[:, 3 * k + i, :], ident[:])
                mm.then_inc(w_turned, 1)
            pe.wait_ge(w_copied, 3)
            pe.wait_ge(in_a, 16 * 16)
            pe.wait_ge(planned, 1)
            together = pe.value_load(plan[0:1, NB:NB + 1], min_val=0, max_val=1)
            with pe.If(together > 0):
                layers_pe(pe, True)
            with pe.Else():
                layers_pe(pe, False)
            pe.nop()

        def layers_dve(dve, together, done):
            v = nc.vector
            seen = [done]

            def link(ins):
                seen[0] += 1
                ins.then_inc(dve_step, 1)
                dve.wait_ge(dve_step, seen[0])

            x3, xc3, root3 = (t[:].rearrange("p (b d) -> p b d", d=D) for t in (xs, xc, root))

            def wide(col):
                return stat[:, col * NB:(col + 1) * NB].rearrange("p (b o) -> p b o", o=1).to_broadcast([BN, NB, D])

            def normalise(n):
                link(v.tensor_reduce(stat[:, 0:NB], x3, AX.X, ALU.add))
                link(v.tensor_scalar(stat[:, 0:NB], stat[:, 0:NB], 1.0 / D, None, ALU.mult))
                link(v.tensor_tensor(xc3, x3, wide(0), ALU.subtract))
                link(v.tensor_tensor(root[:], xc[:], xc[:], ALU.mult))
                link(v.tensor_reduce(stat[:, NB:2 * NB], root3, AX.X, ALU.add))
                v.tensor_scalar(stat[:, 2 * NB:3 * NB], stat[:, NB:2 * NB], 1.0 / D, EPS, ALU.mult, ALU.add).then_inc(var_made, 1)
                dve.wait_ge(std_made, n)
                link(v.reciprocal(stat[:, NB:2 * NB], stat[:, 3 * NB:4 * NB]))

            def linear(layer):
                def rows_of(half, use, b):
                    dve.wait_ge(h_turned[half], use)
                    if layer < 4:
                        r = stat[:, bass.ds(b + NB, 1)] if not isinstance(b, int) else stat[:, NB + b:NB + b + 1]
                        ins = v.tensor_scalar(hcur[:, half, :], cols(xc, b), r, 0.0, ALU.mult, ALU.max)
                        if layer == 2:
                            ins.then_inc(relu_made[half], 1)
                            dve.wait_ge(relu_made[half], use - (NB + 1 - half) // 2 * layer + 1)
                            ins = v.scalar_tensor_tensor(out=hcur[:, half, :], in0=hcur[:, half, :], scalar=0.2,
                                                         in1=hcur[:, half, :], op0=ALU.mult, op1=ALU.max)
                    else:
                        ins = v.tensor_scalar(hcur[:, half, :], cols(root, b), 0.0, None, ALU.max)
                    ins.then_inc(h_made[half], 1)
                    dve.wait_ge(rows_out[half], 16 * use)
                    dve.wait_ge(lin_made[half], use + 1)
                    q, m = ps_qe[half], ps_mx[half]
                    if layer == 0:
                        v.tensor_copy(rows[:, half, 0:512], q[0:BN, 0:512])
                        v.tensor_copy(rows[:, half, 512:640], m[0:BN, 0:128])
                        v.tensor_copy(cols(root, b), m[0:BN, 128:256]).then_inc(lin_read[half], 1)
                    elif layer == 1:
                        v.tensor_copy(rows[:, half, 0:D], q[0:BN, 0:D])
                        v.tensor_tensor(cols(root, b), q[0:BN, D:2 * D], bias1[:], ALU.add).then_inc(lin_read[half], 1)
                    elif layer == 2:
                        v.tensor_copy(cols(root, b), bias2[:])
                        v.tensor_copy(rows[:, half, 0:D], q[0:BN, 0:D]).then_inc(lin_read[half], 1)
                    else:
                        bias = (bias3, bias4)[layer - 3]
                        v.tensor_tensor(rows[:, half, 0:2 * D], q[0:BN, 0:2 * D], bias[:, 0:2 * D], ALU.add)
                        v.tensor_tensor(cols(qs, b), q[0:BN, 2 * D:3 * D], bias[:, 2 * D:3 * D], ALU.add)
                        v.tensor_tensor(cols(root, b), q[0:BN, 3 * D:4 * D], bias[:, 3 * D:4 * D], ALU.add).then_inc(lin_read[half], 1)

                for half, use, b in halves(dve, layer):
                    rows_of(half, use, b)

            def select(t):
                bc = t.col
                own = dst_f[:, bass.ds(bc * TJ, TJ)] if not isinstance(bc, int) else dst_f[:, bc * TJ:(bc + 1) * TJ]
                at = base_n[:, bass.ds(t.block, 1)] if not isinstance(t.block, int) else base_n[:, t.block:t.block + 1]
                dve.wait_ge(group_used[t.half], t.use)
                v.tensor_scalar(dloc[:, t.half, :], own, at, None, ALU.subtract).then_inc(dloc_made[t.half], 1)
                dve.wait_ge(dloc_made[t.half], t.use + 1)
                for c in range(NC):
                    v.tensor_tensor(S[:, t.half, c * CH:(c + 1) * CH, :],
                                    iota_n[:].rearrange("p (a n) -> p a n", a=1).to_broadcast([P, CH, BN]),
                                    dloc[:, t.half, c * CH:(c + 1) * CH].rearrange("p (a n) -> p a n", n=1).to_broadcast([P, CH, BN]),
                                    ALU.is_equal).then_inc(s_made[t.half], 1)

            def add_sums(t):
                dve.wait_ge(group_used[t.half], t.use + 1)
                dve.wait_ge(acc_read, t.acc)
                v.tensor_tensor(cols(root, t.block), ps_acc[0:BN, 0:D], cols(root, t.block), ALU.add).then_inc(acc_read, 1)

            def logit(t, H):
                def product(c):
                    k = c % 2
                    dve.wait_ge(gathered[t.half][c], 16 * CH * (t.use + 1))
                    dve.wait_ge(qe_made[k], t.logit * (NC // 2) + c // 2 + 1)
                    dve.wait_ge(logits_made[k], t.logit * (NC // 2) + c // 2)
                    v.tensor_tensor(prod[:, k, :].rearrange("p (j d) -> p j d", d=D),
                                    ps_qe[k][:, 0:CH * D].rearrange("p (j d) -> p j d", d=D),
                                    kv[:, t.half, c * CH:(c + 1) * CH, 0:D], ALU.mult).then_inc(qe_read[k], 1)

                def head_sums(c):
                    k = c % 2
                    dve.wait_ge(qe_read[k], t.logit * (NC // 2) + c // 2 + 1)
                    v.tensor_reduce(alpha[:, t.half, c * CH * H:(c + 1) * CH * H],
                                    prod[:, k, :].rearrange("p (i d) -> p i d", d=D // H), AX.X, ALU.add).then_inc(logits_made[k], 1)

                product(0)
                for c in range(NC):
                    if c + 1 < NC:
                        product(c + 1)
                    head_sums(c)

            def maxima(t, H):
                n = TJ * H
                a, r = alpha[:, t.half, 0:n], rest[:, t.half, 0:n]

                def own(k):
                    return split, 5 * t.top + k

                for k in range(2):
                    dve.wait_ge(logits_made[k], (t.logit + 1) * (NC // 2))
                v.tensor_copy(parts[:, 0:n, 0], a).then_inc(split, 1)
                dve.wait_ge(*own(1))
                v.tensor_tensor(r, a, parts[:, 0:n, 0], ALU.subtract).then_inc(split, 1)
                dve.wait_ge(*own(2))
                v.tensor_copy(parts[:, 0:n, 1], r).then_inc(split, 1)
                dve.wait_ge(*own(3))
                v.tensor_tensor(r, r, parts[:, 0:n, 1], ALU.subtract).then_inc(split, 1)
                dve.wait_ge(*own(4))
                v.tensor_copy(parts[:, 0:n, 2], r).then_inc(split, 1)
                for j in range(TJ):
                    k = j % 2
                    dve.wait_ge(mx_made[k], t.top * HALF + j // 2 + 1)
                    v.tensor_reduce(tops[:, 0:H, j], ps_mx[k][0:BN, 0:H * P].rearrange("p (h e) -> p h e", e=P), AX.X, ALU.max
                                    ).then_inc(mx_read[k], 1)
                dve.wait_ge(mx_read[0], (t.top + 1) * HALF)
                dve.wait_ge(mx_read[1], (t.top + 1) * HALF)

            def messages(t, H):
                n = TJ * H
                dve.wait_ge(me_made, t.msg + 1)
                v.tensor_tensor(rest[:, t.half, 0:n], alpha[:, t.half, 0:n], ps_misc[:, 0:n], ALU.subtract).then_inc(shifted, 1)
                dve.wait_ge(exp_made, t.msg + 1)
                for c in range(NC):
                    tiles = kv[:, t.half, c * CH:(c + 1) * CH, :]
                    val = tiles[:, :, D:2 * D].rearrange("p j (h d) -> p j h d", h=H)
                    w = tiles[:, :, 2 * D:2 * D + H].rearrange("p j (h o) -> p j h o", o=1).to_broadcast([P, CH, H, D // H])
                    v.tensor_tensor(val, val, w, ALU.mult).then_inc(v_scaled, 1)

            def finish(sums, H, b, n, free):
                v.tensor_scalar(den[:, 0:H], sums[:, D:D + H], 1e-16, None, ALU.add).then_inc(normed, 1)
                dve.wait_ge(normed, 3 * n + 1)
                v.reciprocal(rden[:, 0:H], den[:, 0:H]).then_inc(normed, 1)
                dve.wait_ge(normed, 3 * n + 2)
                ins = v.tensor_tensor(onorm[:].rearrange("p (h d) -> p h d", h=H), sums[:, 0:D].rearrange("p (h d) -> p h d", h=H),
                                      rden[:, 0:H].rearrange("p (h o) -> p h o", o=1).to_broadcast([BN, H, D // H]), ALU.mult)
                ins.then_inc(normed, 1)
                dve.wait_ge(normed, 3 * n + 3)
                ins = v.tensor_tensor(cols(root, b), cols(root, b), onorm[:], ALU.add)
                if free:
                    ins.then_inc(acc_read, 1)
                else:
                    ins.then_inc(out_added, 1)

            var_n = 0
            for layer in range(LAYERS):
                H = HEADS[layer]
                if layer < 4:
                    var_n += 1
                    normalise(var_n)
                linear(layer)
                if together:
                    for t in sorted_turns(dve, layer):
                        select(t)
                        if not H:
                            add_sums(t)
                            continue
                        logit(t, H)
                        maxima(t, H)
                        v.tensor_reduce(top[:, 0:H], tops[:, 0:H, :], AX.X, ALU.max).then_inc(top_all, 1)
                        messages(t, H)
                        dve.wait_ge(group_used[t.half], t.use + 1)
                        finish(ps_acc[0:BN, :], H, t.block, t.acc - 3 * NB, True)
                else:
                    with dve.Fori(0, NB) as b:
                        if not H:
                            for t in any_turns(dve, layer, b, 0):
                                select(t)
                                add_sums(t)
                        else:
                            before = (layer - 3) * NB + b
                            v.memset(msum[:], 0.0).then_inc(out_added, 1)
                            v.memset(topn[:], -BIG).then_inc(out_added, 1)
                            dve.wait_ge(out_added, 3 * before + 2)
                            dve.sem_inc(sums_cleared, 1)
                            for t in any_turns(dve, layer, b, 0):
                                select(t)
                                logit(t, H)
                                maxima(t, H)
                                v.tensor_reduce(top[:, 0:H], tops[:, 0:H, :], AX.X, ALU.max).then_inc(top_made, 1)
                                dve.wait_ge(top_made, 2 * t.top + 1)
                                v.tensor_tensor(topn[:, 0:H], topn[:, 0:H], top[:, 0:H], ALU.max).then_inc(top_made, 1)
                                dve.wait_ge(top_made, 2 * t.top + 2)
                                v.tensor_copy(top[:, 0:H], topn[:, 0:H]).then_inc(top_all, 1)
                            for t in any_turns(dve, layer, b, 1):
                                select(t)
                                logit(t, H)
                                messages(t, H)
                                dve.wait_ge(group_used[t.half], t.use + 1)
                                dve.wait_ge(acc_read, t.acc)
                                v.tensor_tensor(msum[:, 0:D + H], msum[:, 0:D + H], ps_acc[0:BN, 0:D + H], ALU.add).then_inc(acc_read, 1)
                            dve.wait_ge(acc_read, (layer * NB + b + 1) * GG)
                            finish(msum, H, b, before, False)
                groups = (NB if together else NB * GG) * (layer + 1)
                dve.wait_ge(acc_read, groups)
                if H and not together:
                    dve.wait_ge(out_added, 3 * NB * (layer - 2))
                if layer == 0:
                    link(v.tensor_tensor(xs[:], xs[:], root[:], ALU.add))
                elif layer == 1:
                    link(v.scalar_tensor_tensor(out=xs[:], in0=root[:], scalar=0.0, in1=xs[:], op0=ALU.max, op1=ALU.add))
                elif layer == 2:
                    by_col = root[:].rearrange("p (b d) -> p d b", d=D)
                    v.tensor_reduce(bn_s[:, 0, :], by_col, AX.X, ALU.add).then_inc(bn_asked, 1)
                    dve.wait_ge(bn_summed, 1)
                    link(v.tensor_scalar(bn_s[:, 1, :], ps_misc[0:BN, 0:D], 1.0 / N, None, ALU.mult))

                    def rep(k):
                        return bn_s[:, k:k + 1, :].to_broadcast([BN, NB, D])

                    link(v.tensor_tensor(root3, root3, rep(1), ALU.subtract))
                    link(v.tensor_tensor(xc[:], root[:], root[:], ALU.mult))
                    v.tensor_reduce(bn_s[:, 0, :], xc[:].rearrange("p (b d) -> p d b", d=D), AX.X, ALU.add).then_inc(bn_asked, 1)
                    dve.wait_ge(bn_summed, 2)
                    var_n += 1
                    v.tensor_scalar(bn_s[:, 2, :], ps_misc[0:BN, D:2 * D], 1.0 / N, EPS, ALU.mult, ALU.add).then_inc(var_made, 1)
                    dve.wait_ge(std_made, var_n)
                    link(v.reciprocal(bn_s[:, 1, :], bn_s[:, 3, :]))
                    link(v.tensor_tensor(bn_s[:, 0, :], bn_s[:, 1, :], gam[:], ALU.mult))
                    link(v.tensor_tensor(root3, root3, rep(0), ALU.mult))
                    link(v.tensor_tensor(root3, root3, bet[:].rearrange("p (a d) -> p a d", a=1).to_broadcast([BN, NB, D]), ALU.add))
                    link(v.tensor_tensor(xs[:], xs[:], root[:], ALU.add))
                elif layer == 4:
                    v.tensor_tensor(xs[:], xs[:], root[:], ALU.add).then_inc(x_done, 1)

        @block.vector
        def _(dve):
            v = nc.vector
            seen = [0]

            def link(ins):
                seen[0] += 1
                ins.then_inc(dve_step, 1)
                dve.wait_ge(dve_step, seen[0])

            dve.wait_ge(in_all, 32)
            dve.wait_ge(consts_made, 1)
            v.tensor_copy(nxt_f[0:ER - 1, :], nxt_i[0:ER - 1, :])
            link(v.tensor_copy(all_f, all_i))
            for b in range(NB):
                link(v.tensor_scalar(hits, all_f, float(BN * b), 0.0, ALU.is_lt, ALU.add, accum_out=cnt[:, b:b + 1]))
            v.tensor_tensor(cnt[:, NB + 1:NB + 2], all_f[:, EW - 1:EW], nxt_f[:], ALU.is_gt)
            v.memset(cnt[:, NB + 2:NB + 3], 0.0)
            link(v.tensor_tensor(hits[:, 0:EW - 1], all_f[:, 0:EW - 1], all_f[:, 1:EW], ALU.is_gt))
            v.tensor_reduce(cnt[:, NB:NB + 1], hits[:, 0:EW - 1], AX.X, ALU.add).then_inc(all_made, 1)
            dve.wait_ge(in_w, 16 * 5)
            for k in range(BASES):
                for r in range(TYPES):
                    wk = w_in[:, k * D:(k + 1) * D]
                    a = a_bc[:, r * BASES + k:r * BASES + k + 1]
                    if k == 0:
                        ins = v.tensor_scalar(w_r[:, r, :], wk, a, None, ALU.mult)
                    else:
                        ins = v.scalar_tensor_tensor(out=w_r[:, r, :], in0=wk, scalar=a, in1=w_r[:, r, :],
                                                     op0=ALU.mult, op1=ALU.add)
                if k < BASES - 1:
                    link(ins)
            ins.then_inc(w_made, 1)
            dve.wait_ge(counted, 1)
            link(v.tensor_copy(total[:], ps_acc[0:1, 0:NB + 3]))
            v.tensor_scalar(plan_f[:], total[:], float(E - GE), None, ALU.min)
            v.tensor_tensor(steps[:, 0:NB - 1], total[:, 1:NB], total[:, 0:NB - 1], ALU.subtract)
            link(v.tensor_scalar(steps[:, NB - 1:NB], total[:, NB - 1:NB], -1.0, float(E), ALU.mult, ALU.add))
            link(v.tensor_reduce(steps[:, NB:NB + 1], steps[:, 0:NB], AX.X, ALU.max))
            link(v.tensor_scalar(steps[:, NB:NB + 1], steps[:, NB:NB + 1], float(GE), None, ALU.is_le))
            link(v.tensor_tensor(steps[:, NB + 1:NB + 2], total[:, NB:NB + 1], total[:, NB + 1:NB + 2], ALU.add))
            link(v.tensor_scalar(steps[:, NB + 1:NB + 2], steps[:, NB + 1:NB + 2], 0.0, None, ALU.is_equal))
            link(v.tensor_tensor(plan_f[:, NB:NB + 1], steps[:, NB:NB + 1], steps[:, NB + 1:NB + 2], ALU.mult))
            v.tensor_copy(plan[:], plan_f[:]).then_inc(planned, 1)
            dve.wait_ge(planned, 1)
            dve.wait_ge(in_x, 16)
            dve.wait_ge(in_b, 64)
            dve.wait_ge(in_a, 256)
            together = dve.value_load(plan[0:1, NB:NB + 1], min_val=0, max_val=1)
            with dve.If(together > 0):
                dve.wait_ge(edges_in, 16 * 3 * NB)
                v.tensor_copy(dst_f[:], dst_i[:]).then_inc(edges_made, 1)
                v.scalar_tensor_tensor(out=typ_i[:], in0=src_i[:], scalar=float(TYPES), in1=typ_i[:],
                                       op0=ALU.mult, op1=ALU.add).then_inc(edges_made, 2)
                layers_dve(dve, True, seen[0])
            with dve.Else():
                dve.wait_ge(edges_in, 16 * 3 * GG)
                n = GG * TJ
                v.tensor_scalar(rest[:, 0, 0:TJ], iota_e[:], float((GG - 1) * GE - (E - GE)), FAR, ALU.is_lt, ALU.mult)
                v.tensor_copy(dst_f[:, 0:n], dst_i[:, 0:n]).then_inc(edges_made, 1)
                dve.wait_ge(edges_made, 1)
                v.tensor_tensor(dst_f[:, n - TJ:n], dst_f[:, n - TJ:n], rest[:, 0, 0:TJ], ALU.add).then_inc(edges_made, 1)
                v.scalar_tensor_tensor(out=typ_i[:, 0:n], in0=src_i[:, 0:n], scalar=float(TYPES), in1=typ_i[:, 0:n],
                                       op0=ALU.mult, op1=ALU.add).then_inc(edges_made, 1)
                layers_dve(dve, False, seen[0])
            dve.nop()


_INS = ['x', 'src', 'dst', 'edge_type_5', 'L0_gnn_B', 'L0_gnn_A', 'L0_gnn_W0', 'L1_gnn_W', 'L1_gnn_b',
        'L2_gnn_W', 'L2_gnn_b', 'L2_gnn_gamma', 'L2_gnn_beta']
_ATT = [f"L3_gnn_{kind}{n}" for n in (1, 2) for kind in ("Wk", "Wv", "Wq", "Ws", "bk", "bv", "bq", "bs")]


def kernel(**inputs):
    import numpy as _np
    import concourse.bacc as _bacc
    from concourse import mybir as _mybir
    from concourse.bass_utils import run_bass_kernel_spmd as _run

    nc = _bacc.Bacc("TRN2", target_bir_lowering=False, num_devices=1)
    arrays, aps = {}, {}
    for name in _INS + _ATT:
        a = _np.ascontiguousarray(inputs[name])
        arrays[f"in_{name}"] = a
        aps[name] = nc.dram_tensor(f"in_{name}", a.shape, _mybir.dt.from_np(a.dtype), kind="ExternalInput").ap()
    out = nc.dram_tensor("out", (N, D), _mybir.dt.float32, kind="ExternalOutput").ap()
    att = [([aps[n] for n in _ATT[8 * k:8 * k + 4]], [aps[n] for n in _ATT[8 * k + 4:8 * k + 8]]) for k in range(2)]
    build(nc, *[aps[n] for n in _INS], *att, out)
    r = _run(nc, [arrays], core_ids=[0])
    return r.results[0]["out"]
```

```python
from collections import namedtuple
from contextlib import ExitStack

import concourse.bass as bass
from concourse import mybir

ALU = mybir.AluOpType
ACT = mybir.ActivationFunctionType
AX = mybir.AxisListType
BF16 = mybir.dt.bfloat16
F32 = mybir.dt.float32
I32 = mybir.dt.int32

P = 128
N, D, E = 3125, 128, 53125
NB = 25
BN = N // NB
TJ = 18
GE = TJ * P
CH = 3
NC = TJ // CH
GG = -(-E // GE)
TYPES, BASES = 5, 4
HALF = TJ // 2
EW = 425
ER = E // EW
FAR = 1.0e6
BIG = float(2 ** 100)
EPS = 1e-5
LAYERS = 5
HEADS = (0, 0, 0, 4, 1)
TABLE = (TYPES * D, D, D, 2 * D, 2 * D)
KV = 2 * D + 4
UNLIKE = -BIG
assert NB * BN == N and ER * EW == E and NB % 2 == 1 and GG % 2 == 0 and TJ * NB >= TJ * GG

Turn = namedtuple("Turn", "half use logit top msg acc block col")
Rows = namedtuple("Rows", "half use block")
EVEN, ODD = (NB + 1) // 2, NB // 2


def sorted_turns(eng, layer):
    att = max(layer - 3, 0) * NB

    def turn(half, i, b):
        return Turn(half, (EVEN, ODD)[half] * layer + i, att + b, att + b, att + b, NB * layer + b, b, b)

    with eng.Fori(0, ODD) as i:
        yield turn(0, i, 2 * i), turn(1, i, 2 * i + 1)
        yield turn(1, i, 2 * i + 1), turn(0, i + 1, 2 * i + 2)
    yield turn(0, ODD, NB - 1), None


def first_turn(layer):
    att = max(layer - 3, 0) * NB
    return Turn(0, EVEN * layer, att, att, att, NB * layer, 0, 0)


def any_turns(eng, layer, block, sweep):
    h = GG // 2
    att = layer - 3
    use0 = NB * h * layer if layer < 3 else NB * h * 3 + 2 * NB * h * att
    with eng.Fori(0, h) as k:
        for half in range(2):
            g = 2 * k + half
            n = block * GG + g
            if layer < 3:
                yield Turn(half, use0 + block * h + k, 0, 0, 0, NB * GG * layer + n, block, g)
            else:
                yield Turn(half, use0 + block * GG + sweep * h + k,
                           2 * NB * GG * att + block * (2 * GG) + sweep * GG + g,
                           NB * GG * att + n, NB * GG * att + n, NB * GG * layer + n, block, g)


def rows_before(together, layer):
    inside = (EVEN, ODD) if together else (NB, 0)
    per = [(EVEN, ODD), inside, inside, (EVEN, ODD), inside]
    return sum(p[0] for p in per[:layer]), sum(p[1] for p in per[:layer])


def rows_in_order(eng, together, layer):
    n0, n1 = rows_before(together, layer)
    if together or layer in (0, 3):
        with eng.Fori(0, ODD) as i:
            yield Rows(0, n0 + i, 2 * i)
            yield Rows(1, n1 + i, 2 * i + 1)
        yield Rows(0, n0 + ODD, NB - 1)
    else:
        with eng.Fori(0, NB) as b:
            yield Rows(0, n0 + b, b)


def rows_of(t, together, layer):
    n0, n1 = rows_before(together, layer)
    if not together:
        return Rows(0, n0 + t, t)
    return Rows(t.half, (n0, n1)[t.half] + t.use - (EVEN, ODD)[t.half] * (layer - 1), t.block)


def skewed(eng, together, layer):
    base = rows_before(together, layer)

    def rows(j, i=0):
        if not isinstance(i, int):
            return Rows(j % 2, base[j % 2] + i // 2 + j // 2, i + j)
        return Rows((i + j) % 2, base[(i + j) % 2] + (i + j) // 2, i + j)

    def at(k, j):
        return Rows(j % 2, k + (base[j % 2] + j // 2), 2 * k + j)

    yield rows(0), None, None
    yield rows(1), rows(0), None
    with eng.Fori(0, (NB - 3) // 2) as k:
        yield at(k, 2), at(k, 1), at(k, 0)
        yield at(k, 3), at(k, 2), at(k, 1)
    yield rows(NB - 1), rows(NB - 2), rows(NB - 3)
    yield None, rows(NB - 1), rows(NB - 2)
    yield None, None, rows(NB - 1)


def build(nc, x, src, dst, etype, B, A, W0, W1, b1, W2, b2, gamma, beta, att1, att2, out):
    with ExitStack() as ctx:
        def sb(name, shape, dt=F32):
            return ctx.enter_context(nc.sbuf_tensor(name, shape, dt))

        def sem(name):
            return ctx.enter_context(nc.semaphore(name))

        def pair(name):
            return [sem(f"{name}{i}") for i in range(2)]

        bank = [ctx.enter_context(nc.psum_tensor(f"bank{i}", [P, 512], F32)) for i in range(8)]
        ps_qe, ps_st, ps_mx, ps_misc, ps_acc = bank[0:2], bank[2:4], bank[4:6], bank[6], bank[7]

        xs = sb("xs", [BN, NB * D])
        root = sb("root", [BN, NB * D])
        qs = sb("qs", [BN, NB * D])
        xcur = sb("xcur", [BN, 2, D])
        hcur = sb("hcur", [BN, 2, D])
        hT = sb("hT", [P, 2, BN])
        halfstat = sb("halfstat", [BN, 2, 6])
        meanvar = sb("meanvar", [BN, 2, 2])
        sdev = sb("sdev", [BN, 2])
        rsdev = sb("rsdev", [BN, 2])
        eps = sb("eps", [BN, 1])
        rows = sb("rows", [BN, 2, TYPES * D])
        zsum = sb("zsum", [BN, D])
        bn_s = sb("bn_s", [BN, 4, D])
        src_i = sb("src_i", [P, NB * TJ], I32)
        dst_i = sb("dst_i", [P, NB * TJ], I32)
        typ_i = sb("typ_i", [P, NB * TJ], I32)
        dst_f = sb("dst_f", [P, NB * TJ])
        idx = sb("idx", [P, 2, TJ], I32)
        dloc = sb("dloc", [P, 2, TJ])
        kv = sb("kv", [P, 2, TJ, KV])
        S = sb("S", [P, 2, TJ, BN])
        ST = sb("ST", [BN, 2, TJ, P])
        prod = sb("prod", [P, 2, CH * D])
        alpha = sb("alpha", [P, 2, 4 * TJ])
        rest = sb("rest", [P, 2, 4 * TJ])
        fore = sb("fore", [P, 2, 4 * TJ])
        back = sb("back", [P, 2, 4 * TJ])
        parts = sb("parts", [P, TJ * 4, 3], BF16)
        partsT = sb("partsT", [HALF * 12, 2, P], BF16)
        tops = sb("tops", [BN, 4, TJ])
        top = sb("top", [BN, 4])
        topn = sb("topn", [BN, 4])
        den = sb("den", [BN, 4])
        rden = sb("rden", [BN, 4])
        onorm = sb("onorm", [BN, D])
        msum = sb("msum", [BN, D + 4])
        FL = NB * 4 * TJ
        either = sb("either", [P, 2 * FL + 2 * NB * TJ + 2 * NB * P], BF16)
        like_prev = either[:, 0:FL].rearrange("p (b h j) -> p b h j", b=NB, h=4)
        like_next = either[:, FL:2 * FL].rearrange("p (b h j) -> p b h j", b=NB, h=4)
        like_above = either[:, 2 * FL:2 * FL + NB * TJ]
        like_below = either[:, 2 * FL + NB * TJ:2 * FL + 2 * NB * TJ]
        run_down = either[0:4, 2 * FL + 2 * NB * TJ:2 * FL + 2 * NB * TJ + NB * P]
        run_up = either[0:4, 2 * FL + 2 * NB * TJ + NB * P:]
        mask = either[0:BN, 0:2 * TJ * P].rearrange("p (a j e) -> p a j e", a=2, j=TJ)
        ends = sb("ends", [P, 2, NB])
        beyond = sb("beyond", [P, 2, NB])
        runs = sb("runs", [P, 2, NB], BF16)
        down = sb("down", [4, P + 1])
        up = sb("up", [4, P + 1])
        iota_n = sb("iota_n", [P, BN])
        iota_e = sb("iota_e", [P, TJ])
        base_n = sb("base_n", [P, NB])
        ident = sb("ident", [P, P])
        ident_b = sb("ident_b", [P, P], BF16)
        turned_b = sb("turned_b", [P, P], BF16)
        sel = sb("sel", [HALF * 12, HALF * 4, BN], BF16)
        ones = sb("ones", [P, P])
        w_in = sb("w_in", [P, 4 * D])
        w_r = sb("w_r", [P, 9, D])
        a_bc = sb("a_bc", [P, TYPES * BASES])
        w0 = sb("w0", [P, (TYPES + 1) * D])
        w1 = sb("w1", [P, 2 * D])
        w2 = sb("w2", [P, D])
        w3 = sb("w3", [P, 4 * D])
        w4 = sb("w4", [P, 4 * D])
        bias2, gam, bet = (sb(n, [BN, D]) for n in ("bias2", "gam", "bet"))
        bias_rows = sb("bias_rows", [1, 3, 4 * D])
        all_i = S[0:ER, 0, 0:4, :].rearrange("p a b -> p (a b)").bitcast(I32)[:, 0:EW]
        all_f = S[0:ER, 0, 4:8, :].rearrange("p a b -> p (a b)")[:, 0:EW]
        hits = S[0:ER, 0, 8:12, :].rearrange("p a b -> p (a b)")[:, 0:EW]
        squares = kv[0:BN, 0, :, :].rearrange("p a b -> p (a b)")[:, 0:NB * D]
        nxt_i = sb("nxt_i", [ER, 1], I32)
        nxt_f = sb("nxt_f", [ER, 1])
        cnt = sb("cnt", [ER, NB + 3])
        total = sb("total", [1, NB + 3])
        steps = sb("steps", [1, NB + 3])
        plan_f = sb("plan_f", [1, NB + 3])
        plan = sb("plan", [1, NB + 3], I32)

        tables = [nc.dram_tensor(f"table{i}", (N, TABLE[i]), F32, kind="Internal").ap() for i in range(LAYERS)]

        in_x, in_w, in_b, in_all, in_a = sem("in_x"), sem("in_w"), sem("in_b"), sem("in_all"), sem("in_a")
        pool_step, dve_step = sem("pool_step"), sem("dve_step")
        consts_made, w_made, w_turned, sel_made = sem("consts_made"), sem("w_made"), sem("w_turned"), sem("sel_made")
        w_copied, all_made, counted, planned = sem("w_copied"), sem("all_made"), sem("counted"), sem("planned")
        edges_in, edges_made = sem("edges_in"), sem("edges_made")
        ends_made, beyond_in, runs_made, runs_turned, runs_copied = (
            sem("ends_made"), sem("beyond_in"), sem("runs_made"), sem("runs_turned"), sem("runs_copied"))
        x_here, halves_made, var_made, sdev_made, rsdev_made = (
            pair("x_here"), pair("halves_made"), pair("var_made"), pair("sdev_made"), pair("rsdev_made"))
        h_made, h_turned, ht_copied, leaky_made = pair("h_made"), pair("h_turned"), pair("ht_copied"), pair("leaky_made")
        lin_made, rows_made, kept, rows_out = pair("lin_made"), pair("rows_made"), pair("kept"), pair("rows_out")
        bn_asked, bn_summed, bn_var, bn_dev, scaled = (
            sem("bn_asked"), sem("bn_summed"), sem("bn_var"), sem("bn_dev"), sem("scaled"))
        idx_made, dloc_made, s_made, group_used = pair("idx_made"), pair("dloc_made"), pair("s_made"), pair("group_used")
        gathered = [[sem(f"gathered{h}_{c}") for c in range(NC)] for h in range(2)]
        acc_read, block_begun, z_added = sem("acc_read"), sem("block_begun"), sem("z_added")
        waits_passed = sem("waits_passed")
        st_made, st_copied, qe_made, qe_read = pair("st_made"), pair("st_copied"), pair("qe_made"), pair("qe_read")
        logits_made = pair("logits_made")
        scanned, ends_turned, carried, carry_turned, topped = (
            sem("scanned"), sem("ends_turned"), sem("carried"), sem("carry_turned"), sem("topped"))
        split, parts_turned, parts_copied = sem("split"), sem("parts_turned"), sem("parts_copied")
        mx_made, mx_read = pair("mx_made"), pair("mx_read")
        top_made, top_all, me_made, shifted, exp_made, v_scaled, normed = (
            sem("top_made"), sem("top_all"), sem("me_made"), sem("shifted"), sem("exp_made"), sem("v_scaled"),
            sem("normed"))
        x_done, stored = sem("x_done"), sem("stored")

        block = ctx.enter_context(nc.Block())

        def at(t, b, w=D):
            return t[:, b * w:(b + 1) * w] if isinstance(b, int) else t[:, bass.ds(b * w, w)]

        WALL = [w0, w1, w2, w3, w4]
        BIAS = {1: 0, 3: 1, 4: 2}

        def layers_sp(sp, together):
            for layer in range(LAYERS):
                for r in rows_in_order(sp, together, layer):
                    to = tables[layer][bass.ds(r.block * BN, BN), :] if not isinstance(r.block, int) \
                        else tables[layer][r.block * BN:(r.block + 1) * BN, :]
                    sp.wait_ge(rows_made[r.half], r.use + 1)
                    sp.dma_start(to, rows[:, r.half, 0:TABLE[layer]]).then_inc(rows_out[r.half], 16)
            with sp.Fori(0, NB) as b:
                sp.wait_ge(x_done, b + 1)
                sp.dma_start(out[bass.ds(b * BN, BN), :], at(xs, b)).then_inc(stored, 16)
            sp.wait_ge(stored, 16 * NB)
            n0, n1 = rows_before(together, LAYERS)
            sp.wait_ge(rows_out[0], 16 * n0)
            sp.wait_ge(rows_out[1], 16 * n1)

        @block.sync
        def _(sp):
            sp.dma_start(all_i, dst.rearrange("(p w) -> p w", w=EW)).then_inc(in_all, 16)
            sp.dma_start(nxt_i[0:ER - 1, :], dst[EW:E].rearrange("(p w) -> p w", w=EW)[:, 0:1],
                         allow_slow_non_contiguous=True).then_inc(in_all, 16)
            sp.dma_start(xs[:].rearrange("p (b d) -> p b d", d=D), x.rearrange("(b p) d -> p b d", p=BN)).then_inc(in_x, 16)
            sp.wait_ge(planned, 1)
            together = sp.value_load(plan[0:1, NB:NB + 1], min_val=0, max_val=1)
            with sp.If(together > 0):
                with sp.Fori(0, NB) as b:
                    base = sp.value_load(plan[0:1, bass.ds(b, 1)], min_val=0, max_val=E - GE)
                    for arr, own in ((dst, dst_i), (src, src_i), (etype, typ_i)):
                        sp.dma_start(own[:, bass.ds(b * TJ, TJ)],
                                     arr[bass.ds(base, GE)].rearrange("(p j) -> p j", j=TJ)).then_inc(edges_in, 16)
                sp.wait_ge(ends_made, 2)
                sp.dma_start(beyond[1:P, 0, :], ends[0:P - 1, 1, :]).then_inc(beyond_in, 16)
                sp.dma_start(beyond[0:P - 1, 1, :], ends[1:P, 0, :]).then_inc(beyond_in, 16)
                layers_sp(sp, True)
            with sp.Else():
                with sp.Fori(0, GG - 1) as g:
                    for arr, own in ((dst, dst_i), (src, src_i), (etype, typ_i)):
                        sp.dma_start(own[:, bass.ds(g * TJ, TJ)],
                                     arr[bass.ds(g * GE, GE)].rearrange("(p j) -> p j", j=TJ)).then_inc(edges_in, 16)
                for arr, own in ((dst, dst_i), (src, src_i), (etype, typ_i)):
                    sp.dma_start(own[:, (GG - 1) * TJ:GG * TJ],
                                 arr[E - GE:E].rearrange("(p j) -> p j", j=TJ)).then_inc(edges_in, 16)
                layers_sp(sp, False)
            sp.nop()

        def layers_pool(pool, together):
            pool.wait_ge(edges_made, 3)

            def gather(t, layer):
                table = tables[layer] if layer else tables[0].rearrange("n (r d) -> (n r) d", d=D)
                w = table.shape[1]
                pool.wait_ge(group_used[t.half], t.use)
                pool.tensor_copy(idx[:, t.half, :], at(src_i if layer else typ_i, t.col, TJ)).then_inc(idx_made[t.half], 1)
                pool.wait_ge(idx_made[t.half], t.use + 1)
                pool.sem_inc(waits_passed, 1)
                for j in range(TJ):
                    pool.indirect_dma_start(kv[:, t.half, j, 0:w], None, table,
                                            bass.IndirectOffsetOnAxis(ap=idx[:, t.half, j:j + 1], axis=0)
                                            ).then_inc(gathered[t.half][j // CH], 16)

            for layer in range(LAYERS):
                n0, n1 = rows_before(together, layer + 1)
                pool.wait_ge(rows_out[0], 16 * n0)
                pool.wait_ge(rows_out[1], 16 * n1)
                if together:
                    for t, _ in sorted_turns(pool, layer):
                        gather(t, layer)
                else:
                    with pool.Fori(0, NB) as b:
                        for sweep in range(1 if layer < 3 else 2):
                            for t in any_turns(pool, layer, b, sweep):
                                gather(t, layer)

        @block.gpsimd
        def _(pool):
            pool.memset(ident[:], 0.0).then_inc(pool_step, 1)
            pool.wait_ge(pool_step, 1)
            pool.affine_select(out=ident[:], in_=ident[:], compare_op=ALU.not_equal, fill=1.0, base=0,
                               pattern=[[-1, P]], channel_multiplier=1).then_inc(pool_step, 1)
            pool.memset(turned_b[:], 0.0).then_inc(pool_step, 1)
            pool.wait_ge(pool_step, 3)
            pool.affine_select(out=turned_b[:], in_=turned_b[:], compare_op=ALU.not_equal, fill=1.0, base=1 - P,
                               pattern=[[1, P]], channel_multiplier=1).then_inc(pool_step, 1)
            pool.iota(iota_n[:], [[1, BN]], base=0, channel_multiplier=0, allow_small_or_imprecise_dtypes=True)
            pool.iota(iota_e[:], [[1, TJ]], base=0, channel_multiplier=TJ, allow_small_or_imprecise_dtypes=True)
            pool.iota(base_n[:], [[BN, NB]], base=0, channel_multiplier=0, allow_small_or_imprecise_dtypes=True)
            pool.memset(ones[:], 1.0)
            pool.memset(eps[:], EPS)
            pool.memset(zsum[:], 0.0)
            pool.memset(bias_rows[:, 0, 0:D], 0.0)
            pool.memset(beyond[:], -1.0)
            pool.memset(down[:], UNLIKE)
            pool.memset(up[:], UNLIKE)
            pool.memset(nxt_f[:], FAR)
            pool.wait_ge(pool_step, 4)
            pool.tensor_copy(ident_b[:], ident[:]).then_inc(consts_made, 1)
            pool.wait_ge(planned, 1)
            together = pool.value_load(plan[0:1, NB:NB + 1], min_val=0, max_val=1)
            with pool.If(together > 0):
                layers_pool(pool, True)
            with pool.Else():
                pool.memset(sel[:], 1.0).then_inc(pool_step, 1)
                pool.wait_ge(pool_step, 5)
                pool.affine_select(out=sel[:], in_=sel[:], compare_op=ALU.is_ge, fill=0.0, base=0,
                                   pattern=[[-3, HALF * 4], [0, BN]], channel_multiplier=1).then_inc(pool_step, 1)
                pool.wait_ge(pool_step, 6)
                pool.affine_select(out=sel[:], in_=sel[:], compare_op=ALU.is_ge, fill=0.0, base=2,
                                   pattern=[[3, HALF * 4], [0, BN]], channel_multiplier=-1).then_inc(sel_made, 1)
                layers_pool(pool, False)
            pool.nop()

        def layers_act(act, together):
            def deviation(r):
                act.wait_ge(var_made[r.half], r.use + 1)
                act.activation(sdev[:, r.half:r.half + 1], meanvar[:, r.half, 1:2], ACT.Sqrt, bias=eps[:]
                               ).then_inc(sdev_made[r.half], 1)

            def store_x(r):
                act.wait_ge(x_here[r.half], r.use + 1)
                act.copy(at(xs, r.block), xcur[:, r.half, :])

            def turned(r, layer, inside):
                where = ps_mx[0] if layer == 4 else ps_st[r.half]
                act.wait_ge(h_turned[r.half], r.use + 1)
                act.activation(hT[:, r.half, :], where[:, 0:BN], ACT.Relu).then_inc(ht_copied[r.half], 1)

            def put_rows(r, layer):
                q, m = (ps_mx[1], None) if layer == 4 else (ps_qe[r.half], ps_mx[r.half])
                act.wait_ge(lin_made[r.half], r.use + 1)
                act.wait_ge(rows_out[r.half], 16 * r.use)
                w = TABLE[layer]
                if layer == 0:
                    act.copy(rows[:, r.half, 512:w], m[0:BN, 0:w - 512])
                if layer >= 3:
                    act.copy(at(qs, r.block), q[0:BN, w:w + D])
                act.copy(rows[:, r.half, 0:min(w, 512)], q[0:BN, 0:min(w, 512)]).then_inc(rows_made[r.half], 1)

            def logit(t):
                for c in range(NC):
                    k = c % 2
                    if c == 0:
                        act.wait_ge(group_used[t.half], t.use)
                    act.wait_ge(st_made[k], t.logit * (NC // 2) + c // 2 + 1)
                    here = ps_st[k][0:BN, 0:CH * P].rearrange("p (j e) -> p j e", e=P)
                    if not together:
                        act.activation(mask[:, t.half, c * CH:(c + 1) * CH, :], here, ACT.Copy, bias=-BIG, scale=BIG)
                    act.copy(ST[:, t.half, c * CH:(c + 1) * CH, :], here).then_inc(st_copied[k], 1)

            def turn_parts(t, H):
                act.wait_ge(parts_turned, t.top + 1)
                act.copy(partsT[0:HALF * H * 3, :, :],
                         ps_misc[:].bitcast(BF16)[0:HALF * H * 3, 0:2 * P].rearrange("k (a e) -> k a e", e=P)
                         ).then_inc(parts_copied, 1)

            def exponent(t, H, scale):
                act.wait_ge(shifted, t.msg + 1)
                act.activation(kv[:, t.half, :, 2 * D:2 * D + H].rearrange("p j h -> p h j"),
                               rest[:, t.half, 0:TJ * H].rearrange("p (h j) -> p h j", h=H),
                               ACT.Exp, scale=scale).then_inc(exp_made, 1)

            for layer in range(LAYERS):
                H = HEADS[layer]
                scale = float(H / D) ** 0.5
                if layer in (0, 3):
                    for nxt, cur, prev in skewed(act, together, layer):
                        if nxt and layer == 0:
                            act.wait_ge(h_made[nxt.half], nxt.use)
                            act.copy(xcur[:, nxt.half, :], at(xs, nxt.block)).then_inc(x_here[nxt.half], 1)
                        if prev:
                            put_rows(prev, layer)
                        if nxt:
                            if layer:
                                store_x(nxt)
                            deviation(nxt)
                        if cur:
                            turned(cur, layer, False)
                if layer == 0 and together:
                    for k in range(0, 2 * NB, 4):
                        n = min(4, 2 * NB - k)
                        act.wait_ge(runs_turned, k // 4 + 1)
                        act.copy(either[0:4, 2 * FL + 2 * NB * TJ + k * P:2 * FL + 2 * NB * TJ + (k + n) * P],
                                 ps_st[(k // 4) % 2][0:4, 0:n * P]).then_inc(runs_copied, 1)

                def rows_inside(r):
                    if layer in (0, 1):
                        store_x(r)
                        deviation(r)
                    if layer in (0, 1, 3):
                        turned(r, layer + 1, True)
                        put_rows(r, layer + 1)

                if together:
                    for t, _ in sorted_turns(act, layer):
                        if H:
                            logit(t)
                            exponent(t, H, scale)
                        rows_inside(rows_of(t, True, layer + 1))
                else:
                    with act.Fori(0, NB) as b:
                        if H:
                            for t in any_turns(act, layer, b, 0):
                                logit(t)
                                turn_parts(t, H)
                            for t in any_turns(act, layer, b, 1):
                                logit(t)
                                exponent(t, H, scale)
                        rows_inside(rows_of(b, False, layer + 1))
                if layer == 2:
                    act.wait_ge(bn_asked, 2)
                    act.activation(squares, root[:], ACT.Square).then_inc(bn_var, 1)
                    act.wait_ge(bn_var, 2)
                    act.activation(bn_s[:, 3, :], bn_s[:, 2, :], ACT.Sqrt).then_inc(bn_dev, 1)

        @block.scalar
        def _(act):
            act.dma_start(w_in[:].rearrange("o (k d) -> o k d", d=D), B.rearrange("k o d -> o k d")).then_inc(in_w, 16)
            act.dma_start(a_bc[:], A.rearrange("r k -> (r k)").rearrange("(a n) -> a n", a=1).to_broadcast([P, TYPES * BASES])).then_inc(in_w, 16)
            act.dma_start(w_r[:, TYPES, :], W0).then_inc(in_w, 16)
            act.dma_start(w_r[:, TYPES + 1:TYPES + 3, :].rearrange("o a d -> o (a d)"), W1).then_inc(in_w, 16)
            act.dma_start(w_r[:, TYPES + 3, :], W2).then_inc(in_w, 16)
            for k in range(3):
                act.wait_ge(w_turned, k + 1)
                if k < 2:
                    act.copy(w0[:, 3 * D * k:3 * D * (k + 1)], ps_st[k][:, 0:3 * D]).then_inc(w_copied, 1)
                else:
                    act.copy(w1[:, D:2 * D], ps_qe[0][:, 0:D])
                    act.copy(w1[:, 0:D], ps_qe[0][:, D:2 * D])
                    act.copy(w2[:], ps_qe[0][:, 2 * D:3 * D]).then_inc(w_copied, 1)
            for vec, own in ((b2, bias2), (gamma, gam), (beta, bet)):
                act.dma_start(own[:], vec.rearrange("(a n) -> a n", a=1).to_broadcast([BN, D])).then_inc(in_b, 16)
            act.dma_start(bias_rows[:, 0, D:2 * D], b1.rearrange("(a n) -> a n", a=1)).then_inc(in_a, 16)
            for (ws, bs), w, i in ((att1, w3, 1), (att2, w4, 2)):
                for k in range(4):
                    act.dma_start(w[:, k * D:(k + 1) * D], ws[k]).then_inc(in_a, 16)
                    act.dma_start(bias_rows[:, i, k * D:(k + 1) * D], bs[k].rearrange("(a n) -> a n", a=1)).then_inc(in_a, 16)
            act.wait_ge(in_x, 16)
            act.wait_ge(planned, 1)
            together = act.value_load(plan[0:1, NB:NB + 1], min_val=0, max_val=1)
            with act.If(together > 0):
                layers_act(act, True)
            with act.Else():
                layers_act(act, False)
            act.nop()

        def layers_pe(pe, together):
            def make_rows(r, layer, before):
                turn_at = ps_mx[0] if layer == 4 else ps_st[r.half]
                banks = (ps_mx[1],) if layer == 4 else (ps_qe[r.half], ps_mx[r.half])
                w = WALL[layer]
                width = w.shape[1]
                pe.wait_ge(h_made[r.half], r.use + 1)
                pe.transpose(turn_at[:, 0:BN], hcur[:, r.half, :], ident[0:BN, 0:BN]).then_inc(h_turned[r.half], 1)
                pe.wait_ge(*before)
                if layer == 2:
                    pe.wait_ge(leaky_made[r.half], r.use - rows_before(together, 2)[r.half] + 1)
                else:
                    pe.wait_ge(ht_copied[r.half], r.use + 1)
                for k, to in enumerate(banks[0:-(-width // 512)]):
                    n = min(512, width - 512 * k)
                    if layer in BIAS:
                        pe.matmul(to[0:BN, 0:n], ones[0:1, 0:BN], bias_rows[:, BIAS[layer], 0:n], start=True, stop=False)
                    mm = pe.matmul(to[0:BN, 0:n], hT[:, r.half, :], w[:, 512 * k:512 * k + n],
                                   start=layer not in BIAS, stop=True)
                mm.then_inc(lin_made[r.half], 1)

            def last_kept(r, layer):
                n0, n1 = rows_before(together, layer)
                if layer != 4 or not together:
                    return kept[r.half], r.use
                return (kept[1], r.use - n0 + n1) if r.half == 0 else (kept[0], r.use - n1 + n0 + 1)

            def add_up(t, H):
                lo, w = (D, D + H) if H else (0, D)
                for c in range(NC):
                    if c == 0:
                        pe.wait_ge(acc_read, t.acc)
                    if H:
                        pe.wait_ge(v_scaled, t.msg * NC + c + 1)
                    else:
                        pe.wait_ge(gathered[t.half][c], 16 * CH * (t.use + 1))
                        pe.wait_ge(s_made[t.half], t.use * NC + c + 1)
                    for j in range(c * CH, (c + 1) * CH):
                        mm = pe.matmul(ps_acc[0:BN, 0:w], S[:, t.half, j, :], kv[:, t.half, j, lo:lo + w],
                                       start=(j == 0), stop=(j == TJ - 1))
                mm.then_inc(group_used[t.half], 1)

            def logit(t):
                def turn(c):
                    k = c % 2
                    pe.wait_ge(s_made[t.half], t.use * NC + c + 1)
                    pe.wait_ge(st_copied[k], t.logit * (NC // 2) + c // 2)
                    for i in range(CH):
                        mm = pe.transpose(ps_st[k][0:BN, i * P:(i + 1) * P], S[:, t.half, c * CH + i, :], ident[:])
                    mm.then_inc(st_made[k], 1)

                def queries(c):
                    k = c % 2
                    pe.wait_ge(st_copied[k], t.logit * (NC // 2) + c // 2 + 1)
                    pe.wait_ge(qe_read[k], t.logit * (NC // 2) + c // 2)
                    for i in range(CH):
                        mm = pe.matmul(ps_qe[k][:, i * D:(i + 1) * D], ST[:, t.half, c * CH + i, :], at(qs, t.block),
                                       start=True, stop=True)
                    mm.then_inc(qe_made[k], 1)

                turn(0)
                for c in range(NC):
                    if c + 1 < NC:
                        turn(c + 1)
                    queries(c)

            def carries(t, H):
                pe.wait_ge(scanned, 2 * (t.top + 1))
                f = fore[:, t.half, 0:H * TJ].rearrange("p (h j) -> p h j", h=H)
                g = back[:, t.half, 0:H * TJ].rearrange("p (h j) -> p h j", h=H)
                pe.transpose(ps_misc[0:H, 0:P], f[:, :, TJ - 1], ident[:])
                pe.transpose(ps_misc[0:H, P:2 * P], g[:, :, 0], ident[:]).then_inc(ends_turned, 1)
                pe.wait_ge(carried, 2 * (t.top + 1))
                pe.sem_inc(waits_passed, 1)
                pe.transpose(ps_misc[:, 2 * P:2 * P + H], down[0:H, 0:P], ident[0:H, 0:H])
                pe.transpose(ps_misc[:, 2 * P + 4:2 * P + 4 + H], up[0:H, 1:P + 1], ident[0:H, 0:H]).then_inc(carry_turned, 1)

            def maxima(t, H):
                pe.wait_ge(split, 5 * (t.top + 1))
                n = HALF * H * 3
                for a in range(2):
                    mm = pe.transpose(ps_misc[:].bitcast(BF16)[0:n, a * P:(a + 1) * P],
                                      parts[:, a * HALF * H:(a + 1) * HALF * H, :].rearrange("p i k -> p (i k)"), ident_b[:])
                mm.then_inc(parts_turned, 1)
                pe.wait_ge(parts_copied, t.top + 1)
                for j in range(TJ):
                    k = j % 2
                    pe.wait_ge(mx_read[k], t.top * HALF + j // 2)
                    own = mask[:, t.half, j, :]
                    for h in range(H):
                        pe.matmul(ps_mx[k][0:BN, h * P:(h + 1) * P], ident_b[0:BN, 0:BN], own, start=True, stop=False)
                        mm = pe.matmul(ps_mx[k][0:BN, h * P:(h + 1) * P], sel[0:n, (j % HALF) * H + h, :],
                                       partsT[0:n, j // HALF, :], start=False, stop=True)
                    mm.then_inc(mx_made[k], 1)
                pe.wait_ge(mx_read[0], (t.top + 1) * HALF)
                pe.wait_ge(mx_read[1], (t.top + 1) * HALF)
                pe.matmul(ps_misc[0:1, 0:1], ones[:, 0:1], ones[:, 0:1], start=True, stop=True).then_inc(group_used[t.half], 1)

            def spread(t, H, made):
                pe.wait_ge(top_all, made)
                for j in range(TJ):
                    mm = pe.matmul(ps_misc[:, j * H:(j + 1) * H], ST[:, t.half, j, :], top[:, 0:H], start=True, stop=True)
                mm.then_inc(me_made, 1)

            if not together:
                pe.wait_ge(sel_made, 1)
            for layer in range(LAYERS):
                H = HEADS[layer]
                if layer in (0, 3):
                    for _, cur, _ in skewed(pe, together, layer):
                        if cur:
                            make_rows(cur, layer, (kept[cur.half], cur.use))
                if layer == 0 and together:
                    pe.wait_ge(runs_made, 1)
                    for k in range(2 * NB):
                        if k % 4 == 0 and k >= 8:
                            pe.wait_ge(runs_copied, k // 4 - 1)
                        mm = pe.matmul(ps_st[(k // 4) % 2][0:4, (k % 4) * P:(k % 4 + 1) * P],
                                       runs[:, k // NB, k % NB:k % NB + 1].to_broadcast([P, 4]),
                                       (ident_b, turned_b)[k // NB][:], start=True, stop=True)
                        if k % 4 == 3 or k == 2 * NB - 1:
                            mm.then_inc(runs_turned, 1)
                if together:
                    for t, _ in sorted_turns(pe, layer):
                        if H:
                            logit(t)
                            carries(t, H)
                        add_up(t, H)
                        if layer in (0, 1, 3):
                            r = rows_of(t, True, layer + 1)
                            make_rows(r, layer + 1, last_kept(r, layer + 1))
                else:
                    with pe.Fori(0, NB) as b:
                        for sweep in range(2 if H else 1):
                            for t in any_turns(pe, layer, b, sweep):
                                if H:
                                    logit(t)
                                if H and sweep == 0:
                                    maxima(t, H)
                                else:
                                    if H:
                                        spread(t, H, (layer - 3) * NB * GG + (b + 1) * GG)
                                    add_up(t, H)
                        if layer in (0, 1, 3):
                            r = rows_of(b, False, layer + 1)
                            make_rows(r, layer + 1, last_kept(r, layer + 1))
                            pe.wait_ge(kept[0], r.use + 1)
                if layer == 2:
                    for k in range(2):
                        pe.wait_ge(bn_asked, (1, 3)[k])
                        pe.matmul(ps_misc[0:BN, k * D:(k + 1) * D], ones[0:BN, 0:BN], (zsum[:], bn_s[:, 0, :])[k],
                                  start=True, stop=True).then_inc(bn_summed, 1)

        @block.tensor
        def _(pe):
            pe.wait_ge(consts_made, 1)
            pe.wait_ge(all_made, 1)
            pe.matmul(ps_acc[0:1, 0:NB + 3], ones[0:ER, 0:1], cnt[:], start=True, stop=True).then_inc(counted, 1)
            for k in range(3):
                pe.wait_ge(w_made, 1)
                to = (ps_st[0], ps_st[1], ps_qe[0])[k]
                for i in range(3):
                    mm = pe.transpose(to[:, i * D:(i + 1) * D], w_r[:, 3 * k + i, :], ident[:])
                mm.then_inc(w_turned, 1)
            pe.wait_ge(w_copied, 3)
            pe.wait_ge(in_a, 16 * 17)
            pe.wait_ge(planned, 1)
            together = pe.value_load(plan[0:1, NB:NB + 1], min_val=0, max_val=1)
            with pe.If(together > 0):
                layers_pe(pe, True)
            with pe.Else():
                layers_pe(pe, False)
            pe.nop()

        def layers_dve(dve, together, done):
            v = nc.vector
            seen = [done]

            def link(ins):
                seen[0] += 1
                ins.then_inc(dve_step, 1)
                dve.wait_ge(dve_step, seen[0])

            root3 = root[:].rearrange("p (b d) -> p b d", d=D)

            def statistics(r):
                dve.wait_ge(x_here[r.half], r.use + 1)
                v.bn_stats(halfstat[:, r.half, :], xcur[:, r.half, :]).then_inc(halves_made[r.half], 1)
                dve.wait_ge(halves_made[r.half], r.use + 1)
                dve.sem_inc(waits_passed, 1)
                v.bn_aggr(meanvar[:, r.half, :], halfstat[:, r.half, :]).then_inc(var_made[r.half], 1)

            def normalise(r):
                dve.wait_ge(h_turned[r.half], r.use)
                dve.wait_ge(sdev_made[r.half], r.use + 1)
                v.reciprocal(rsdev[:, r.half:r.half + 1], sdev[:, r.half:r.half + 1]).then_inc(rsdev_made[r.half], 1)
                dve.wait_ge(rsdev_made[r.half], r.use + 1)
                v.tensor_scalar(hcur[:, r.half, :], xcur[:, r.half, :], meanvar[:, r.half, 0:1], rsdev[:, r.half:r.half + 1],
                                ALU.subtract, ALU.mult).then_inc(h_made[r.half], 1)

            def leaky(r):
                dve.wait_ge(ht_copied[r.half], r.use + 1)
                v.scalar_tensor_tensor(out=hT[:, r.half, :], in0=hT[:, r.half, :], scalar=0.2, in1=hT[:, r.half, :],
                                       op0=ALU.mult, op1=ALU.max).then_inc(leaky_made[r.half], 1)

            def keep(r, layer):
                dve.wait_ge(rows_made[r.half], r.use + 1)
                q, m = (ps_mx[1], None) if layer == 4 else (ps_qe[r.half], ps_mx[r.half])
                own, x_own = at(root, r.block), at(xs, r.block)
                if layer == 0:
                    ins = v.tensor_tensor(own, m[0:BN, D:2 * D], x_own, ALU.add)
                elif layer == 1:
                    ins = v.tensor_scalar(own, q[0:BN, D:2 * D], 1.0, None, ALU.mult)
                elif layer == 2:
                    ins = v.tensor_tensor(x_own, bet[:], x_own, ALU.add)
                elif layer == 3:
                    ins = v.tensor_scalar(own, q[0:BN, 3 * D:4 * D], 1.0, None, ALU.mult)
                else:
                    ins = v.tensor_tensor(own, q[0:BN, 3 * D:4 * D], x_own, ALU.add)
                ins.then_inc(kept[r.half], 1)

            def select_begin(t):
                dve.wait_ge(group_used[t.half], t.use)
                v.tensor_scalar(dloc[:, t.half, :], at(dst_f, t.col, TJ), at(base_n, t.block, 1), None, ALU.subtract
                                ).then_inc(dloc_made[t.half], 1)

            def select(t, c):
                if c == 0:
                    dve.wait_ge(dloc_made[t.half], t.use + 1)
                v.tensor_tensor(S[:, t.half, c * CH:(c + 1) * CH, :],
                                iota_n[:].rearrange("p (a n) -> p a n", a=1).to_broadcast([P, CH, BN]),
                                dloc[:, t.half, c * CH:(c + 1) * CH].rearrange("p (a n) -> p a n", n=1).to_broadcast([P, CH, BN]),
                                ALU.is_equal).then_inc(s_made[t.half], 1)

            def select_all(t):
                select_begin(t)
                for c in range(NC):
                    select(t, c)

            def logit(t, H, between=None):
                def product(c):
                    k = c % 2
                    dve.wait_ge(gathered[t.half][c], 16 * CH * (t.use + 1))
                    dve.wait_ge(logits_made[k], t.logit * (NC // 2) + c // 2)
                    dve.wait_ge(qe_made[k], t.logit * (NC // 2) + c // 2 + 1)
                    v.tensor_tensor(prod[:, k, :].rearrange("p (j d) -> p j d", d=D),
                                    ps_qe[k][:, 0:CH * D].rearrange("p (j d) -> p j d", d=D),
                                    kv[:, t.half, c * CH:(c + 1) * CH, 0:D], ALU.mult).then_inc(qe_read[k], 1)

                def head_sums(c):
                    k = c % 2
                    dve.wait_ge(qe_read[k], t.logit * (NC // 2) + c // 2 + 1)
                    if together:
                        to = alpha[:, t.half, 0:H * TJ].rearrange("p (h j) -> p h j", h=H)[:, :, c * CH:(c + 1) * CH] \
                            .rearrange("p h j -> p j h")
                    else:
                        to = alpha[:, t.half, c * CH * H:(c + 1) * CH * H].rearrange("p (j h) -> p j h", h=H)
                    v.tensor_reduce(to, prod[:, k, :].rearrange("p (j h d) -> p j h d", j=CH, h=H), AX.X, ALU.add
                                    ).then_inc(logits_made[k], 1)

                product(0)
                for c in range(NC):
                    if c + 1 < NC:
                        product(c + 1)
                    if c == 1 and between:
                        between()
                    head_sums(c)

            def logits_here(t):
                for k in range(2):
                    dve.wait_ge(logits_made[k], (t.logit + 1) * (NC // 2))

            def shift(t, H, nxt):
                n = TJ * H
                a, f, g = alpha[:, t.half, 0:n], fore[:, t.half, 0:n], back[:, t.half, 0:n]
                prev, foll = (at(either[:, k * FL:(k + 1) * FL], t.block, 4 * TJ)[:, 0:n] for k in range(2))
                if nxt:
                    select_begin(nxt)
                logits_here(t)
                v.tensor_tensor_scan(f, prev, a, UNLIKE, ALU.add, ALU.max).then_inc(scanned, 1)
                v.tensor_tensor_scan(g[:, ::-1], foll, a[:, ::-1], UNLIKE, ALU.add, ALU.max).then_inc(scanned, 1)
                if nxt:
                    select(nxt, 0)
                    select(nxt, 1)
                dve.wait_ge(scanned, 2 * (t.top + 1))
                m = rest[:, t.half, 0:n]
                v.tensor_tensor(m, f, g, ALU.max).then_inc(topped, 1)
                dve.wait_ge(ends_turned, t.top + 1)
                v.tensor_tensor_scan(down[0:H, 1:P + 1], at(run_down, t.block, P)[0:H], ps_misc[0:H, 0:P], UNLIKE,
                                     ALU.add, ALU.max).then_inc(carried, 1)
                v.tensor_tensor_scan(up[0:H, 0:P][:, ::-1], at(run_up, t.block, P)[0:H], ps_misc[0:H, P:2 * P][:, ::-1],
                                     UNLIKE, ALU.add, ALU.max).then_inc(carried, 1)
                if nxt:
                    select(nxt, 2)
                    select(nxt, 3)
                dve.wait_ge(carry_turned, t.top + 1)
                dve.wait_ge(topped, 5 * t.top + 1)
                for k, (like, own) in enumerate(((like_above, f), (like_below, g))):
                    v.tensor_tensor(own.rearrange("p (h j) -> p h j", h=H),
                                    ps_misc[:, 2 * P + 4 * k:2 * P + 4 * k + H].rearrange("p (h o) -> p h o", o=1).to_broadcast([P, H, TJ]),
                                    at(like, t.block, TJ).rearrange("p (o j) -> p o j", o=1).to_broadcast([P, H, TJ]),
                                    ALU.add).then_inc(topped, 1)
                dve.wait_ge(topped, 5 * t.top + 3)
                v.tensor_tensor(f, f, g, ALU.max).then_inc(topped, 1)
                dve.wait_ge(topped, 5 * t.top + 4)
                v.tensor_tensor(m, m, f, ALU.max).then_inc(topped, 1)
                dve.wait_ge(topped, 5 * t.top + 5)
                v.tensor_tensor(m, a, m, ALU.subtract).then_inc(shifted, 1)

            def maxima(t, H):
                n = TJ * H
                a, r = alpha[:, t.half, 0:n], rest[:, t.half, 0:n]
                logits_here(t)
                v.tensor_copy(parts[:, 0:n, 0], a).then_inc(split, 1)
                dve.wait_ge(split, 5 * t.top + 1)
                v.tensor_tensor(r, a, parts[:, 0:n, 0], ALU.subtract).then_inc(split, 1)
                dve.wait_ge(split, 5 * t.top + 2)
                v.tensor_copy(parts[:, 0:n, 1], r).then_inc(split, 1)
                dve.wait_ge(split, 5 * t.top + 3)
                v.tensor_tensor(r, r, parts[:, 0:n, 1], ALU.subtract).then_inc(split, 1)
                dve.wait_ge(split, 5 * t.top + 4)
                v.tensor_copy(parts[:, 0:n, 2], r).then_inc(split, 1)
                for j in range(TJ):
                    k = j % 2
                    dve.wait_ge(mx_made[k], t.top * HALF + j // 2 + 1)
                    v.tensor_reduce(tops[:, 0:H, j], ps_mx[k][0:BN, 0:H * P].rearrange("p (h e) -> p h e", e=P), AX.X, ALU.max
                                    ).then_inc(mx_read[k], 1)
                dve.wait_ge(mx_read[0], (t.top + 1) * HALF)
                dve.wait_ge(mx_read[1], (t.top + 1) * HALF)
                v.tensor_reduce(top[:, 0:H], tops[:, 0:H, :], AX.X, ALU.max).then_inc(top_made, 1)
                dve.wait_ge(top_made, 2 * t.top + 1)
                v.tensor_tensor(topn[:, 0:H], topn[:, 0:H], top[:, 0:H], ALU.max).then_inc(top_made, 1)
                dve.wait_ge(top_made, 2 * t.top + 2)
                v.tensor_copy(top[:, 0:H], topn[:, 0:H]).then_inc(top_all, 1)

            def shift_any(t, H):
                logits_here(t)
                dve.wait_ge(me_made, t.msg + 1)
                v.tensor_tensor(rest[:, t.half, 0:TJ * H].rearrange("p (h j) -> p j h", h=H),
                                alpha[:, t.half, 0:TJ * H].rearrange("p (j h) -> p j h", h=H),
                                ps_misc[:, 0:TJ * H].rearrange("p (j h) -> p j h", h=H), ALU.subtract).then_inc(shifted, 1)

            def messages(t, H):
                dve.wait_ge(exp_made, t.msg + 1)
                for c in range(NC):
                    tiles = kv[:, t.half, c * CH:(c + 1) * CH, :]
                    val = tiles[:, :, D:2 * D].rearrange("p j (h d) -> p j h d", h=H)
                    w = tiles[:, :, 2 * D:2 * D + H].rearrange("p j (h o) -> p j h o", o=1).to_broadcast([P, CH, H, D // H])
                    v.tensor_tensor(val, val, w, ALU.mult).then_inc(v_scaled, 1)

            def divide(sums, H, n, read):
                per = 3 if read is None else 2
                v.tensor_scalar(den[:, 0:H], sums[:, D:D + H], 1e-16, None, ALU.add).then_inc(normed, 1)
                dve.wait_ge(normed, per * n + 1)
                v.reciprocal(rden[:, 0:H], den[:, 0:H]).then_inc(normed, 1)
                dve.wait_ge(normed, per * n + 2)
                v.tensor_tensor(onorm[:].rearrange("p (h d) -> p h d", h=H), sums[:, 0:D].rearrange("p (h d) -> p h d", h=H),
                                rden[:, 0:H].rearrange("p (h o) -> p h o", o=1).to_broadcast([BN, H, D // H]), ALU.mult
                                ).then_inc(normed if read is None else read[0], 1)
                if read is None:
                    dve.wait_ge(normed, per * n + 3)
                else:
                    dve.wait_ge(*read)

            def to_hidden(r):
                dve.wait_ge(h_turned[r.half], r.use)
                v.tensor_tensor(hcur[:, r.half, :], onorm[:], at(root, r.block), ALU.add).then_inc(h_made[r.half], 1)

            def to_result(b):
                v.tensor_tensor(at(xs, b), onorm[:], at(root, b), ALU.add).then_inc(x_done, 1)

            def flags():
                d3 = dst_f[:].rearrange("p (b j) -> p b j", j=TJ)
                dve.wait_ge(beyond_in, 32)

                def outside(k):
                    return beyond[:, k, :].rearrange("p (b o) -> p b o", o=1).to_broadcast([P, NB, TJ])

                for h in range(4):
                    v.tensor_tensor(like_prev[:, :, h, 1:TJ], d3[:, :, 1:TJ], d3[:, :, 0:TJ - 1], ALU.not_equal)
                    v.tensor_tensor(like_next[:, :, h, TJ - 1:0:-1], d3[:, :, 1:TJ], d3[:, :, 0:TJ - 1], ALU.not_equal)
                v.tensor_tensor(like_above.rearrange("p (b j) -> p b j", j=TJ), d3, outside(0), ALU.not_equal)
                v.tensor_tensor(like_below.rearrange("p (b j) -> p b j", j=TJ), d3, outside(1), ALU.not_equal)
                v.tensor_tensor(runs[:, 0, :], ends[:, 1, :], beyond[:, 0, :], ALU.not_equal)
                v.memset(like_prev[:, :, :, 0:1], 1.0)
                v.memset(like_next[:, :, :, 0:1], 1.0)
                link(v.tensor_tensor(runs[:, 1, :], ends[:, 0, :], beyond[:, 1, :], ALU.not_equal))
                v.tensor_scalar(runs[:], runs[:], UNLIKE, None, ALU.mult).then_inc(runs_made, 1)
                flat = either[:, 0:2 * FL + 2 * NB * TJ]
                link(v.tensor_scalar(flat, flat, UNLIKE, None, ALU.mult))

            def add_sums(t, layer, r):
                own = at(root, t.block)
                if layer == 0:
                    dve.wait_ge(rows_made[r.half], r.use)
                    v.tensor_tensor(xcur[:, r.half, :], ps_acc[0:BN, 0:D], own, ALU.add).then_inc(x_here[r.half], 1)
                    dve.wait_ge(x_here[r.half], r.use + 1)
                    dve.sem_inc(acc_read, 1)
                elif layer == 1:
                    dve.wait_ge(rows_made[r.half], r.use)
                    v.tensor_tensor(onorm[:], ps_acc[0:BN, 0:D], own, ALU.add).then_inc(acc_read, 1)
                    dve.wait_ge(acc_read, t.acc + 1)
                    v.scalar_tensor_tensor(out=xcur[:, r.half, :], in0=onorm[:], scalar=0.0, in1=at(xs, t.block),
                                           op0=ALU.max, op1=ALU.add).then_inc(x_here[r.half], 1)
                else:
                    v.tensor_tensor(own, ps_acc[0:BN, 0:D], bias2[:], ALU.add).then_inc(acc_read, 1)
                    dve.wait_ge(acc_read, t.acc + 1)
                    dve.wait_ge(z_added, t.block)
                    v.tensor_tensor(zsum[:], zsum[:], own, ALU.add).then_inc(z_added, 1)

            def take_sums(b, layer, r):
                own = at(root, b)
                if layer == 0:
                    dve.wait_ge(rows_made[r.half], r.use)
                    v.tensor_copy(xcur[:, r.half, :], own).then_inc(x_here[r.half], 1)
                elif layer == 1:
                    dve.wait_ge(rows_made[r.half], r.use)
                    v.scalar_tensor_tensor(out=xcur[:, r.half, :], in0=own, scalar=0.0, in1=at(xs, b),
                                           op0=ALU.max, op1=ALU.add).then_inc(x_here[r.half], 1)
                else:
                    dve.wait_ge(z_added, 2 * b + 1)
                    v.tensor_tensor(zsum[:], zsum[:], own, ALU.add).then_inc(z_added, 1)

            def next_rows(r, layer):
                statistics(r)
                normalise(r)
                if layer == 1:
                    leaky(r)
                keep(r, layer + 1)

            for layer in range(LAYERS):
                H = HEADS[layer]
                if layer in (0, 3):
                    for nxt, cur, prev in skewed(dve, together, layer):
                        if nxt:
                            if layer:
                                dve.wait_ge(rows_made[nxt.half], nxt.use)
                                v.tensor_tensor(onorm[:], at(root, nxt.block), bn_s[:, 0, :], ALU.mult).then_inc(scaled, 1)
                                dve.wait_ge(scaled, nxt.block + 1)
                                v.tensor_tensor(xcur[:, nxt.half, :], onorm[:], at(xs, nxt.block), ALU.add).then_inc(x_here[nxt.half], 1)
                            statistics(nxt)
                        if cur:
                            normalise(cur)
                        if prev:
                            keep(prev, layer)
                if together:
                    select_all(first_turn(layer))
                    if layer == 0:
                        flags()
                    for t, nxt in sorted_turns(dve, layer):
                        r = rows_of(t, True, layer + 1)
                        if not H:
                            if nxt:
                                select_all(nxt)
                            dve.wait_ge(group_used[t.half], t.use + 1)
                            add_sums(t, layer, r)
                            if layer < 2:
                                next_rows(r, layer)
                            continue
                        logit(t, H)
                        shift(t, H, nxt)
                        messages(t, H)
                        dve.wait_ge(group_used[t.half], t.use + 1)
                        if layer == 4:
                            dve.wait_ge(x_done, t.block)
                        divide(ps_acc[0:BN, :], H, t.msg, (acc_read, t.acc + 1))
                        if layer == 3:
                            to_hidden(r)
                        else:
                            to_result(t.block)
                        if nxt:
                            select(nxt, 4)
                            select(nxt, 5)
                        if layer == 3:
                            keep(r, 4)
                else:
                    with dve.Fori(0, NB) as b:
                        r = rows_of(b, False, layer + 1)
                        if not H:
                            if layer == 2:
                                v.tensor_copy(at(root, b), bias2[:]).then_inc(z_added, 1)
                                dve.wait_ge(z_added, 2 * b + 1)
                                dve.sem_inc(waits_passed, 1)
                            for t in any_turns(dve, layer, b, 0):
                                select_all(t)
                                dve.wait_ge(group_used[t.half], t.use + 1)
                                dve.wait_ge(acc_read, t.acc)
                                v.tensor_tensor(at(root, b), ps_acc[0:BN, 0:D], at(root, b), ALU.add).then_inc(acc_read, 1)
                            dve.wait_ge(acc_read, (layer * NB + b + 1) * GG)
                            take_sums(b, layer, r)
                            if layer < 2:
                                next_rows(r, layer)
                            else:
                                dve.wait_ge(z_added, 2 * b + 2)
                                dve.sem_inc(waits_passed, 1)
                        else:
                            before = (layer - 3) * NB + b
                            v.memset(msum[:], 0.0).then_inc(block_begun, 1)
                            v.memset(topn[:], -BIG).then_inc(block_begun, 1)
                            dve.wait_ge(block_begun, 2 * before + 2)
                            dve.sem_inc(waits_passed, 1)
                            for t in any_turns(dve, layer, b, 0):
                                select_all(t)
                                logit(t, H)
                                maxima(t, H)
                            for t in any_turns(dve, layer, b, 1):
                                select_all(t)
                                logit(t, H)
                                shift_any(t, H)
                                messages(t, H)
                                dve.wait_ge(group_used[t.half], t.use + 1)
                                dve.wait_ge(acc_read, t.acc)
                                v.tensor_tensor(msum[:, 0:D + H], msum[:, 0:D + H], ps_acc[0:BN, 0:D + H], ALU.add).then_inc(acc_read, 1)
                            dve.wait_ge(acc_read, (layer * NB + b + 1) * GG)
                            divide(msum, H, before, None)
                            if layer == 3:
                                to_hidden(r)
                                keep(r, 4)
                            else:
                                to_result(b)
                                dve.wait_ge(x_done, b + 1)
                                dve.sem_inc(waits_passed, 1)
                if layer == 2:
                    dve.wait_ge(z_added, NB if together else 2 * NB)
                    v.memset(den[:], 0.0).then_inc(bn_asked, 1)
                    dve.wait_ge(bn_summed, 1)
                    link(v.tensor_scalar(bn_s[:, 1, :], ps_misc[0:BN, 0:D], 1.0 / N, None, ALU.mult))
                    v.tensor_tensor(root3, root3, bn_s[:, 1:2, :].to_broadcast([BN, NB, D]), ALU.subtract).then_inc(bn_asked, 1)
                    dve.wait_ge(bn_var, 1)
                    v.tensor_reduce(bn_s[:, 0, :], squares.rearrange("p (b d) -> p d b", d=D), AX.X, ALU.add).then_inc(bn_asked, 1)
                    dve.wait_ge(bn_summed, 2)
                    v.tensor_scalar(bn_s[:, 2, :], ps_misc[0:BN, D:2 * D], 1.0 / N, EPS, ALU.mult, ALU.add).then_inc(bn_var, 1)
                    dve.wait_ge(bn_dev, 1)
                    link(v.reciprocal(bn_s[:, 1, :], bn_s[:, 3, :]))
                    link(v.tensor_tensor(bn_s[:, 0, :], bn_s[:, 1, :], gam[:], ALU.mult))

        @block.vector
        def _(dve):
            v = nc.vector
            seen = [0]

            def link(ins):
                seen[0] += 1
                ins.then_inc(dve_step, 1)
                dve.wait_ge(dve_step, seen[0])

            dve.wait_ge(in_all, 32)
            dve.wait_ge(consts_made, 1)
            v.tensor_copy(nxt_f[0:ER - 1, :], nxt_i[0:ER - 1, :])
            link(v.tensor_copy(all_f, all_i))
            for b in range(NB):
                link(v.tensor_scalar(hits, all_f, float(BN * b), 0.0, ALU.is_lt, ALU.add, accum_out=cnt[:, b:b + 1]))
            v.tensor_tensor(cnt[:, NB + 1:NB + 2], all_f[:, EW - 1:EW], nxt_f[:], ALU.is_gt)
            v.memset(cnt[:, NB + 2:NB + 3], 0.0)
            link(v.tensor_tensor(hits[:, 0:EW - 1], all_f[:, 0:EW - 1], all_f[:, 1:EW], ALU.is_gt))
            v.tensor_reduce(cnt[:, NB:NB + 1], hits[:, 0:EW - 1], AX.X, ALU.add).then_inc(all_made, 1)
            dve.wait_ge(in_w, 16 * 5)
            for k in range(BASES):
                for r in range(TYPES):
                    wk = w_in[:, k * D:(k + 1) * D]
                    a = a_bc[:, r * BASES + k:r * BASES + k + 1]
                    if k == 0:
                        ins = v.tensor_scalar(w_r[:, r, :], wk, a, None, ALU.mult)
                    else:
                        ins = v.scalar_tensor_tensor(out=w_r[:, r, :], in0=wk, scalar=a, in1=w_r[:, r, :],
                                                     op0=ALU.mult, op1=ALU.add)
                if k < BASES - 1:
                    link(ins)
            ins.then_inc(w_made, 1)
            dve.wait_ge(counted, 1)
            link(v.tensor_copy(total[:], ps_acc[0:1, 0:NB + 3]))
            v.tensor_scalar(plan_f[:], total[:], float(E - GE), None, ALU.min)
            v.tensor_tensor(steps[:, 0:NB - 1], total[:, 1:NB], total[:, 0:NB - 1], ALU.subtract)
            link(v.tensor_scalar(steps[:, NB - 1:NB], total[:, NB - 1:NB], -1.0, float(E), ALU.mult, ALU.add))
            link(v.tensor_reduce(steps[:, NB:NB + 1], steps[:, 0:NB], AX.X, ALU.max))
            link(v.tensor_scalar(steps[:, NB:NB + 1], steps[:, NB:NB + 1], float(GE), None, ALU.is_le))
            link(v.tensor_tensor(steps[:, NB + 1:NB + 2], total[:, NB:NB + 1], total[:, NB + 1:NB + 2], ALU.add))
            link(v.tensor_scalar(steps[:, NB + 1:NB + 2], steps[:, NB + 1:NB + 2], 0.0, None, ALU.is_equal))
            link(v.tensor_tensor(plan_f[:, NB:NB + 1], steps[:, NB:NB + 1], steps[:, NB + 1:NB + 2], ALU.mult))
            v.tensor_copy(plan[:], plan_f[:]).then_inc(planned, 1)
            dve.wait_ge(in_x, 16)
            dve.wait_ge(in_b, 48)
            dve.wait_ge(planned, 1)
            together = dve.value_load(plan[0:1, NB:NB + 1], min_val=0, max_val=1)
            with dve.If(together > 0):
                dve.wait_ge(edges_in, 16 * 3 * NB)
                v.tensor_copy(dst_f[:], dst_i[:]).then_inc(edges_made, 1)
                v.scalar_tensor_tensor(out=typ_i[:], in0=src_i[:], scalar=float(TYPES), in1=typ_i[:],
                                       op0=ALU.mult, op1=ALU.add).then_inc(edges_made, 2)
                dve.wait_ge(edges_made, 3)
                for k in range(2):
                    v.tensor_copy(ends[:, k, :], dst_f[:].rearrange("p (b j) -> p b j", j=TJ)[:, :, k * (TJ - 1)]
                                  ).then_inc(ends_made, 1)
                layers_dve(dve, True, seen[0])
            with dve.Else():
                dve.wait_ge(edges_in, 16 * 3 * GG)
                n = GG * TJ
                v.tensor_scalar(rest[:, 0, 0:TJ], iota_e[:], float((GG - 1) * GE - (E - GE)), FAR, ALU.is_lt, ALU.mult)
                v.tensor_copy(dst_f[:, 0:n], dst_i[:, 0:n]).then_inc(edges_made, 1)
                dve.wait_ge(edges_made, 1)
                v.tensor_tensor(dst_f[:, n - TJ:n], dst_f[:, n - TJ:n], rest[:, 0, 0:TJ], ALU.add).then_inc(edges_made, 1)
                v.scalar_tensor_tensor(out=typ_i[:, 0:n], in0=src_i[:, 0:n], scalar=float(TYPES), in1=typ_i[:, 0:n],
                                       op0=ALU.mult, op1=ALU.add).then_inc(edges_made, 1)
                dve.wait_ge(edges_made, 3)
                layers_dve(dve, False, seen[0])
            dve.nop()


_INS = ['x', 'src', 'dst', 'edge_type_5', 'L0_gnn_B', 'L0_gnn_A', 'L0_gnn_W0', 'L1_gnn_W', 'L1_gnn_b',
        'L2_gnn_W', 'L2_gnn_b', 'L2_gnn_gamma', 'L2_gnn_beta']
_ATT = [f"L3_gnn_{kind}{n}" for n in (1, 2) for kind in ("Wk", "Wv", "Wq", "Ws", "bk", "bv", "bq", "bs")]


def kernel(**inputs):
    import numpy as _np
    import concourse.bacc as _bacc
    from concourse import mybir as _mybir
    from concourse.bass_utils import run_bass_kernel_spmd as _run

    nc = _bacc.Bacc("TRN2", target_bir_lowering=False, num_devices=1)
    arrays, aps = {}, {}
    for name in _INS + _ATT:
        a = _np.ascontiguousarray(inputs[name])
        arrays[f"in_{name}"] = a
        aps[name] = nc.dram_tensor(f"in_{name}", a.shape, _mybir.dt.from_np(a.dtype), kind="ExternalInput").ap()
    out = nc.dram_tensor("out", (N, D), _mybir.dt.float32, kind="ExternalOutput").ap()
    att = [([aps[n] for n in _ATT[8 * k:8 * k + 4]], [aps[n] for n in _ATT[8 * k + 4:8 * k + 8]]) for k in range(2)]
    build(nc, *[aps[n] for n in _INS], *att, out)
    r = _run(nc, [arrays], core_ids=[0])
    return r.results[0]["out"]
```

```python
from collections import namedtuple
from contextlib import ExitStack

import concourse.bass as bass
from concourse import mybir

ALU = mybir.AluOpType
ACT = mybir.ActivationFunctionType
AX = mybir.AxisListType
BF16 = mybir.dt.bfloat16
F32 = mybir.dt.float32
I32 = mybir.dt.int32

P = 128
N, D, E = 3125, 128, 53125
NB = 25
BN = N // NB
TJ = 18
GE = TJ * P
LE = GE - P
CH = 3
NC = TJ // CH
GG = -(-E // GE)
TYPES, BASES = 5, 4
HALF = TJ // 2
EW = 425
ER = E // EW
FAR = 1.0e6
BIG = float(2 ** 100)
EPS = 1e-5
LAYERS = 5
HEADS = (0, 0, 0, 4, 1)
TABLE = (TYPES * D, D, D, 2 * D, 2 * D)
KV = 2 * D + 4
UNLIKE = -BIG
PIECES = (0, 15, NB)
assert NB * BN == N and ER * EW == E and NB % 2 == 1 and GG % 2 == 0 and TJ * NB >= TJ * GG

LEAD = 1

Turn = namedtuple("Turn", "half use logit top msg acc block col")
Rows = namedtuple("Rows", "half use block slot slot_use", defaults=(0, 0))
SLOTS = 4
EVEN, ODD = (NB + 1) // 2, NB // 2


def sorted_turn(layer, half, i):
    att = max(layer - 3, 0) * NB
    b = 2 * i + half
    return Turn(half, (EVEN, ODD)[half] * layer + i, att + b, att + b, att + b, NB * layer + b, b, b)


def turns_two_on(eng, layer):
    with eng.Fori(0, ODD - 1) as i:
        for half in range(2):
            yield sorted_turn(layer, half, i), sorted_turn(layer, half, i + 1)
    yield sorted_turn(layer, 0, ODD - 1), sorted_turn(layer, 0, ODD)
    yield sorted_turn(layer, 1, ODD - 1), None
    yield sorted_turn(layer, 0, ODD), None


def sorted_turns(eng, layer):
    with eng.Fori(0, ODD) as i:
        yield sorted_turn(layer, 0, i), sorted_turn(layer, 1, i)
        yield sorted_turn(layer, 1, i), sorted_turn(layer, 0, i + 1)
    yield sorted_turn(layer, 0, ODD), None


def any_turns(eng, layer, block, sweep):
    h = GG // 2
    att = layer - 3
    use0 = NB * h * layer if layer < 3 else NB * h * 3 + 2 * NB * h * att
    with eng.Fori(0, h) as k:
        for half in range(2):
            g = 2 * k + half
            n = block * GG + g
            if layer < 3:
                yield Turn(half, use0 + block * h + k, 0, 0, 0, NB * GG * layer + n, block, g)
            else:
                yield Turn(half, use0 + block * GG + sweep * h + k,
                           2 * NB * GG * att + block * (2 * GG) + sweep * GG + g,
                           NB * GG * att + n, NB * GG * att + n, NB * GG * layer + n, block, g)


def rows_before(together, layer):
    inside = (EVEN, ODD) if together else (NB, 0)
    per = [(EVEN, ODD), inside, inside, (EVEN, ODD), inside]
    return sum(p[0] for p in per[:layer]), sum(p[1] for p in per[:layer])


def rows_in_order(eng, together, layer):
    n0, n1 = rows_before(together, layer)
    if together or layer in (0, 3):
        with eng.Fori(0, ODD) as i:
            yield Rows(0, n0 + i, 2 * i)
            yield Rows(1, n1 + i, 2 * i + 1)
        yield Rows(0, n0 + ODD, NB - 1)
    else:
        with eng.Fori(0, NB) as b:
            yield Rows(0, n0 + b, b)


def rows_of(t, together, layer):
    n0, n1 = rows_before(together, layer)
    if not together:
        return Rows(0, n0 + t, t)
    return Rows(t.half, (n0, n1)[t.half] + t.use - (EVEN, ODD)[t.half] * (layer - 1), t.block)


def skewed(eng, together, layer):
    base = rows_before(together, layer)

    def rows(j):
        return Rows(j % 2, base[j % 2] + j // 2, j, j % SLOTS, j // SLOTS)

    def at(k, j):
        return Rows(j % 2, k * (SLOTS // 2) + (base[j % 2] + j // 2), k * SLOTS + j, j % SLOTS, k + j // SLOTS)

    begin = 2 * SLOTS + (NB - 2 * SLOTS) % SLOTS
    for b in range(begin):
        yield tuple(rows(b - k) if b >= k else None for k in range(5))
    with eng.Fori(0, (NB - begin) // SLOTS) as k:
        for b in range(begin, begin + SLOTS):
            yield tuple(at(k, b - j) for j in range(5))
    for b in range(NB, NB + 4):
        yield tuple(rows(b - k) if b - k < NB else None for k in range(5))


def build(nc, x, src, dst, etype, B, A, W0, W1, b1, W2, b2, gamma, beta, att1, att2, out):
    with ExitStack() as ctx:
        def sb(name, shape, dt=F32):
            return ctx.enter_context(nc.sbuf_tensor(name, shape, dt))

        def sem(name):
            return ctx.enter_context(nc.semaphore(name))

        def pair(name):
            return [sem(f"{name}{i}") for i in range(2)]

        bank = [ctx.enter_context(nc.psum_tensor(f"bank{i}", [P, 512], F32)) for i in range(8)]
        ps_qe, ps_st, ps_mx, ps_misc, ps_acc = bank[0:2], bank[2:4], bank[4:6], bank[6], bank[7]

        xs = sb("xs", [BN, NB * D])
        root = sb("root", [BN, NB * D])
        qs = sb("qs", [BN, NB * D])
        xcur = sb("xcur", [BN, 2, D])
        hcur = sb("hcur", [BN, 2, D])
        hT = sb("hT", [P, 2, BN])
        halfstat = sb("halfstat", [BN, 2, 6])
        meanvar = sb("meanvar", [BN, 2, 2])
        sdev = sb("sdev", [BN, 2])
        rsdev = sb("rsdev", [BN, 2])
        eps = sb("eps", [BN, 1])
        rows = sb("rows", [BN, 2, 2 * D])
        zsum = sb("zsum", [BN, D])
        bn_s = sb("bn_s", [BN, 4, D])
        src_i = sb("src_i", [P, NB * TJ], I32)
        dst_i = sb("dst_i", [P, NB * TJ], I32)
        typ_i = sb("typ_i", [P, NB * TJ], I32)
        dst_f = sb("dst_f", [P, NB * TJ])
        idx = sb("idx", [P, 2, TJ], I32)
        dloc = sb("dloc", [P, 2, TJ])
        kv = sb("kv", [P, 2, TJ, KV])
        S = sb("S", [P, 2, TJ, BN])
        ST = sb("ST", [BN, 2, TJ, P])
        prod = sb("prod", [P, 2, CH * D])
        alpha = sb("alpha", [P, 2, 4 * TJ])
        rest = sb("rest", [P, 2, 4 * TJ])
        fore = sb("fore", [P, 2, 4 * TJ])
        back = sb("back", [P, 2, 4 * TJ])
        parts = sb("parts", [P, TJ * 4, 3], BF16)
        partsT = sb("partsT", [HALF * 12, 2, P], BF16)
        tops = sb("tops", [BN, 4, TJ])
        top = sb("top", [BN, 4])
        topn = sb("topn", [BN, 4])
        den = sb("den", [BN, 4])
        rden = sb("rden", [BN, 4])
        onorm = sb("onorm", [BN, D])
        msum = sb("msum", [BN, D + 4])
        FL = NB * 4 * TJ
        either = sb("either", [P, 2 * FL + 2 * NB * TJ + 2 * NB * P], BF16)
        like_prev = either[:, 0:FL].rearrange("p (b h j) -> p b h j", b=NB, h=4)
        like_next = either[:, FL:2 * FL].rearrange("p (b h j) -> p b h j", b=NB, h=4)
        like_above = either[:, 2 * FL:2 * FL + NB * TJ]
        like_below = either[:, 2 * FL + NB * TJ:2 * FL + 2 * NB * TJ]
        run_down = either[0:4, 2 * FL + 2 * NB * TJ:2 * FL + 2 * NB * TJ + NB * P]
        run_up = either[0:4, 2 * FL + 2 * NB * TJ + NB * P:]
        mask = either[0:BN, 0:2 * TJ * P].rearrange("p (a j e) -> p a j e", a=2, j=TJ)
        ends = sb("ends", [P, 2, NB])
        beyond = sb("beyond", [P, 2, NB])
        runs = sb("runs", [P, 2, NB], BF16)
        down = sb("down", [4, P + 1])
        up = sb("up", [4, P + 1])
        first_rows = ST[:].rearrange("p a j e -> p (a j e)")[:, 0:SLOTS * TABLE[0]].rearrange("p (s w) -> p s w", s=SLOTS)
        iota_n = sb("iota_n", [P, BN])
        iota_e = sb("iota_e", [P, TJ])
        base_n = sb("base_n", [P, NB])
        ident = sb("ident", [P, P])
        ident_b = sb("ident_b", [P, P], BF16)
        turned_b = sb("turned_b", [P, P], BF16)
        sel = sb("sel", [HALF * 12, HALF * 4, BN], BF16)
        ones = sb("ones", [P, P])
        bases_in = sb("bases_in", [P, 4 * D])
        w_r = sb("w_r", [P, 9, D])
        a_bc = sb("a_bc", [P, TYPES * BASES])
        w0 = sb("w0", [P, (TYPES + 1) * D])
        w1 = sb("w1", [P, 2 * D])
        w2 = sb("w2", [P, D])
        w3 = sb("w3", [P, 4 * D])
        w4 = sb("w4", [P, 4 * D])
        bias2, gam, bet = (sb(n, [BN, D]) for n in ("bias2", "gam", "bet"))
        bias_rows, bias_rest = sb("bias_rows", [3, 3, 4 * D]), sb("bias_rest", [3, 3, 4 * D])
        bias_part, bias_parts = sb("bias_part", [3, 3, 4 * D], BF16), sb("bias_parts", [3, 3, 4 * D], BF16)
        ones_b = sb("ones_b", [3, BN], BF16)
        all_i = S[0:ER, 0, 0:4, :].rearrange("p a b -> p (a b)").bitcast(I32)[:, 0:EW]
        all_f = S[0:ER, 0, 4:8, :].rearrange("p a b -> p (a b)")[:, 0:EW]
        hits = [S[0:ER, 1, 4 * k:4 * k + 4, :].rearrange("p a b -> p (a b)")[:, 0:EW] for k in range(4)]
        squares = kv[0:BN, 0, :, :].rearrange("p a b -> p (a b)")[:, 0:NB * D]
        nxt_i = sb("nxt_i", [ER, 1], I32)
        nxt_f = sb("nxt_f", [ER, 1])
        cnt = sb("cnt", [ER, NB + 3])
        total = sb("total", [1, NB + 3])
        block_edges = sb("block_edges", [1, NB + 3])
        plan_f = sb("plan_f", [1, NB + 3])
        plan = sb("plan", [1, NB + 3], I32)
        full_f, full = sb("full_f", [1, NB]), sb("full", [1, NB], I32)
        due_f, due = sb("due_f", [1, 2 + LAYERS, NB + 1]), sb("due", [1, LAYERS * NB], I32)
        lean_p, full_p = sb("lean_p", [P, NB]), sb("full_p", [P, NB])
        beyond_lean = sb("beyond_lean", [P, NB])

        tables = [nc.dram_tensor(f"table{i}", (N, TABLE[i]), F32, kind="Internal").ap() for i in range(LAYERS)]

        in_x, in_w, in_b, in_all, in_a = sem("in_x"), sem("in_w"), sem("in_b"), sem("in_all"), sem("in_a")
        pool_step, dve_step = sem("pool_step"), sem("dve_step")
        consts_made, w_made, w_turned, sel_made = sem("consts_made"), sem("w_made"), sem("w_turned"), sem("sel_made")
        bias_cleared, bias_split = sem("bias_cleared"), sem("bias_split")
        w_copied, all_made, counted, planned = sem("w_copied"), sem("all_made"), sem("counted"), sem("planned")
        edges_in, edges_made = sem("edges_in"), sem("edges_made")
        ends_made, beyond_in, runs_made, runs_turned, runs_copied = (
            sem("ends_made"), sem("beyond_in"), sem("runs_made"), sem("runs_turned"), sem("runs_copied"))
        x_here, halves_made, var_made, sdev_made, rsdev_made = (
            pair("x_here"), pair("halves_made"), pair("var_made"), pair("sdev_made"), pair("rsdev_made"))
        h_made, h_turned, ht_copied, leaky_made = pair("h_made"), pair("h_turned"), pair("ht_copied"), pair("leaky_made")
        lin_made, rows_made, kept = pair("lin_made"), pair("rows_made"), pair("kept")
        first_out, rows_out = [sem(f"first_out{i}") for i in range(SLOTS)], pair("rows_out")
        x_stored = pair("x_stored")
        bn_asked, bn_summed, bn_var, bn_dev, scaled = (
            sem("bn_asked"), sem("bn_summed"), sem("bn_var"), sem("bn_dev"), sem("scaled"))
        idx_in, dloc_made, s_made, group_used = pair("idx_in"), pair("dloc_made"), pair("s_made"), pair("group_used")
        gathered = [[[sem(f"gathered_{kind}{h}_{c}") for c in range(NC)] for h in range(2)] for kind in ("sum", "att")]
        last_in = pair("last_in")
        due_made, full_spread, full_here, lean_made, lean_below = sem("due_made"), sem("full_spread"), sem("full_here"), sem("lean_made"), sem("lean_below")
        acc_read, block_begun, z_added = sem("acc_read"), sem("block_begun"), sem("z_added")
        waits_passed = sem("waits_passed")
        st_made, st_copied, qe_made, qe_read = pair("st_made"), pair("st_copied"), pair("qe_made"), pair("qe_read")
        logits_made = pair("logits_made")
        scanned, ends_turned, carried, carry_turned, topped = (
            sem("scanned"), sem("ends_turned"), sem("carried"), sem("carry_turned"), sem("topped"))
        split, parts_turned, parts_copied = sem("split"), sem("parts_turned"), sem("parts_copied")
        mx_made, mx_read = pair("mx_made"), pair("mx_read")
        top_made, top_all, me_made, shifted, exp_made, v_scaled, normed = (
            sem("top_made"), sem("top_all"), sem("me_made"), sem("shifted"), sem("exp_made"), sem("v_scaled"),
            sem("normed"))
        x_done, stored = sem("x_done"), sem("stored")

        block = ctx.enter_context(nc.Block())

        def wait_kv(eng, t, layer, c, together):
            before = 0 if layer < 3 else 3 * (EVEN, ODD)[t.half] if together else 3 * NB * (GG // 2)
            tiles = CH if c < NC - 1 else CH - 1
            eng.wait_ge(gathered[layer >= 3][t.half][c], 16 * tiles * (t.use - before + 1))
            if c == NC - 1 and together:
                own = due[0:1, bass.ds(t.block + NB * layer, 1)] if not isinstance(t.block, int) \
                    else due[0:1, NB * layer + t.block:NB * layer + t.block + 1]
                eng.wait_ge(last_in[t.half], eng.value_load(own, min_val=16, max_val=16 * LAYERS * NB))
            elif c == NC - 1:
                eng.wait_ge(last_in[t.half], 16 * (t.use + 1))

        def at(t, b, w=D):
            return t[:, b * w:(b + 1) * w] if isinstance(b, int) else t[:, bass.ds(b * w, w)]

        WALL = [w0, w1, w2, w3, w4]
        BIAS = {1: 0, 3: 1, 4: 2}

        def load_blocks(sp, piece):
            with sp.Fori(PIECES[piece] // 5, PIECES[piece + 1] // 5) as i:
                fulls = [sp.value_load(full[0:1, bass.ds(i * 5 + k, 1)], min_val=0, max_val=1) for k in range(5)]

                def load(k, tiles):
                    base = sp.value_load(plan[0:1, bass.ds(i * 5 + k, 1)], min_val=0, max_val=E - tiles * P)
                    for arr, own in ((dst, dst_i), (src, src_i), (etype, typ_i)):
                        sp.dma_start(own[:, bass.ds(i * (5 * TJ) + k * TJ, tiles)],
                                     arr[bass.ds(base, tiles * P)].rearrange("(p j) -> p j", j=tiles)).then_inc(edges_in, 16)

                for k in range(5):
                    with sp.If(fulls[k] > 0):
                        load(k, TJ)
                    with sp.Else():
                        load(k, TJ - 1)

        def layers_sp(sp, together):
            def indices(t, layer):
                sp.wait_ge(group_used[t.half], t.use + LEAD)
                sp.dma_start(idx[:, t.half, :], at(src_i if layer else typ_i, t.col, TJ)).then_inc(idx_in[t.half], 16)

            def store_rows(r, layer):
                to = tables[layer][bass.ds(r.block * BN, BN), :] if not isinstance(r.block, int) \
                    else tables[layer][r.block * BN:(r.block + 1) * BN, :]
                sp.wait_ge(rows_made[r.half], r.use + 1 + LEAD)
                sp.dma_start(to, rows[:, r.half, 0:TABLE[layer]]).then_inc(rows_out[r.half], 16)

            def store_result(b):
                to = out[bass.ds(b * BN, BN), :] if not isinstance(b, int) else out[b * BN:(b + 1) * BN, :]
                sp.wait_ge(x_done, b + 1 + LEAD)
                sp.dma_start(to, at(xs, b)).then_inc(stored, 16)

            if together:
                load_blocks(sp, 0)
            sp.wait_ge(edges_made, 3)
            for layer in range(LAYERS):
                if layer == 3:
                    for r in rows_in_order(sp, together, 3):
                        store_rows(r, 3)
                if together:
                    for half in range(2):
                        indices(sorted_turn(layer, half, 0), layer)
                    if layer == 0:
                        load_blocks(sp, 1)
                        sp.wait_ge(ends_made, 2)
                        sp.dma_start(beyond[1:P, 0, :], ends[0:P - 1, 1, :]).then_inc(beyond_in, 16)
                        sp.dma_start(beyond[0:P - 1, 1, :], ends[1:P, 0, :]).then_inc(beyond_in, 16)
                        sp.wait_ge(edges_made, 6)
                    for t, ahead in turns_two_on(sp, layer):
                        if ahead:
                            indices(ahead, layer)
                        if layer in (0, 1, 3):
                            store_rows(rows_of(t, True, layer + 1), layer + 1)
                        elif layer == 4:
                            store_result(t.block)
                else:
                    with sp.Fori(0, NB) as b:
                        for sweep in range(1 if layer < 3 else 2):
                            for t in any_turns(sp, layer, b, sweep):
                                indices(t, layer)
                        if layer in (0, 1, 3):
                            store_rows(rows_of(b, False, layer + 1), layer + 1)
                        elif layer == 4:
                            store_result(b)
            sp.wait_ge(stored, 16 * NB)
            for half in range(2):
                sp.wait_ge(rows_out[half], 16 * (rows_before(together, LAYERS)[half] - (EVEN, ODD)[half]) + LEAD)

        @block.sync
        def _(sp):
            for room in rows_out:
                sp.sem_inc(room, LEAD)
            sp.dma_start(all_i, dst.rearrange("(p w) -> p w", w=EW)).then_inc(in_all, 16)
            sp.dma_start(nxt_i[0:ER - 1, :], dst[EW:E].rearrange("(p w) -> p w", w=EW)[:, 0:1],
                         allow_slow_non_contiguous=True).then_inc(in_all, 16)
            sp.dma_start(xs[:].rearrange("p (b d) -> p b d", d=D), x.rearrange("(b p) d -> p b d", p=BN)).then_inc(in_x, 16)
            sp.wait_ge(bias_cleared, 1)
            sp.dma_start(bias_rows[:, 0, D:2 * D], b1.rearrange("(a n) -> a n", a=1).to_broadcast([3, D])).then_inc(in_a, 16)
            for (ws, bs), w, i in ((att1, w3, 1), (att2, w4, 2)):
                for k in range(4):
                    sp.dma_start(w[:, k * D:(k + 1) * D], ws[k]).then_inc(in_a, 16)
                    sp.dma_start(bias_rows[:, i, k * D:(k + 1) * D], bs[k].rearrange("(a n) -> a n", a=1).to_broadcast([3, D])
                                  ).then_inc(in_a, 16)
            sp.wait_ge(consts_made, 1)
            sp.wait_ge(planned, 1)
            together = sp.value_load(plan[0:1, NB:NB + 1], min_val=0, max_val=1)
            with sp.If(together > 0):
                layers_sp(sp, True)
            with sp.Else():
                with sp.Fori(0, GG - 1) as g:
                    for arr, own in ((dst, dst_i), (src, src_i), (etype, typ_i)):
                        sp.dma_start(own[:, bass.ds(g * TJ, TJ)],
                                     arr[bass.ds(g * GE, GE)].rearrange("(p j) -> p j", j=TJ)).then_inc(edges_in, 16)
                for arr, own in ((dst, dst_i), (src, src_i), (etype, typ_i)):
                    sp.dma_start(own[:, (GG - 1) * TJ:GG * TJ],
                                 arr[E - GE:E].rearrange("(p j) -> p j", j=TJ)).then_inc(edges_in, 16)
                layers_sp(sp, False)
            sp.nop()

        def layers_pool(pool, together):
            def gather(t, layer):
                table = tables[layer] if layer else tables[0].rearrange("n (r d) -> (n r) d", d=D)
                w = table.shape[1]
                pool.wait_ge(group_used[t.half], t.use + LEAD)
                pool.wait_ge(idx_in[t.half], 16 * (t.use + 1))
                pool.sem_inc(waits_passed, 1)
                def tile(j, done):
                    pool.indirect_dma_start(kv[:, t.half, j, 0:w], None, table,
                                            bass.IndirectOffsetOnAxis(ap=idx[:, t.half, j:j + 1], axis=0)).then_inc(done, 16)

                for j in range(TJ - 1):
                    tile(j, gathered[layer >= 3][t.half][j // CH])
                if together:
                    own = full[0:1, bass.ds(t.block, 1)] if not isinstance(t.block, int) else full[0:1, t.block:t.block + 1]
                    with pool.If(pool.value_load(own, min_val=0, max_val=1) > 0):
                        tile(TJ - 1, last_in[t.half])
                else:
                    tile(TJ - 1, last_in[t.half])

            for layer in range(LAYERS):
                for half in range(2):
                    if layer:
                        pool.wait_ge(rows_out[half], 16 * (rows_before(together, layer + 1)[half] - (EVEN, ODD)[half]) + LEAD)
                for slot in range(SLOTS if layer == 0 else 0):
                    pool.wait_ge(first_out[slot], 16 * len(range(slot, NB, SLOTS)))
                if together:
                    for t, _ in sorted_turns(pool, layer):
                        gather(t, layer)
                else:
                    with pool.Fori(0, NB) as b:
                        for sweep in range(1 if layer < 3 else 2):
                            for t in any_turns(pool, layer, b, sweep):
                                gather(t, layer)

        @block.gpsimd
        def _(pool):
            pool.memset(bias_rows[:], 0.0).then_inc(bias_cleared, 1)
            pool.memset(ident[:], 0.0).then_inc(pool_step, 1)
            pool.wait_ge(pool_step, 1)
            pool.affine_select(out=ident[:], in_=ident[:], compare_op=ALU.not_equal, fill=1.0, base=0,
                               pattern=[[-1, P]], channel_multiplier=1).then_inc(pool_step, 1)
            pool.memset(turned_b[:], 0.0).then_inc(pool_step, 1)
            pool.wait_ge(pool_step, 3)
            pool.affine_select(out=turned_b[:], in_=turned_b[:], compare_op=ALU.not_equal, fill=1.0, base=1 - P,
                               pattern=[[1, P]], channel_multiplier=1).then_inc(pool_step, 1)
            pool.iota(iota_n[:], [[1, BN]], base=0, channel_multiplier=0, allow_small_or_imprecise_dtypes=True)
            pool.iota(iota_e[:], [[1, TJ]], base=0, channel_multiplier=TJ, allow_small_or_imprecise_dtypes=True)
            pool.iota(base_n[:], [[BN, NB]], base=0, channel_multiplier=0, allow_small_or_imprecise_dtypes=True)
            pool.memset(ones[:], 1.0)
            for own in (dst_i, src_i, typ_i):
                pool.memset(own[:].rearrange("p (b j) -> p b j", j=TJ)[:, :, TJ - 1:TJ], 0)
            pool.memset(eps[:], EPS)
            pool.memset(zsum[:], 0.0)
            pool.memset(ones_b[:], 1.0)
            pool.memset(beyond[:], -1.0)
            pool.memset(down[:], UNLIKE)
            pool.memset(up[:], UNLIKE)
            pool.memset(nxt_f[:], FAR)
            pool.wait_ge(pool_step, 4)
            pool.tensor_copy(ident_b[:], ident[:]).then_inc(consts_made, 1)
            def store_rows(j, k=0):
                b = k * SLOTS + j
                to = tables[0][bass.ds(b * BN, BN), :] if not isinstance(b, int) else tables[0][b * BN:(b + 1) * BN, :]
                pool.wait_ge(rows_made[j % 2], k * (SLOTS // 2) + j // 2 + 1 + LEAD)
                pool.sem_inc(waits_passed, 1)
                pool.dma_start(to, first_rows[:, j % SLOTS, :]).then_inc(first_out[j % SLOTS], 16)

            with pool.Fori(0, NB // SLOTS) as k:
                for j in range(SLOTS):
                    store_rows(j, k)
            for b in range(NB // SLOTS * SLOTS, NB):
                store_rows(b)
            pool.wait_ge(planned, 1)
            together = pool.value_load(plan[0:1, NB:NB + 1], min_val=0, max_val=1)
            with pool.If(together > 0):
                layers_pool(pool, True)
            with pool.Else():
                pool.memset(sel[:], 1.0).then_inc(pool_step, 1)
                pool.wait_ge(pool_step, 5)
                pool.affine_select(out=sel[:], in_=sel[:], compare_op=ALU.is_ge, fill=0.0, base=0,
                                   pattern=[[-3, HALF * 4], [0, BN]], channel_multiplier=1).then_inc(pool_step, 1)
                pool.wait_ge(pool_step, 6)
                pool.affine_select(out=sel[:], in_=sel[:], compare_op=ALU.is_ge, fill=0.0, base=2,
                                   pattern=[[3, HALF * 4], [0, BN]], channel_multiplier=-1).then_inc(sel_made, 1)
                layers_pool(pool, False)
            pool.nop()

        def layers_act(act, together):
            def deviation(r):
                act.wait_ge(var_made[r.half], r.use + 1)
                act.activation(sdev[:, r.half:r.half + 1], meanvar[:, r.half, 1:2], ACT.Sqrt, bias=eps[:]
                               ).then_inc(sdev_made[r.half], 1)

            def store_x(r):
                act.wait_ge(x_here[r.half], r.use - (EVEN, ODD)[r.half] + 1)
                act.copy(at(xs, r.block), xcur[:, r.half, :]).then_inc(x_stored[r.half], 1)

            def turned(r, layer):
                where = ps_mx[0] if layer == 4 else ps_st[r.half]
                act.wait_ge(h_turned[r.half], r.use + 1 + LEAD)
                act.activation(hT[:, r.half, :], where[:, 0:BN], ACT.Relu).then_inc(ht_copied[r.half], 1)

            def put_rows(r, layer):
                q, m = (ps_mx[1], None) if layer == 4 else (ps_qe[r.half], ps_mx[r.half])
                act.wait_ge(lin_made[r.half], r.use + 1)
                if layer:
                    act.wait_ge(rows_out[r.half], 16 * (r.use - (EVEN, ODD)[r.half]) + LEAD)
                else:
                    act.wait_ge(first_out[r.slot], 16 * r.slot_use)
                w = TABLE[layer]
                to = rows[:, r.half, :] if layer else first_rows[:, r.slot, :]
                if layer == 0:
                    act.copy(to[:, 512:w], m[0:BN, 0:w - 512])
                if layer >= 3:
                    act.copy(at(qs, r.block), q[0:BN, w:w + D])
                act.copy(to[:, 0:min(w, 512)], q[0:BN, 0:min(w, 512)]).then_inc(rows_made[r.half], 1)

            def copy_st(t, chunks):
                for c in chunks:
                    k = c % 2
                    if c == 0:
                        act.wait_ge(group_used[t.half], t.use + LEAD)
                    act.wait_ge(st_made[k], t.logit * (NC // 2) + c // 2 + 1)
                    here = ps_st[k][0:BN, 0:CH * P].rearrange("p (j e) -> p j e", e=P)
                    if not together:
                        act.activation(mask[:, t.half, c * CH:(c + 1) * CH, :], here, ACT.Copy, bias=-BIG, scale=BIG)
                    act.copy(ST[:, t.half, c * CH:(c + 1) * CH, :], here).then_inc(st_copied[k], 1)

            def turn_parts(t, H):
                act.wait_ge(parts_turned, t.top + 1)
                act.copy(partsT[0:HALF * H * 3, :, :],
                         ps_misc[:].bitcast(BF16)[0:HALF * H * 3, 0:2 * P].rearrange("k (a e) -> k a e", e=P)
                         ).then_inc(parts_copied, 1)

            def exponent(t, H, scale):
                act.wait_ge(shifted, t.msg + 1)
                act.activation(kv[:, t.half, :, 2 * D:2 * D + H].rearrange("p j h -> p h j"),
                               rest[:, t.half, 0:TJ * H].rearrange("p (h j) -> p h j", h=H),
                               ACT.Exp, scale=scale).then_inc(exp_made, 1)

            def all_rows(layer):
                for nxt, cur, _, before, _ in skewed(act, together, layer):
                    if nxt:
                        deviation(nxt)
                    if cur:
                        turned(cur, layer)
                    if nxt and layer:
                        store_x(nxt)
                    if before:
                        put_rows(before, layer)

            if together is None:
                all_rows(0)
                for slot in range(SLOTS):
                    act.wait_ge(first_out[slot], 16 * len(range(slot, NB, SLOTS)))
                return
            for layer in range(LAYERS):
                H = HEADS[layer]
                scale = float(H / D) ** 0.5
                if layer == 3:
                    all_rows(layer)
                if layer == 1 and together:
                    for k in range(0, 2 * NB, 4):
                        n = min(4, 2 * NB - k)
                        act.wait_ge(runs_turned, k // 4 + 1)
                        act.copy(either[0:4, 2 * FL + 2 * NB * TJ + k * P:2 * FL + 2 * NB * TJ + (k + n) * P],
                                 ps_st[(k // 4) % 2][0:4, 0:n * P]).then_inc(runs_copied, 1)

                def rows_inside(r):
                    if layer in (0, 1):
                        store_x(r)
                        deviation(r)
                    if layer in (0, 1, 3):
                        turned(r, layer + 1)
                        put_rows(r, layer + 1)

                if together:
                    if H:
                        copy_st(sorted_turn(layer, 0, 0), range(NC))
                    for t, nxt in sorted_turns(act, layer):
                        r = rows_of(t, True, layer + 1)
                        if not H:
                            rows_inside(r)
                            continue
                        if nxt:
                            copy_st(nxt, (0, 1))
                        exponent(t, H, scale)
                        if nxt:
                            copy_st(nxt, (2, 3, 4))
                        if layer == 3:
                            turned(r, 4)
                        if nxt:
                            copy_st(nxt, (5,))
                        if layer == 3:
                            put_rows(r, 4)
                else:
                    with act.Fori(0, NB) as b:
                        if H:
                            for t in any_turns(act, layer, b, 0):
                                copy_st(t, range(NC))
                                turn_parts(t, H)
                            for t in any_turns(act, layer, b, 1):
                                copy_st(t, range(NC))
                                exponent(t, H, scale)
                        rows_inside(rows_of(b, False, layer + 1))
                if layer == 2:
                    act.wait_ge(bn_asked, 2)
                    act.activation(squares, root[:], ACT.Square).then_inc(bn_var, 1)
                    act.wait_ge(bn_var, 2)
                    act.activation(bn_s[:, 3, :], bn_s[:, 2, :], ACT.Sqrt).then_inc(bn_dev, 1)

        @block.scalar
        def _(act):
            for room in (*st_copied, *rows_made, *sdev_made):
                act.sem_inc(room, LEAD)
            act.dma_start(bases_in[:].rearrange("o (k d) -> o k d", d=D), B.rearrange("k o d -> o k d")).then_inc(in_w, 16)
            act.dma_start(a_bc[:], A.rearrange("r k -> (r k)").rearrange("(a n) -> a n", a=1).to_broadcast([P, TYPES * BASES])).then_inc(in_w, 16)
            act.dma_start(w_r[:, TYPES, :], W0).then_inc(in_w, 16)
            act.dma_start(w_r[:, TYPES + 1:TYPES + 3, :].rearrange("o a d -> o (a d)"), W1).then_inc(in_w, 16)
            act.dma_start(w_r[:, TYPES + 3, :], W2).then_inc(in_w, 16)
            for k in range(3):
                act.wait_ge(w_turned, k + 1)
                if k < 2:
                    act.copy(w0[:, 3 * D * k:3 * D * (k + 1)], ps_st[k][:, 0:3 * D]).then_inc(w_copied, 1)
                else:
                    act.copy(w1[:, D:2 * D], ps_qe[0][:, 0:D])
                    act.copy(w1[:, 0:D], ps_qe[0][:, D:2 * D])
                    act.copy(w2[:], ps_qe[0][:, 2 * D:3 * D]).then_inc(w_copied, 1)
            for vec, own in ((b2, bias2), (gamma, gam), (beta, bet)):
                act.dma_start(own[:], vec.rearrange("(a n) -> a n", a=1).to_broadcast([BN, D])).then_inc(in_b, 16)
            act.wait_ge(in_x, 16)
            layers_act(act, None)
            act.wait_ge(planned, 1)
            together = act.value_load(plan[0:1, NB:NB + 1], min_val=0, max_val=1)
            with act.If(together > 0):
                layers_act(act, True)
            with act.Else():
                layers_act(act, False)
            act.nop()

        def layers_pe(pe, together):
            def turn_h(r, layer):
                turn_at = ps_mx[0] if layer == 4 else ps_st[r.half]
                pe.wait_ge(h_made[r.half], r.use + 1 + LEAD)
                pe.transpose(turn_at[:, 0:BN], hcur[:, r.half, :], ident[0:BN, 0:BN]).then_inc(h_turned[r.half], 1)

            def make_rows(r, layer, before):
                banks = (ps_mx[1],) if layer == 4 else (ps_qe[r.half], ps_mx[r.half])
                w = WALL[layer]
                width = w.shape[1]
                pe.wait_ge(*before)
                if layer == 2:
                    pe.wait_ge(leaky_made[r.half], r.use - rows_before(together, 2)[r.half] + 1)
                else:
                    pe.wait_ge(ht_copied[r.half], r.use + 1)
                for k, to in enumerate(banks[0:-(-width // 512)]):
                    n = min(512, width - 512 * k)
                    if layer in BIAS:
                        pe.matmul(to[0:BN, 0:n], ones_b[:], bias_parts[:, BIAS[layer], 0:n], start=True, stop=False)
                    mm = pe.matmul(to[0:BN, 0:n], hT[:, r.half, :], w[:, 512 * k:512 * k + n],
                                   start=layer not in BIAS, stop=True)
                mm.then_inc(lin_made[r.half], 1)

            def last_kept(r, layer):
                n0, n1 = rows_before(together, layer)
                if layer != 4 or not together:
                    return kept[r.half], r.use + LEAD
                return (kept[1], r.use - n0 + n1 + LEAD) if r.half == 0 else (kept[0], r.use - n1 + n0 + 1 + LEAD)

            def add_up(t, layer, H):
                lo, w = (D, D + H) if H else (0, D)
                for c in range(NC):
                    if c == 0:
                        pe.wait_ge(acc_read, t.acc + LEAD)
                    if H:
                        pe.wait_ge(v_scaled, t.msg * NC + c + 1)
                    else:
                        wait_kv(pe, t, layer, c, together)
                        pe.wait_ge(s_made[t.half], t.use * NC + c + 1)
                    for j in range(c * CH, (c + 1) * CH):
                        mm = pe.matmul(ps_acc[0:BN, 0:w], S[:, t.half, j, :], kv[:, t.half, j, lo:lo + w],
                                       start=(j == 0), stop=(j == TJ - 1))
                mm.then_inc(group_used[t.half], 1)

            def turn(t, c):
                k = c % 2
                pe.wait_ge(s_made[t.half], t.use * NC + c + 1)
                pe.wait_ge(st_copied[k], t.logit * (NC // 2) + c // 2 + LEAD)
                for i in range(CH):
                    mm = pe.transpose(ps_st[k][0:BN, i * P:(i + 1) * P], S[:, t.half, c * CH + i, :], ident[:])
                mm.then_inc(st_made[k], 1)

            def queries(t, c):
                k = c % 2
                pe.wait_ge(st_copied[k], t.logit * (NC // 2) + c // 2 + 1 + LEAD)
                pe.wait_ge(qe_read[k], t.logit * (NC // 2) + c // 2 + LEAD)
                for i in range(CH):
                    mm = pe.matmul(ps_qe[k][:, i * D:(i + 1) * D], ST[:, t.half, c * CH + i, :], at(qs, t.block),
                                   start=True, stop=True)
                mm.then_inc(qe_made[k], 1)

            def logit(t):
                turn(t, 0)
                for c in range(NC):
                    if c + 1 < NC:
                        turn(t, c + 1)
                    queries(t, c)

            def ends_of_rows(t, H):
                pe.wait_ge(scanned, 2 * (t.top + 1))
                f = fore[:, t.half, 0:H * TJ].rearrange("p (h j) -> p h j", h=H)
                g = back[:, t.half, 0:H * TJ].rearrange("p (h j) -> p h j", h=H)
                pe.transpose(ps_misc[0:H, 0:P], f[:, :, TJ - 1], ident[:])
                pe.transpose(ps_misc[0:H, P:2 * P], g[:, :, 0], ident[:]).then_inc(ends_turned, 1)

            def carries(t, H):
                pe.wait_ge(carried, 2 * (t.top + 1))
                pe.sem_inc(waits_passed, 1)
                pe.transpose(ps_misc[:, 2 * P:2 * P + H], down[0:H, 0:P], ident[0:H, 0:H])
                pe.transpose(ps_misc[:, 2 * P + 4:2 * P + 4 + H], up[0:H, 1:P + 1], ident[0:H, 0:H]).then_inc(carry_turned, 1)

            def maxima(t, H):
                pe.wait_ge(split, 5 * (t.top + 1))
                n = HALF * H * 3
                for a in range(2):
                    mm = pe.transpose(ps_misc[:].bitcast(BF16)[0:n, a * P:(a + 1) * P],
                                      parts[:, a * HALF * H:(a + 1) * HALF * H, :].rearrange("p i k -> p (i k)"), ident_b[:])
                mm.then_inc(parts_turned, 1)
                pe.wait_ge(parts_copied, t.top + 1)
                for j in range(TJ):
                    k = j % 2
                    pe.wait_ge(mx_read[k], t.top * HALF + j // 2 + LEAD)
                    own = mask[:, t.half, j, :]
                    for h in range(H):
                        pe.matmul(ps_mx[k][0:BN, h * P:(h + 1) * P], ident_b[0:BN, 0:BN], own, start=True, stop=False)
                        mm = pe.matmul(ps_mx[k][0:BN, h * P:(h + 1) * P], sel[0:n, (j % HALF) * H + h, :],
                                       partsT[0:n, j // HALF, :], start=False, stop=True)
                    mm.then_inc(mx_made[k], 1)
                pe.wait_ge(mx_read[0], (t.top + 1) * HALF + LEAD)
                pe.wait_ge(mx_read[1], (t.top + 1) * HALF + LEAD)
                pe.matmul(ps_misc[0:1, 0:1], ones[:, 0:1], ones[:, 0:1], start=True, stop=True).then_inc(group_used[t.half], 1)

            def spread(t, H, made):
                pe.wait_ge(top_all, made)
                for j in range(TJ):
                    mm = pe.matmul(ps_misc[:, j * H:(j + 1) * H], ST[:, t.half, j, :], top[:, 0:H], start=True, stop=True)
                mm.then_inc(me_made, 1)

            def all_rows(layer):
                for _, cur, prev, _, _ in skewed(pe, together, layer):
                    if cur:
                        turn_h(cur, layer)
                    if prev:
                        make_rows(prev, layer, (kept[prev.half], prev.use + LEAD))

            if together is None:
                all_rows(0)
                return
            if not together:
                pe.wait_ge(sel_made, 1)
            else:
                pe.wait_ge(due_made, 1)
            for layer in range(LAYERS):
                H = HEADS[layer]
                if layer == 3:
                    all_rows(layer)
                if layer == 1 and together:
                    pe.wait_ge(runs_made, 1)
                    for k in range(2 * NB):
                        if k % 4 == 0 and k >= 8:
                            pe.wait_ge(runs_copied, k // 4 - 1)
                        mm = pe.matmul(ps_st[(k // 4) % 2][0:4, (k % 4) * P:(k % 4 + 1) * P],
                                       runs[:, k // NB, k % NB:k % NB + 1].to_broadcast([P, 4]),
                                       (ident_b, turned_b)[k // NB][:], start=True, stop=True)
                        if k % 4 == 3 or k == 2 * NB - 1:
                            mm.then_inc(runs_turned, 1)
                if layer == 0:
                    pe.wait_ge(bias_split, 1)
                if together:
                    if H:
                        logit(sorted_turn(layer, 0, 0))
                    for t, nxt in sorted_turns(pe, layer):
                        r = rows_of(t, True, layer + 1)
                        if not H:
                            add_up(t, layer, H)
                            if layer < 2:
                                turn_h(r, layer + 1)
                                make_rows(r, layer + 1, last_kept(r, layer + 1))
                            continue
                        ends_of_rows(t, H)
                        if nxt:
                            turn(nxt, 0)
                            turn(nxt, 1)
                        carries(t, H)
                        if nxt:
                            queries(nxt, 0)
                            queries(nxt, 1)
                        add_up(t, layer, H)
                        if nxt:
                            turn(nxt, 2)
                            turn(nxt, 3)
                            queries(nxt, 2)
                            turn(nxt, 4)
                            queries(nxt, 3)
                        if layer == 3:
                            turn_h(r, 4)
                        if nxt:
                            turn(nxt, 5)
                            queries(nxt, 4)
                        if layer == 3:
                            make_rows(r, 4, last_kept(r, 4))
                        if nxt:
                            queries(nxt, 5)
                else:
                    with pe.Fori(0, NB) as b:
                        for sweep in range(2 if H else 1):
                            for t in any_turns(pe, layer, b, sweep):
                                if H:
                                    logit(t)
                                if H and sweep == 0:
                                    maxima(t, H)
                                else:
                                    if H:
                                        spread(t, H, (layer - 3) * NB * GG + (b + 1) * GG)
                                    add_up(t, layer, H)
                        if layer in (0, 1, 3):
                            r = rows_of(b, False, layer + 1)
                            turn_h(r, layer + 1)
                            make_rows(r, layer + 1, last_kept(r, layer + 1))
                            pe.wait_ge(kept[0], r.use + 1 + LEAD)
                if layer == 2:
                    for k in range(2):
                        pe.wait_ge(bn_asked, (1, 3)[k])
                        pe.matmul(ps_misc[0:BN, k * D:(k + 1) * D], ones[0:BN, 0:BN], (zsum[:], bn_s[:, 0, :])[k],
                                  start=True, stop=True).then_inc(bn_summed, 1)

        @block.tensor
        def _(pe):
            for room in (*group_used, *h_turned):
                pe.sem_inc(room, LEAD)
            pe.wait_ge(consts_made, 1)
            pe.wait_ge(all_made, 1)
            pe.matmul(ps_acc[0:1, 0:NB + 3], ones[0:ER, 0:1], cnt[:], start=True, stop=True).then_inc(counted, 1)
            pe.wait_ge(full_here, 1)
            pe.matmul(ps_acc[:, 0:NB], ones[0:1, :], full_f[:], start=True, stop=True).then_inc(full_spread, 1)
            for k in range(3):
                pe.wait_ge(w_made, 1)
                to = (ps_st[0], ps_st[1], ps_qe[0])[k]
                for i in range(3):
                    mm = pe.transpose(to[:, i * D:(i + 1) * D], w_r[:, 3 * k + i, :], ident[:])
                mm.then_inc(w_turned, 1)
            pe.wait_ge(w_copied, 3)
            layers_pe(pe, None)
            pe.wait_ge(planned, 1)
            together = pe.value_load(plan[0:1, NB:NB + 1], min_val=0, max_val=1)
            with pe.If(together > 0):
                layers_pe(pe, True)
            with pe.Else():
                layers_pe(pe, False)
            pe.nop()

        def layers_dve(dve, together, done):
            v = nc.vector
            seen = [done]

            def link(ins):
                seen[0] += 1
                ins.then_inc(dve_step, 1)
                dve.wait_ge(dve_step, seen[0])

            root3 = root[:].rearrange("p (b d) -> p b d", d=D)

            def wait_x(r):
                dve.wait_ge(x_here[r.half], r.use - (EVEN, ODD)[r.half] + 1)

            def halves(r, x_now):
                v.bn_stats(halfstat[:, r.half, :], x_now).then_inc(halves_made[r.half], 1)

            def moments(r):
                dve.wait_ge(halves_made[r.half], r.use + 1)
                dve.sem_inc(waits_passed, 1)
                v.bn_aggr(meanvar[:, r.half, :], halfstat[:, r.half, :]).then_inc(var_made[r.half], 1)

            def one_over(r):
                dve.wait_ge(sdev_made[r.half], r.use + 1 + LEAD)
                v.reciprocal(rsdev[:, r.half:r.half + 1], sdev[:, r.half:r.half + 1]).then_inc(rsdev_made[r.half], 1)

            def centre(r, x_now):
                dve.wait_ge(h_turned[r.half], r.use + LEAD)
                dve.wait_ge(rsdev_made[r.half], r.use + 1)
                v.tensor_scalar(hcur[:, r.half, :], x_now, meanvar[:, r.half, 0:1], rsdev[:, r.half:r.half + 1],
                                ALU.subtract, ALU.mult).then_inc(h_made[r.half], 1)

            def leaky(r):
                dve.wait_ge(ht_copied[r.half], r.use + 1)
                v.scalar_tensor_tensor(out=hT[:, r.half, :], in0=hT[:, r.half, :], scalar=0.2, in1=hT[:, r.half, :],
                                       op0=ALU.mult, op1=ALU.max).then_inc(leaky_made[r.half], 1)

            def keep(r, layer):
                dve.wait_ge(rows_made[r.half], r.use + 1 + LEAD)
                q, m = (ps_mx[1], None) if layer == 4 else (ps_qe[r.half], ps_mx[r.half])
                own, x_own = at(root, r.block), at(xs, r.block)
                if layer == 0:
                    ins = v.tensor_tensor(own, m[0:BN, D:2 * D], x_own, ALU.add)
                elif layer == 1:
                    ins = v.tensor_scalar(own, q[0:BN, D:2 * D], 1.0, None, ALU.mult)
                elif layer == 2:
                    ins = v.tensor_tensor(x_own, bet[:], x_own, ALU.add)
                elif layer == 3:
                    ins = v.tensor_scalar(own, q[0:BN, 3 * D:4 * D], 1.0, None, ALU.mult)
                else:
                    ins = v.tensor_tensor(own, q[0:BN, 3 * D:4 * D], x_own, ALU.add)
                ins.then_inc(kept[r.half], 1)

            def select_begin(t):
                dve.wait_ge(group_used[t.half], t.use + LEAD)
                v.tensor_scalar(dloc[:, t.half, :], at(dst_f, t.col, TJ), at(base_n, t.block, 1), None, ALU.subtract
                                ).then_inc(dloc_made[t.half], 1)

            def select(t, c):
                if c == 0:
                    dve.wait_ge(dloc_made[t.half], t.use + 1)
                v.tensor_tensor(S[:, t.half, c * CH:(c + 1) * CH, :],
                                iota_n[:].rearrange("p (a n) -> p a n", a=1).to_broadcast([P, CH, BN]),
                                dloc[:, t.half, c * CH:(c + 1) * CH].rearrange("p (a n) -> p a n", n=1).to_broadcast([P, CH, BN]),
                                ALU.is_equal).then_inc(s_made[t.half], 1)

            def select_all(t):
                select_begin(t)
                for c in range(NC):
                    select(t, c)

            def product(t, layer, c):
                k = c % 2
                wait_kv(dve, t, layer, c, together)
                dve.wait_ge(logits_made[k], t.logit * (NC // 2) + c // 2 + LEAD)
                dve.wait_ge(qe_made[k], t.logit * (NC // 2) + c // 2 + 1)
                v.tensor_tensor(prod[:, k, :].rearrange("p (j d) -> p j d", d=D),
                                ps_qe[k][:, 0:CH * D].rearrange("p (j d) -> p j d", d=D),
                                kv[:, t.half, c * CH:(c + 1) * CH, 0:D], ALU.mult).then_inc(qe_read[k], 1)

            def head_sums(t, H, c):
                k = c % 2
                dve.wait_ge(qe_read[k], t.logit * (NC // 2) + c // 2 + 1 + LEAD)
                if together:
                    to = alpha[:, t.half, 0:H * TJ].rearrange("p (h j) -> p h j", h=H)[:, :, c * CH:(c + 1) * CH] \
                        .rearrange("p h j -> p j h")
                else:
                    to = alpha[:, t.half, c * CH * H:(c + 1) * CH * H].rearrange("p (j h) -> p j h", h=H)
                v.tensor_reduce(to, prod[:, k, :].rearrange("p (j h d) -> p j h d", j=CH, h=H), AX.X, ALU.add
                                ).then_inc(logits_made[k], 1)

            def logit(t, layer, H):
                product(t, layer, 0)
                for c in range(NC):
                    if c + 1 < NC:
                        product(t, layer, c + 1)
                    head_sums(t, H, c)

            def logits_here(t):
                for k in range(2):
                    dve.wait_ge(logits_made[k], (t.logit + 1) * (NC // 2) + LEAD)

            def shift(t, H, nxt):
                n = TJ * H
                a, f, g = alpha[:, t.half, 0:n], fore[:, t.half, 0:n], back[:, t.half, 0:n]
                prev, foll = (at(either[:, k * FL:(k + 1) * FL], t.block, 4 * TJ)[:, 0:n] for k in range(2))
                if nxt:
                    select_begin(nxt)
                logits_here(t)
                last = a.rearrange("p (h j) -> p h j", h=H)[:, :, TJ - 1]
                v.tensor_tensor(last, last, at(lean_p, t.block, 1).to_broadcast([P, H]), ALU.add).then_inc(lean_below, 1)
                dve.wait_ge(lean_below, t.msg + 1)
                v.tensor_tensor_scan(f, prev, a, UNLIKE, ALU.add, ALU.max).then_inc(scanned, 1)
                v.tensor_tensor_scan(g[:, ::-1], foll, a[:, ::-1], UNLIKE, ALU.add, ALU.max).then_inc(scanned, 1)
                if nxt:
                    select(nxt, 0)
                    select(nxt, 1)
                dve.wait_ge(scanned, 2 * (t.top + 1))
                m = rest[:, t.half, 0:n]
                v.tensor_tensor(m, f, g, ALU.max).then_inc(topped, 1)
                dve.wait_ge(ends_turned, t.top + 1)
                v.tensor_tensor_scan(down[0:H, 1:P + 1], at(run_down, t.block, P)[0:H], ps_misc[0:H, 0:P], UNLIKE,
                                     ALU.add, ALU.max).then_inc(carried, 1)
                v.tensor_tensor_scan(up[0:H, 0:P][:, ::-1], at(run_up, t.block, P)[0:H], ps_misc[0:H, P:2 * P][:, ::-1],
                                     UNLIKE, ALU.add, ALU.max).then_inc(carried, 1)
                if nxt:
                    select(nxt, 2)
                    select(nxt, 3)
                dve.wait_ge(carry_turned, t.top + 1)
                dve.wait_ge(topped, 5 * t.top + 1)
                for k, (like, own) in enumerate(((like_above, f), (like_below, g))):
                    v.tensor_tensor(own.rearrange("p (h j) -> p h j", h=H),
                                    ps_misc[:, 2 * P + 4 * k:2 * P + 4 * k + H].rearrange("p (h o) -> p h o", o=1).to_broadcast([P, H, TJ]),
                                    at(like, t.block, TJ).rearrange("p (o j) -> p o j", o=1).to_broadcast([P, H, TJ]),
                                    ALU.add).then_inc(topped, 1)
                dve.wait_ge(topped, 5 * t.top + 3)
                v.tensor_tensor(f, f, g, ALU.max).then_inc(topped, 1)
                dve.wait_ge(topped, 5 * t.top + 4)
                v.tensor_tensor(m, m, f, ALU.max).then_inc(topped, 1)
                dve.wait_ge(topped, 5 * t.top + 5)
                v.tensor_tensor(m, a, m, ALU.subtract).then_inc(shifted, 1)

            def maxima(t, H):
                n = TJ * H
                a, r = alpha[:, t.half, 0:n], rest[:, t.half, 0:n]
                logits_here(t)
                v.tensor_copy(parts[:, 0:n, 0], a).then_inc(split, 1)
                dve.wait_ge(split, 5 * t.top + 1)
                v.tensor_tensor(r, a, parts[:, 0:n, 0], ALU.subtract).then_inc(split, 1)
                dve.wait_ge(split, 5 * t.top + 2)
                v.tensor_copy(parts[:, 0:n, 1], r).then_inc(split, 1)
                dve.wait_ge(split, 5 * t.top + 3)
                v.tensor_tensor(r, r, parts[:, 0:n, 1], ALU.subtract).then_inc(split, 1)
                dve.wait_ge(split, 5 * t.top + 4)
                v.tensor_copy(parts[:, 0:n, 2], r).then_inc(split, 1)
                for j in range(TJ):
                    k = j % 2
                    dve.wait_ge(mx_made[k], t.top * HALF + j // 2 + 1)
                    v.tensor_reduce(tops[:, 0:H, j], ps_mx[k][0:BN, 0:H * P].rearrange("p (h e) -> p h e", e=P), AX.X, ALU.max
                                    ).then_inc(mx_read[k], 1)
                dve.wait_ge(mx_read[0], (t.top + 1) * HALF + LEAD)
                dve.wait_ge(mx_read[1], (t.top + 1) * HALF + LEAD)
                v.tensor_reduce(top[:, 0:H], tops[:, 0:H, :], AX.X, ALU.max).then_inc(top_made, 1)
                dve.wait_ge(top_made, 2 * t.top + 1)
                v.tensor_tensor(topn[:, 0:H], topn[:, 0:H], top[:, 0:H], ALU.max).then_inc(top_made, 1)
                dve.wait_ge(top_made, 2 * t.top + 2)
                v.tensor_copy(top[:, 0:H], topn[:, 0:H]).then_inc(top_all, 1)

            def shift_any(t, H):
                logits_here(t)
                dve.wait_ge(me_made, t.msg + 1)
                v.tensor_tensor(rest[:, t.half, 0:TJ * H].rearrange("p (h j) -> p j h", h=H),
                                alpha[:, t.half, 0:TJ * H].rearrange("p (j h) -> p j h", h=H),
                                ps_misc[:, 0:TJ * H].rearrange("p (j h) -> p j h", h=H), ALU.subtract).then_inc(shifted, 1)

            def messages(t, H):
                dve.wait_ge(exp_made, t.msg + 1)
                for c in range(NC):
                    tiles = kv[:, t.half, c * CH:(c + 1) * CH, :]
                    val = tiles[:, :, D:2 * D].rearrange("p j (h d) -> p j h d", h=H)
                    w = tiles[:, :, 2 * D:2 * D + H].rearrange("p j (h o) -> p j h o", o=1).to_broadcast([P, CH, H, D // H])
                    v.tensor_tensor(val, val, w, ALU.mult).then_inc(v_scaled, 1)

            def divide(sums, H, n, read):
                per = 3 if read is None else 2
                v.tensor_scalar(den[:, 0:H], sums[:, D:D + H], 1e-16, None, ALU.add).then_inc(normed, 1)
                dve.wait_ge(normed, per * n + 1)
                v.reciprocal(rden[:, 0:H], den[:, 0:H]).then_inc(normed, 1)
                dve.wait_ge(normed, per * n + 2)
                v.tensor_tensor(onorm[:].rearrange("p (h d) -> p h d", h=H), sums[:, 0:D].rearrange("p (h d) -> p h d", h=H),
                                rden[:, 0:H].rearrange("p (h o) -> p h o", o=1).to_broadcast([BN, H, D // H]), ALU.mult
                                ).then_inc(normed if read is None else read[0], 1)
                if read is None:
                    dve.wait_ge(normed, per * n + 3)
                else:
                    dve.wait_ge(*read)

            def to_hidden(r):
                dve.wait_ge(h_turned[r.half], r.use + LEAD)
                v.tensor_tensor(hcur[:, r.half, :], onorm[:], at(root, r.block), ALU.add).then_inc(h_made[r.half], 1)

            def to_result(b):
                v.tensor_tensor(at(xs, b), onorm[:], at(root, b), ALU.add).then_inc(x_done, 1)

            def prepare_edges(piece):
                lo, hi = PIECES[piece:piece + 2]
                dve.wait_ge(edges_in, 16 * 3 * hi)
                own = slice(lo * TJ, hi * TJ)
                v.tensor_copy(dst_f[:, own], dst_i[:, own]).then_inc(edges_made, 1)
                v.scalar_tensor_tensor(out=typ_i[:, own], in0=src_i[:, own], scalar=float(TYPES), in1=typ_i[:, own],
                                       op0=ALU.mult, op1=ALU.add).then_inc(edges_made, 2)
                dve.wait_ge(edges_made, 3 * (piece + 1))
                by_column = dst_f[:, own].rearrange("p (b j) -> p b j", j=TJ)
                last, one_before = by_column[:, :, TJ - 1], by_column[:, :, TJ - 2]
                after = beyond_lean[:, lo:hi]
                link(v.tensor_tensor(after, last, one_before, ALU.subtract))
                link(v.tensor_tensor(after, after, full_p[:, lo:hi], ALU.mult))
                link(v.tensor_tensor(ends[:, 1, lo:hi], after, one_before, ALU.add))
                v.tensor_copy(dst_i[:, own].rearrange("p (b j) -> p b j", j=TJ)[:, :, TJ - 1], ends[:, 1, lo:hi])
                v.tensor_copy(ends[:, 0, lo:hi], by_column[:, :, 0]).then_inc(ends_made, 1)
                link(v.scalar_tensor_tensor(out=last, in0=lean_p[:, lo:hi], scalar=FAR, in1=last, op0=ALU.mult, op1=ALU.add))

            def split_biases():
                dve.wait_ge(in_a, 16 * 17)
                link(v.tensor_copy(bias_part[:], bias_rows[:]))
                link(v.tensor_tensor(bias_rest[:], bias_rows[:], bias_part[:], ALU.subtract))
                link(v.tensor_scalar(bias_parts[:], bias_part[:], ident[0:3, 0:1], None, ALU.mult))
                for k in (1, 2):
                    link(v.tensor_copy(bias_part[:], bias_rest[:]))
                    if k == 1:
                        link(v.tensor_tensor(bias_rest[:], bias_rest[:], bias_part[:], ALU.subtract))
                    ins = v.scalar_tensor_tensor(out=bias_parts[:], in0=bias_part[:], scalar=ident[0:3, k:k + 1],
                                                 in1=bias_parts[:], op0=ALU.mult, op1=ALU.add)
                    if k == 1:
                        link(ins)
                ins.then_inc(bias_split, 1)

            def flags():
                d3 = dst_i[:].rearrange("p (b j) -> p b j", j=TJ)
                dve.wait_ge(beyond_in, 32)

                def outside(k):
                    return beyond[:, k, :].rearrange("p (b o) -> p b o", o=1).to_broadcast([P, NB, TJ])

                for h in range(4):
                    v.tensor_tensor(like_prev[:, :, h, 1:TJ], d3[:, :, 1:TJ], d3[:, :, 0:TJ - 1], ALU.not_equal)
                    v.tensor_tensor(like_next[:, :, h, TJ - 1:0:-1], d3[:, :, 1:TJ], d3[:, :, 0:TJ - 1], ALU.not_equal)
                v.tensor_tensor(like_above.rearrange("p (b j) -> p b j", j=TJ), d3, outside(0), ALU.not_equal)
                v.tensor_tensor(like_below.rearrange("p (b j) -> p b j", j=TJ), d3, outside(1), ALU.not_equal)
                v.tensor_tensor(runs[:, 0, :], ends[:, 1, :], beyond[:, 0, :], ALU.not_equal)
                v.memset(like_prev[:, :, :, 0:1], 1.0)
                v.memset(like_next[:, :, :, 0:1], 1.0)
                link(v.tensor_tensor(runs[:, 1, :], ends[:, 0, :], beyond[:, 1, :], ALU.not_equal))
                v.tensor_scalar(runs[:], runs[:], UNLIKE, None, ALU.mult).then_inc(runs_made, 1)
                flat = either[:, 0:2 * FL + 2 * NB * TJ]
                link(v.tensor_scalar(flat, flat, UNLIKE, None, ALU.mult))

            def add_sums(t, layer, r):
                own = at(root, t.block)
                if layer == 0:
                    dve.wait_ge(rows_made[r.half], r.use + LEAD)
                    v.tensor_tensor(xcur[:, r.half, :], ps_acc[0:BN, 0:D], own, ALU.add).then_inc(x_here[r.half], 1)
                    wait_x(r)
                    dve.sem_inc(acc_read, 1)
                elif layer == 1:
                    dve.wait_ge(rows_made[r.half], r.use + LEAD)
                    v.tensor_tensor(onorm[:], ps_acc[0:BN, 0:D], own, ALU.add).then_inc(acc_read, 1)
                    dve.wait_ge(acc_read, t.acc + 1 + LEAD)
                    v.scalar_tensor_tensor(out=xcur[:, r.half, :], in0=onorm[:], scalar=0.0, in1=at(xs, t.block),
                                           op0=ALU.max, op1=ALU.add).then_inc(x_here[r.half], 1)
                else:
                    v.tensor_tensor(own, ps_acc[0:BN, 0:D], bias2[:], ALU.add).then_inc(acc_read, 1)
                    dve.wait_ge(acc_read, t.acc + 1 + LEAD)
                    dve.wait_ge(z_added, t.block + LEAD)
                    v.tensor_tensor(zsum[:], zsum[:], own, ALU.add).then_inc(z_added, 1)

            def take_sums(b, layer, r):
                own = at(root, b)
                if layer == 0:
                    dve.wait_ge(rows_made[r.half], r.use + LEAD)
                    v.tensor_copy(xcur[:, r.half, :], own).then_inc(x_here[r.half], 1)
                elif layer == 1:
                    dve.wait_ge(rows_made[r.half], r.use + LEAD)
                    v.scalar_tensor_tensor(out=xcur[:, r.half, :], in0=own, scalar=0.0, in1=at(xs, b),
                                           op0=ALU.max, op1=ALU.add).then_inc(x_here[r.half], 1)
                else:
                    dve.wait_ge(z_added, 2 * b + 1 + LEAD)
                    v.tensor_tensor(zsum[:], zsum[:], own, ALU.add).then_inc(z_added, 1)

            def next_rows(r, layer):
                x_now = xcur[:, r.half, :]
                wait_x(r)
                halves(r, x_now)
                moments(r)
                one_over(r)
                centre(r, x_now)
                if layer == 1:
                    leaky(r)
                keep(r, layer + 1)

            def all_rows(layer):
                for nxt, cur, _, _, old in skewed(dve, together, layer):
                    if nxt and layer:
                        dve.wait_ge(x_stored[nxt.half], nxt.use - (EVEN, ODD)[nxt.half])
                        v.tensor_tensor(onorm[:], at(root, nxt.block), bn_s[:, 0, :], ALU.mult).then_inc(scaled, 1)
                    if cur:
                        one_over(cur)
                    if nxt and layer:
                        dve.wait_ge(scaled, nxt.block + 1)
                        v.tensor_tensor(xcur[:, nxt.half, :], onorm[:], at(xs, nxt.block), ALU.add).then_inc(x_here[nxt.half], 1)
                    if cur:
                        centre(cur, xcur[:, cur.half, :] if layer else at(xs, cur.block))
                    if nxt:
                        if layer:
                            wait_x(nxt)
                        halves(nxt, xcur[:, nxt.half, :] if layer else at(xs, nxt.block))
                    if nxt:
                        moments(nxt)
                    if old:
                        keep(old, layer)

            if together is None:
                all_rows(0)
                return
            for layer in range(LAYERS):
                H = HEADS[layer]
                if layer == 3:
                    all_rows(layer)
                if layer == 0 and not together:
                    split_biases()
                if together:
                    if layer == 0:
                        prepare_edges(0)
                    select_all(sorted_turn(layer, 0, 0))
                    if layer == 0:
                        split_biases()
                        prepare_edges(1)
                        v.tensor_scalar(lean_p[:], lean_p[:], -BIG, None, ALU.mult).then_inc(lean_made, 1)
                    if layer == 1:
                        flags()
                    if H:
                        logit(sorted_turn(layer, 0, 0), layer, H)
                    for t, nxt in sorted_turns(dve, layer):
                        r = rows_of(t, True, layer + 1)
                        if not H:
                            if nxt:
                                select_all(nxt)
                            dve.wait_ge(group_used[t.half], t.use + 1 + LEAD)
                            add_sums(t, layer, r)
                            if layer < 2:
                                next_rows(r, layer)
                            continue
                        shift(t, H, nxt)
                        messages(t, H)
                        if nxt:
                            select(nxt, 4)
                            select(nxt, 5)
                            product(nxt, layer, 0)
                            product(nxt, layer, 1)
                            head_sums(nxt, H, 0)
                            head_sums(nxt, H, 1)
                        dve.wait_ge(group_used[t.half], t.use + 1 + LEAD)
                        if layer == 4:
                            dve.wait_ge(x_done, t.block + LEAD)
                        divide(ps_acc[0:BN, :], H, t.msg, (acc_read, t.acc + 1 + LEAD))
                        if layer == 3:
                            to_hidden(r)
                        else:
                            to_result(t.block)
                        if nxt:
                            product(nxt, layer, 2)
                            for c in range(3, NC):
                                product(nxt, layer, c)
                                head_sums(nxt, H, c - 1)
                                if c == NC - 1 and layer == 3:
                                    keep(r, 4)
                            head_sums(nxt, H, NC - 1)
                        elif layer == 3:
                            keep(r, 4)
                else:
                    with dve.Fori(0, NB) as b:
                        r = rows_of(b, False, layer + 1)
                        if not H:
                            if layer == 2:
                                v.tensor_copy(at(root, b), bias2[:]).then_inc(z_added, 1)
                                dve.wait_ge(z_added, 2 * b + 1 + LEAD)
                                dve.sem_inc(waits_passed, 1)
                            for t in any_turns(dve, layer, b, 0):
                                select_all(t)
                                dve.wait_ge(group_used[t.half], t.use + 1 + LEAD)
                                dve.wait_ge(acc_read, t.acc + LEAD)
                                v.tensor_tensor(at(root, b), ps_acc[0:BN, 0:D], at(root, b), ALU.add).then_inc(acc_read, 1)
                            dve.wait_ge(acc_read, (layer * NB + b + 1) * GG + LEAD)
                            take_sums(b, layer, r)
                            if layer < 2:
                                next_rows(r, layer)
                            else:
                                dve.wait_ge(z_added, 2 * b + 2 + LEAD)
                                dve.sem_inc(waits_passed, 1)
                        else:
                            before = (layer - 3) * NB + b
                            v.memset(msum[:], 0.0).then_inc(block_begun, 1)
                            v.memset(topn[:], -BIG).then_inc(block_begun, 1)
                            dve.wait_ge(block_begun, 2 * before + 2)
                            dve.sem_inc(waits_passed, 1)
                            for t in any_turns(dve, layer, b, 0):
                                select_all(t)
                                logit(t, layer, H)
                                maxima(t, H)
                            for t in any_turns(dve, layer, b, 1):
                                select_all(t)
                                logit(t, layer, H)
                                shift_any(t, H)
                                messages(t, H)
                                dve.wait_ge(group_used[t.half], t.use + 1 + LEAD)
                                dve.wait_ge(acc_read, t.acc + LEAD)
                                v.tensor_tensor(msum[:, 0:D + H], msum[:, 0:D + H], ps_acc[0:BN, 0:D + H], ALU.add).then_inc(acc_read, 1)
                            dve.wait_ge(acc_read, (layer * NB + b + 1) * GG + LEAD)
                            divide(msum, H, before, None)
                            if layer == 3:
                                to_hidden(r)
                                keep(r, 4)
                            else:
                                to_result(b)
                                dve.wait_ge(x_done, b + 1 + LEAD)
                                dve.sem_inc(waits_passed, 1)
                if layer == 2:
                    dve.wait_ge(z_added, (NB if together else 2 * NB) + LEAD)
                    v.memset(den[:], 0.0).then_inc(bn_asked, 1)
                    dve.wait_ge(bn_summed, 1)
                    link(v.tensor_scalar(bn_s[:, 1, :], ps_misc[0:BN, 0:D], 1.0 / N, None, ALU.mult))
                    v.tensor_tensor(root3, root3, bn_s[:, 1:2, :].to_broadcast([BN, NB, D]), ALU.subtract).then_inc(bn_asked, 1)
                    dve.wait_ge(bn_var, 1)
                    v.tensor_reduce(bn_s[:, 0, :], squares.rearrange("p (b d) -> p d b", d=D), AX.X, ALU.add).then_inc(bn_asked, 1)
                    dve.wait_ge(bn_summed, 2)
                    v.tensor_scalar(bn_s[:, 2, :], ps_misc[0:BN, D:2 * D], 1.0 / N, EPS, ALU.mult, ALU.add).then_inc(bn_var, 1)
                    dve.wait_ge(bn_dev, 1)
                    link(v.reciprocal(bn_s[:, 1, :], bn_s[:, 3, :]))
                    link(v.tensor_tensor(bn_s[:, 0, :], bn_s[:, 1, :], gam[:], ALU.mult))

        @block.vector
        def _(dve):
            for room in (*qe_read, *logits_made, *kept, *h_made, *mx_read, acc_read, z_added, x_done):
                dve.sem_inc(room, LEAD)
            v = nc.vector
            seen = [0]

            def link(ins):
                seen[0] += 1
                ins.then_inc(dve_step, 1)
                dve.wait_ge(dve_step, seen[0])

            dve.wait_ge(in_all, 32)
            dve.wait_ge(consts_made, 1)
            v.tensor_copy(nxt_f[0:ER - 1, :], nxt_i[0:ER - 1, :])
            link(v.tensor_copy(all_f, all_i))
            for b in range(NB):
                if b >= len(hits):
                    dve.wait_ge(dve_step, seen[0] - (len(hits) - 1))
                v.tensor_scalar(hits[b % len(hits)], all_f, float(BN * b), 0.0, ALU.is_lt, ALU.add,
                                accum_out=cnt[:, b:b + 1]).then_inc(dve_step, 1)
                seen[0] += 1
            dve.wait_ge(dve_step, seen[0])
            v.tensor_tensor(cnt[:, NB + 1:NB + 2], all_f[:, EW - 1:EW], nxt_f[:], ALU.is_gt)
            v.memset(cnt[:, NB + 2:NB + 3], 0.0)
            link(v.tensor_tensor(hits[0][:, 0:EW - 1], all_f[:, 0:EW - 1], all_f[:, 1:EW], ALU.is_gt))
            v.tensor_reduce(cnt[:, NB:NB + 1], hits[0][:, 0:EW - 1], AX.X, ALU.add).then_inc(all_made, 1)
            dve.wait_ge(in_w, 16 * 5)
            for k in range(BASES):
                for r in range(TYPES):
                    wk = bases_in[:, k * D:(k + 1) * D]
                    a = a_bc[:, r * BASES + k:r * BASES + k + 1]
                    if k == 0:
                        ins = v.tensor_scalar(w_r[:, r, :], wk, a, None, ALU.mult)
                    else:
                        ins = v.scalar_tensor_tensor(out=w_r[:, r, :], in0=wk, scalar=a, in1=w_r[:, r, :],
                                                     op0=ALU.mult, op1=ALU.add)
                if k < BASES - 1:
                    link(ins)
            ins.then_inc(w_made, 1)
            dve.wait_ge(counted, 1)
            link(v.tensor_copy(total[:], ps_acc[0:1, 0:NB + 3]))
            v.tensor_tensor(block_edges[:, 0:NB - 1], total[:, 1:NB], total[:, 0:NB - 1], ALU.subtract)
            link(v.tensor_scalar(block_edges[:, NB - 1:NB], total[:, NB - 1:NB], -1.0, float(E), ALU.mult, ALU.add))
            link(v.tensor_scalar(full_f[:], block_edges[:, 0:NB], float(LE), None, ALU.is_gt))
            link(v.memset(full_f[:, 0:2], 1.0))
            v.tensor_scalar(plan_f[:, 0:NB], full_f[:], float(-P), float(E - LE), ALU.mult, ALU.add).then_inc(full_here, 1)
            v.tensor_copy(full[:], full_f[:])
            link(v.tensor_reduce(block_edges[:, NB:NB + 1], block_edges[:, 0:NB], AX.X, ALU.max))
            v.tensor_tensor(plan_f[:, 0:NB], plan_f[:, 0:NB], total[:, 0:NB], ALU.min)
            link(v.tensor_scalar(block_edges[:, NB:NB + 1], block_edges[:, NB:NB + 1], float(GE), None, ALU.is_le))
            link(v.tensor_tensor(block_edges[:, NB + 1:NB + 2], total[:, NB:NB + 1], total[:, NB + 1:NB + 2], ALU.add))
            link(v.tensor_scalar(block_edges[:, NB + 1:NB + 2], block_edges[:, NB + 1:NB + 2], 0.0, None, ALU.is_equal))
            link(v.tensor_tensor(plan_f[:, NB:NB + 1], block_edges[:, NB:NB + 1], block_edges[:, NB + 1:NB + 2], ALU.mult))
            v.tensor_copy(plan[:, 0:NB + 1], plan_f[:, 0:NB + 1]).then_inc(planned, 1)
            def half_of(row, half):
                return due_f[:, row, 0:NB + 1].rearrange("p (i two) -> p i two", two=2)[:, :, half]

            link(v.memset(due_f[:], 0.0))
            link(v.tensor_scalar(due_f[:, 0, 0:NB], full_f[:], 16.0, None, ALU.mult))
            here = 0
            for k in (2, 4, 8, 16):
                v.tensor_copy(due_f[:, 1 - here, 0:k], due_f[:, here, 0:k])
                link(v.tensor_tensor(due_f[:, 1 - here, k:NB + 1], due_f[:, here, k:NB + 1], due_f[:, here, 0:NB + 1 - k], ALU.add))
                here = 1 - here
            for layer in range(LAYERS):
                for half in range(2):
                    ins = v.scalar_tensor_tensor(out=half_of(2 + layer, half), in0=half_of(here, half)[:, EVEN - 1:EVEN].to_broadcast([1, EVEN]),
                                                 scalar=float(layer), in1=half_of(here, half), op0=ALU.mult, op1=ALU.add)
            link(ins)
            v.tensor_copy(due[:].rearrange("p (a b) -> p a b", b=NB), due_f[:, 2:, 0:NB]).then_inc(due_made, 1)
            dve.wait_ge(full_spread, 1)
            v.tensor_scalar(full_p[:], ps_acc[:, 0:NB], 1.0, None, ALU.mult)
            v.tensor_scalar(lean_p[:], ps_acc[:, 0:NB], -1.0, 1.0, ALU.mult, ALU.add).then_inc(lean_made, 1)
            dve.wait_ge(in_x, 16)
            layers_dve(dve, None, seen[0])
            dve.wait_ge(in_b, 48)
            dve.wait_ge(planned, 1)
            together = dve.value_load(plan[0:1, NB:NB + 1], min_val=0, max_val=1)
            with dve.If(together > 0):
                dve.wait_ge(due_made, 1)
                dve.wait_ge(lean_made, 1)
                layers_dve(dve, True, seen[0])
            with dve.Else():
                dve.wait_ge(edges_in, 16 * 3 * GG)
                n = GG * TJ
                v.tensor_scalar(rest[:, 0, 0:TJ], iota_e[:], float((GG - 1) * GE - (E - GE)), FAR, ALU.is_lt, ALU.mult)
                v.tensor_copy(dst_f[:, 0:n], dst_i[:, 0:n]).then_inc(edges_made, 1)
                dve.wait_ge(edges_made, 1)
                v.tensor_tensor(dst_f[:, n - TJ:n], dst_f[:, n - TJ:n], rest[:, 0, 0:TJ], ALU.add).then_inc(edges_made, 1)
                v.scalar_tensor_tensor(out=typ_i[:, 0:n], in0=src_i[:, 0:n], scalar=float(TYPES), in1=typ_i[:, 0:n],
                                       op0=ALU.mult, op1=ALU.add).then_inc(edges_made, 1)
                dve.wait_ge(edges_made, 3)
                layers_dve(dve, False, seen[0])
            dve.nop()


_INS = ['x', 'src', 'dst', 'edge_type_5', 'L0_gnn_B', 'L0_gnn_A', 'L0_gnn_W0', 'L1_gnn_W', 'L1_gnn_b',
        'L2_gnn_W', 'L2_gnn_b', 'L2_gnn_gamma', 'L2_gnn_beta']
_ATT = [f"L3_gnn_{kind}{n}" for n in (1, 2) for kind in ("Wk", "Wv", "Wq", "Ws", "bk", "bv", "bq", "bs")]


def kernel(**inputs):
    import numpy as _np
    import concourse.bacc as _bacc
    from concourse import mybir as _mybir
    from concourse.bass_utils import run_bass_kernel_spmd as _run

    nc = _bacc.Bacc("TRN2", target_bir_lowering=False, num_devices=1)
    arrays, aps = {}, {}
    for name in _INS + _ATT:
        a = _np.ascontiguousarray(inputs[name])
        arrays[f"in_{name}"] = a
        aps[name] = nc.dram_tensor(f"in_{name}", a.shape, _mybir.dt.from_np(a.dtype), kind="ExternalInput").ap()
    out = nc.dram_tensor("out", (N, D), _mybir.dt.float32, kind="ExternalOutput").ap()
    att = [([aps[n] for n in _ATT[8 * k:8 * k + 4]], [aps[n] for n in _ATT[8 * k + 4:8 * k + 8]]) for k in range(2)]
    build(nc, *[aps[n] for n in _INS], *att, out)
    r = _run(nc, [arrays], core_ids=[0])
    return r.results[0]["out"]
```
